# Optimizing a Trainium2 kernel written in Bass

```python
import numpy as np
import jax
import jax.numpy as jnp

def _softmax(x, axis=-1):
    return jax.nn.softmax(x, axis=axis)

def _gelu(x):
    return jax.nn.gelu(x, approximate=True)

def _silu(x):
    return jax.nn.silu(x)

def _sigmoid(x):
    return jax.nn.sigmoid(x)

def _layernorm(x, axis=-1, eps=1e-05):
    m = jnp.mean(x, axis=axis, keepdims=True)
    v = jnp.var(x, axis=axis, keepdims=True)
    return (x - m) / jnp.sqrt(v + eps)

def _scatter_add(tgt, idx, src, axis=0):
    return tgt.at[idx].add(src)

def _segment_sum(src, seg, n):
    return jax.ops.segment_sum(src, seg, n)
kernel_name = 'mk_gnn_resnorm_d2_gnn_r32_296134'

def setup_inputs(seed: int=0):
    np.random.seed(seed)
    _w = jnp.asarray

    def _rec_inputs():
        import jax
        import jax.numpy as jnp
        _gk = jax.random.key(seed)
        x = -0.0003713 + 1 * jax.random.normal(jax.random.fold_in(_gk, 1), (3125, 256), jnp.float32)
        src = jax.random.randint(jax.random.fold_in(_gk, 2), (50000,), 0, 3125, jnp.int32)
        dst = jnp.minimum((3125 * jax.random.uniform(jax.random.fold_in(_gk, 3), (50000,)) ** 2.0).astype(jnp.int32), 99999)
        _o = jnp.argsort(dst, stable=True)
        src = src[_o]
        dst = dst[_o]
        edge_attr_18 = 0.00023367 + 0.999922 * jax.random.normal(jax.random.fold_in(_gk, 12), (50000, 18), jnp.float32)
        edge_type_16 = jax.random.randint(jax.random.fold_in(_gk, 14), (50000,), 0, 16, jnp.int32)
        return (x, src, dst, edge_attr_18, edge_type_16)
    x, src, dst, edge_attr_18, edge_type_16 = _rec_inputs()

    def _L0_gnn_setup():
        import jax, jax.numpy as jnp
        import numpy as np
        N, E = (50000, 25000)
        DIM, H, D = (256, 16, 8)
        DH = D * H
        IN_RPE = 18
        SCALE = D ** (-0.5)
        EPS = 1e-16

        def _segment_softmax(compat, s, num_nodes):
            m = jax.ops.segment_max(compat, s, num_segments=num_nodes)
            ex = jnp.exp(compat - m[s])
            den = jax.ops.segment_sum(ex, s, num_segments=num_nodes)
            return ex / (den[s] + EPS)
        key = jax.random.key(seed)
        ks = jax.random.split(key, 10)
        x = jax.random.normal(ks[0], (N, DIM), dtype=jnp.float32)
        edge_index = jax.random.randint(ks[1], (2, E), 0, N, dtype=jnp.int64)
        edge_attr = jax.random.normal(ks[2], (E, IN_RPE), dtype=jnp.float32)
        Wqkv = jax.random.normal(ks[3], (DIM, 2 * DH + DIM), dtype=jnp.float32) * DIM ** (-0.5)
        bqkv = jnp.zeros((2 * DH + DIM,), dtype=jnp.float32)
        Wk_rpe = jax.random.normal(ks[4], (IN_RPE, DH), dtype=jnp.float32) * IN_RPE ** (-0.5)
        bk_rpe = jnp.zeros((DH,), dtype=jnp.float32)
        Wq_rpe = jax.random.normal(ks[5], (IN_RPE, DH), dtype=jnp.float32) * IN_RPE ** (-0.5)
        bq_rpe = jnp.zeros((DH,), dtype=jnp.float32)
        return {'x': x, 'edge_index': edge_index, 'edge_attr': edge_attr, 'Wqkv': Wqkv, 'bqkv': bqkv, 'Wk_rpe': Wk_rpe, 'bk_rpe': bk_rpe, 'Wq_rpe': Wq_rpe, 'bq_rpe': bq_rpe}
    _L0_gnn_all = _L0_gnn_setup()
    _L0_gnn_in = {k: v for k, v in _L0_gnn_all.items() if k in ('Wqkv', 'bqkv', 'Wk_rpe', 'bk_rpe', 'Wq_rpe', 'bq_rpe')}
    del _L0_gnn_all

    def _L1_gnn_setup():
        import jax, jax.numpy as jnp
        import numpy as np
        N_NODES = 50000
        N_EDGES = 25000
        HDIM = 256
        NUMRELS = 16

        def _gru_cell(x, h, w_ih, w_hh, b_ih, b_hh):
            gi = x @ w_ih.T + b_ih
            gh = h @ w_hh.T + b_hh
            i_r, i_z, i_n = jnp.split(gi, 3, axis=-1)
            h_r, h_z, h_n = jnp.split(gh, 3, axis=-1)
            r = jax.nn.sigmoid(i_r + h_r)
            z = jax.nn.sigmoid(i_z + h_z)
            n = jnp.tanh(i_n + r * h_n)
            return (1.0 - z) * n + z * h
        key = jax.random.key(seed)
        ks = jax.random.split(key, 9)
        h = jax.random.normal(ks[0], (N_NODES, HDIM), dtype=jnp.float32)
        relvectors = jax.random.normal(ks[1], (NUMRELS, HDIM), dtype=jnp.float32)
        s = 1.0 / np.sqrt(HDIM)
        w_ih = jax.random.uniform(ks[2], (3 * HDIM, HDIM), minval=-s, maxval=s, dtype=jnp.float32)
        w_hh = jax.random.uniform(ks[3], (3 * HDIM, HDIM), minval=-s, maxval=s, dtype=jnp.float32)
        b_ih = jax.random.uniform(ks[4], (3 * HDIM,), minval=-s, maxval=s, dtype=jnp.float32)
        b_hh = jax.random.uniform(ks[5], (3 * HDIM,), minval=-s, maxval=s, dtype=jnp.float32)
        edge_src = jax.random.randint(ks[6], (N_EDGES,), 0, N_NODES, dtype=jnp.int32)
        edge_dst = jax.random.randint(ks[7], (N_EDGES,), 0, N_NODES, dtype=jnp.int32)
        edge_rel = jax.random.randint(ks[8], (N_EDGES,), 0, NUMRELS, dtype=jnp.int32)
        return {'h': h, 'relvectors': relvectors, 'w_ih': w_ih, 'w_hh': w_hh, 'b_ih': b_ih, 'b_hh': b_hh, 'edge_src': edge_src, 'edge_dst': edge_dst, 'edge_rel': edge_rel}
    _L1_gnn_all = _L1_gnn_setup()
    _L1_gnn_in = {k: v for k, v in _L1_gnn_all.items() if k in ('relvectors', 'w_ih', 'w_hh', 'b_ih', 'b_hh')}
    del _L1_gnn_all
    return {'x': x, 'src': src, 'dst': dst, 'edge_attr_18': edge_attr_18, 'edge_type_16': edge_type_16, 'L0_gnn_Wqkv': _L0_gnn_in['Wqkv'], 'L0_gnn_bqkv': _L0_gnn_in['bqkv'], 'L0_gnn_Wk_rpe': _L0_gnn_in['Wk_rpe'], 'L0_gnn_bk_rpe': _L0_gnn_in['bk_rpe'], 'L0_gnn_Wq_rpe': _L0_gnn_in['Wq_rpe'], 'L0_gnn_bq_rpe': _L0_gnn_in['bq_rpe'], 'L1_gnn_relvectors': _L1_gnn_in['relvectors'], 'L1_gnn_w_ih': _L1_gnn_in['w_ih'], 'L1_gnn_w_hh': _L1_gnn_in['w_hh'], 'L1_gnn_b_ih': _L1_gnn_in['b_ih'], 'L1_gnn_b_hh': _L1_gnn_in['b_hh']}

def reference(x, src, dst, edge_attr_18, edge_type_16, L0_gnn_Wqkv, L0_gnn_bqkv, L0_gnn_Wk_rpe, L0_gnn_bk_rpe, L0_gnn_Wq_rpe, L0_gnn_bq_rpe, L1_gnn_relvectors, L1_gnn_w_ih, L1_gnn_w_hh, L1_gnn_b_ih, L1_gnn_b_hh):
    import jax
    import jax.numpy as jnp

    def _L0_gnn_ref(x, edge_index, edge_attr, Wqkv, bqkv, Wk_rpe, bk_rpe, Wq_rpe, bq_rpe):
        import jax, jax.numpy as jnp
        import numpy as np
        N, E = (50000, 25000)
        DIM, H, D = (256, 16, 8)
        DH = D * H
        IN_RPE = 18
        SCALE = D ** (-0.5)
        EPS = 1e-16

        def _segment_softmax(compat, s, num_nodes):
            m = jax.ops.segment_max(compat, s, num_segments=num_nodes)
            ex = jnp.exp(compat - m[s])
            den = jax.ops.segment_sum(ex, s, num_segments=num_nodes)
            return ex / (den[s] + EPS)
        n = x.shape[0]
        e = edge_index.shape[1]
        qkv = x @ Wqkv + bqkv
        q = qkv[:, :DH].reshape(n, H, D)
        k = qkv[:, DH:2 * DH].reshape(n, H, D)
        v = qkv[:, 2 * DH:].reshape(n, H, DIM // H)
        s, t = (edge_index[0], edge_index[1])
        qe = q[s] * SCALE
        ke = k[t]
        ke = ke + (edge_attr @ Wk_rpe + bk_rpe).reshape(e, H, D)
        qe = qe + (edge_attr @ Wq_rpe + bq_rpe).reshape(e, H, D)
        compat = jnp.einsum('ehd,ehd->eh', qe, ke)
        attn = _segment_softmax(compat, s, n)
        msg = (v[t] * attn[..., None]).reshape(e, DIM)
        out = jax.ops.segment_sum(msg, s, num_segments=n)
        return out

    def _L1_gnn_ref(h, relvectors, w_ih, w_hh, b_ih, b_hh, edge_src, edge_dst, edge_rel):
        import jax, jax.numpy as jnp
        import numpy as np
        N_NODES = 50000
        N_EDGES = 25000
        HDIM = 256
        NUMRELS = 16

        def _gru_cell(x, h, w_ih, w_hh, b_ih, b_hh):
            gi = x @ w_ih.T + b_ih
            gh = h @ w_hh.T + b_hh
            i_r, i_z, i_n = jnp.split(gi, 3, axis=-1)
            h_r, h_z, h_n = jnp.split(gh, 3, axis=-1)
            r = jax.nn.sigmoid(i_r + h_r)
            z = jax.nn.sigmoid(i_z + h_z)
            n = jnp.tanh(i_n + r * h_n)
            return (1.0 - z) * n + z * h
        msg = h[edge_src] + relvectors[edge_rel]
        red = jax.ops.segment_sum(msg, edge_dst, num_segments=h.shape[0])
        return _gru_cell(red, h, w_ih, w_hh, b_ih, b_hh)
    edge_index = jnp.stack([src, dst])
    x = _layernorm(x + _L0_gnn_ref(x, edge_index, edge_attr_18, L0_gnn_Wqkv, L0_gnn_bqkv, L0_gnn_Wk_rpe, L0_gnn_bk_rpe, L0_gnn_Wq_rpe, L0_gnn_bq_rpe), axis=-1)
    x = _layernorm(x + _L1_gnn_ref(x, L1_gnn_relvectors, L1_gnn_w_ih, L1_gnn_w_hh, L1_gnn_b_ih, L1_gnn_b_hh, src, dst, edge_type_16), axis=-1)
    return x

_drawn_inputs = setup_inputs


def setup_inputs(seed=0):
    import zlib

    import numpy as np

    out = dict(_drawn_inputs(seed))
    spreads = {'L0_gnn_bqkv': (0.0, 0.1), 'L0_gnn_bk_rpe': (0.0, 0.1), 'L0_gnn_bq_rpe': (0.0, 0.1)}
    factors = {'L1_gnn_b_ih': 8.0, 'L1_gnn_b_hh': 8.0}
    for name, (base, spread) in spreads.items():
        noise = np.random.default_rng([zlib.crc32(name.encode()), seed]).standard_normal(out[name].shape)
        drawn = base * np.exp(spread * noise) if base else spread * noise
        out[name] = jnp.asarray(drawn.astype(out[name].dtype))
    for name, factor in factors.items():
        out[name] = (out[name] * factor).astype(out[name].dtype)
    return out
```

```python
from contextlib import ExitStack, contextmanager

import concourse.bass as bass
import numpy as np
from concourse import mybir

ALU = mybir.AluOpType
ACT = mybir.ActivationFunctionType
AX_X = mybir.AxisListType.X
F32 = mybir.dt.float32
BF16 = mybir.dt.bfloat16
I32 = mybir.dt.int32

P = 128
N, E = 3125, 50000
DIM, H, D, RP, NREL = 256, 16, 8, 18, 16
DH = H * D
NT = -(-N // P)
NPAD = NT * P
LAST = N - (NT - 1) * P
EP, EC = 125, 400
G = 8
TWO = 2 * G
J = -(-((E + NT * (P - 1)) // P) // TWO) * TWO
EPAD = E + P
SCALE = D ** -0.5
BIG = 1e30
SKIP = float(1 << 17)

REC = 24
C_ONE, C_SRC, C_DST, C_TYPE, C_RANK = 18, 19, 20, 21, 22
ROW = DIM + DH + REC
KM = DH + REC
UW = DIM + H
LW = DIM + NREL
EPS_SOFTMAX, EPS_NORM = 1e-16, 1e-5


@contextmanager
def chunks(engine, count, body):
    with engine.Fori(0, count // body) as n:
        yield engine.snap(n * body)


def makers(nc, ctx, stage):
    sems = []

    def give_back():
        nc.clear_and_free_semaphores(sems)
        nc.all_engine_barrier()

    def sem(name):
        sems.append(nc.alloc_semaphore(f"{stage}_{name}"))
        return sems[-1]

    ctx.callback(give_back)
    return (lambda name, shape, dt: ctx.enter_context(nc.sbuf_tensor(f"{stage}_{name}", shape, dt)),
            lambda name, shape, dt: ctx.enter_context(nc.psum_tensor(f"{stage}_{name}", shape, dt)), sem)


class Shared:
    pass


def constants(nc, s, sb):
    s.iota = sb("iota", [P, P], F32)
    s.iota_b = sb("iota_b", [P, P], BF16)
    s.pcol = sb("pcol", [P, 1], F32)
    s.before = sb("before", [P, P], F32)
    s.after = sb("after", [P, P], F32)
    s.ident = sb("ident", [P, P], F32)
    s.ident_b = sb("ident_b", [P, P], BF16)
    s.ones = sb("ones", [P, P], F32)
    s.eps = sb("eps", [P, 2], F32)


def stage_constants(nc, s, io):
    with ExitStack() as ctx:
        sb, pb, sem = makers(nc, ctx, "constants")
        attr = sb("attr_in", [EP, EC * RP], F32)
        ints = [sb(f"ints{k}", [EP, EC], I32) for k in range(3)]
        tmp = [sb(f"shifted{k}", [EP, EC], I32) for k in range(4)]
        keysT = [sb(f"keysT{k}", [100, E // 100], I32) for k in range(2)]
        hiTi = [sb(f"hiTi{k}", [100, E // 100], I32) for k in range(2)]
        hiTf = [sb(f"hiTf{k}", [100, E // 100], F32) for k in range(2)]
        iota_i = sb("iota_i", [P, P], I32)
        pcol_i = sb("pcol_i", [P, 1], I32)
        pad = sb("pad", [P, ROW], F32)
        loads, loaded_attr, loadedT = sem("loads"), sem("loaded_attr"), sem("loadedT")
        iotas, filled, base_done, dve_done = sem("iotas"), sem("filled"), sem("base_done"), sem("dve_done")
        pads, hi_out, attr_done = sem("pads"), sem("hi_out"), sem("attr_done")
        with nc.Block() as block:
            @block.sync
            def _(sp):
                for k, name in enumerate(("src", "dst", "type")):
                    sp.dma_start(ints[k][:, :], io[name]).then_inc(loads, 16)
                for k, name in enumerate(("srcT", "dstT")):
                    sp.dma_start(keysT[k][:, :], io[name].rearrange("(a b) c -> a (b c)", a=100)).then_inc(loadedT, 16)
                sp.dma_start(attr[:, :], io["attr"]).then_inc(loaded_attr, 16)
                sp.wait_ge(base_done, 3)
                sp.dma_start(s.rows[E:EPAD, :], pad[:, :]).then_inc(pads, 16)
                sp.dma_start(s.recs[E:EPAD, :], pad[:, DIM + DH:ROW]).then_inc(pads, 16)
                sp.wait_ge(hi_out, 2)
                for k in range(2):
                    sp.dma_start(s.hiT[k].rearrange("(a b) -> a b", a=100), hiTf[k][:, :]).then_inc(pads, 16)
                sp.wait_ge(pads, 64)

            @block.gpsimd
            def _(pool):
                pool.iota(iota_i[:, :], pattern=[[1, P]], base=0, channel_multiplier=0).then_inc(iotas, 1)
                pool.iota(pcol_i[:, :], pattern=[[0, 1]], base=0, channel_multiplier=1).then_inc(iotas, 1)
                for t in (s.ident, s.before, s.after):
                    pool.memset(t[:, :], 0.0 if t is s.ident else 1.0).then_inc(filled, 1)
                pool.wait_ge(filled, 3)
                pool.affine_select(out=s.ident[:, :], in_=s.ident[:, :], compare_op=ALU.not_equal, fill=1.0,
                                   base=0, pattern=[[-1, P]], channel_multiplier=1).then_inc(filled, 1)
                pool.affine_select(out=s.before[:, :], in_=s.before[:, :], compare_op=ALU.is_gt, fill=0.0,
                                   base=0, pattern=[[-1, P]], channel_multiplier=1).then_inc(filled, 1)
                pool.affine_select(out=s.after[:, :], in_=s.after[:, :], compare_op=ALU.is_gt, fill=0.0,
                                   base=0, pattern=[[1, P]], channel_multiplier=-1).then_inc(filled, 1)
                pool.wait_ge(loaded_attr, 16)
                pool.tensor_copy(s.rec[:, :, 0:RP], attr[:, :].rearrange("p (c k) -> p c k", k=RP)).then_inc(attr_done, 1)

            @block.vector
            def _(dve):
                dve.memset(pad[:, :], 0.0).then_inc(base_done, 1)
                dve.wait_ge(base_done, 1)
                dve.memset(pad[:, DIM + DH + C_SRC:DIM + DH + C_SRC + 1], -1.0).then_inc(base_done, 1)
                dve.memset(pad[:, DIM + DH + C_DST:DIM + DH + C_DST + 1], -1.0).then_inc(base_done, 1)
                dve.memset(s.ones[:, :], 1.0).then_inc(dve_done, 1)
                dve.memset(s.rec[:, :, C_ONE:C_ONE + 1], 1.0).then_inc(dve_done, 1)
                dve.memset(s.rec[:, :, REC - 1:REC], 0.0).then_inc(dve_done, 1)
                dve.memset(s.eps[:, 0:1], EPS_NORM).then_inc(dve_done, 1)
                dve.wait_ge(iotas, 2)
                dve.tensor_copy(s.iota[:, :], iota_i[:, :]).then_inc(dve_done, 1)
                dve.tensor_copy(s.iota_b[:, :], iota_i[:, :]).then_inc(dve_done, 1)
                dve.tensor_copy(s.pcol[:, :], pcol_i[:, :]).then_inc(dve_done, 1)
                dve.wait_ge(filled, 4)
                dve.tensor_copy(s.ident_b[:, :], s.ident[:, :]).then_inc(dve_done, 1)
                dve.wait_ge(loadedT, 32)
                for k in range(2):
                    dve.tensor_scalar(hiTi[k][:, :], keysT[k][:, :], 7, None, ALU.arith_shift_right).then_inc(dve_done, 1)
                dve.wait_ge(dve_done, 10)
                for k in range(2):
                    dve.tensor_copy(hiTf[k][:, :], hiTi[k][:, :]).then_inc(hi_out, 1)
                dve.wait_ge(loads, 48)
                for k in range(2):
                    dve.tensor_scalar(tmp[2 * k][:, :], ints[k][:, :], 7, None, ALU.arith_shift_right).then_inc(dve_done, 1)
                    dve.tensor_scalar(tmp[2 * k + 1][:, :], ints[k][:, :], 127, None, ALU.bitwise_and).then_inc(dve_done, 1)
                    dve.tensor_copy(s.key[k][:, :], ints[k][:, :]).then_inc(dve_done, 1)
                for k, c in enumerate((C_SRC, C_DST, C_TYPE)):
                    dve.tensor_copy(s.rec[:, :, c], ints[k][:, :]).then_inc(dve_done, 1)
                dve.wait_ge(dve_done, 19)
                for k in range(2):
                    dve.tensor_copy(s.hi[k][:, :], tmp[2 * k][:, :]).then_inc(dve_done, 1)
                    dve.tensor_copy(s.lo[k][:, :], tmp[2 * k + 1][:, :]).then_inc(dve_done, 1)


def stage_schedule(nc, s, k, hist_ps, psum):
    with ExitStack() as ctx:
        sb, pb, sem = makers(nc, ctx, f"schedule{k}")
        count = sb("count", [NT, P], F32)
        incl = sb("incl", [NT, P], F32)
        small = sb("small", [NT, 8], F32)
        small_i = sb("small_i", [NT, 2], I32)
        wide = sb("wide", [NT, 3, P], F32)
        gone = sb("gone", [NT, J], F32)
        iotaj_i = sb("iotaj_i", [P, J], I32)
        iotaj = sb("iotaj", [P, J], F32)
        fl = sb("fl", [P, 2, J], F32)
        step = sem("step")
        iota_made = sem("iota_made")
        sums = sem("sums")
        pre, pt, pst = psum[1][0:NT, 0:2], psum[2][:, 0:J], psum[3][:, 0:J]
        n_t, nch, t0, c0, cend = (small[:, a:a + 1] for a in range(5))
        with nc.Block() as block:
            @block.gpsimd
            def _(pool):
                pool.iota(iotaj_i[:, :], pattern=[[1, J]], base=0, channel_multiplier=0).then_inc(iota_made, 1)

            @block.tensor
            def _(pe):
                pe.wait_ge(step, 7)
                pe.matmul(pre, s.after[0:NT, 0:NT], small[:, 0:2], start=True, stop=True).then_inc(sums, 1)
                pe.wait_ge(step, 16)
                pe.matmul(pt, wide[:, 0, :], gone[:, :], start=True, stop=True).then_inc(sums, 1)
                pe.matmul(pst, wide[:, 1, :], gone[:, :], start=True, stop=True).then_inc(sums, 1)

            @block.vector
            def _(dve):
                n = [0]

                def link(ins):
                    n[0] += 1
                    ins.then_inc(step, 1)
                    dve.wait_ge(step, n[0])

                link(dve.tensor_copy(count[:, :], hist_ps[0:NT, 0:P]))
                link(dve.tensor_reduce(n_t, count[:, :], AX_X, ALU.add))
                link(dve.tensor_scalar(small[:, 5:6], n_t, float(P - 1), None, ALU.add))
                link(dve.tensor_copy(small_i[:, 0:1], small[:, 5:6]))
                link(dve.tensor_scalar(small_i[:, 1:2], small_i[:, 0:1], 7, None, ALU.arith_shift_right))
                link(dve.tensor_copy(nch, small_i[:, 1:2]))
                link(dve.tensor_tensor_scan(incl[:, :], s.ones[0:NT, :], count[:, :], 0.0, ALU.mult, ALU.add))
                dve.wait_ge(sums, 1)
                link(dve.tensor_copy(small[:, 2:4], pre))
                link(dve.tensor_tensor(incl[:, :], incl[:, :], count[:, :], ALU.subtract))
                link(dve.tensor_scalar(s.start[:, :], incl[:, :], t0, None, ALU.add))
                link(dve.tensor_tensor(cend, c0, nch, ALU.add))
                dve.wait_ge(iota_made, 1)
                link(dve.tensor_copy(iotaj[:, :], iotaj_i[:, :]))
                link(dve.tensor_scalar(gone[:, :], iotaj[0:NT, :], cend, None, ALU.is_ge))
                link(dve.tensor_scalar(small[:, 6:7], nch, -float(P), n_t, ALU.mult, ALU.add))
                link(dve.memset(wide[:, 0, :], 1.0))
                link(dve.tensor_scalar(wide[:, 1, :], s.ones[0:NT, :], small[:, 6:7], None, ALU.mult))
                dve.wait_ge(sums, 3)
                link(dve.tensor_scalar(s.base[k][:, :], pt, float(P), None, ALU.mult))
                link(dve.tensor_scalar(fl[:, 0, :], pt, float(NT - 1), None, ALU.min))
                link(dve.tensor_copy(s.tile_of[k][:, :], fl[0:1, 0, :]))
                link(dve.tensor_scalar(fl[:, 1, :], iotaj[:, :], float(P), None, ALU.mult))
                link(dve.tensor_tensor(fl[:, 1, :], fl[:, 1, :], pst, ALU.add))
                link(dve.tensor_scalar(fl[:, 1, :], fl[:, 1, :], float(E), None, ALU.min))
                link(dve.tensor_copy(s.start_of[k][:, :], fl[0:1, 1, :]))


def stage_rank(nc, s, io, k):
    keyT = io[("srcT", "dstT")[k]]
    with ExitStack() as ctx:
        sb, pb, sem = makers(nc, ctx, f"rank{k}")
        psum = [pb(f"rank_ps{a}", [P, 512], F32) for a in range(6)]
        hist = psum[0]
        Lr = sb("Lr", [EP, G, P], BF16)
        Hr = sb("Hr", [EP, G, NT], BF16)
        zero = sb("zero", [EP, P], BF16)
        counted, lo_made, hi_made, zeroed = sem("counted"), sem("lo_made"), sem("hi_made"), sem("zeroed")
        with nc.Block() as block:
            @block.vector
            def _(dve):
                dve.memset(zero[:, :], 0.0).then_inc(zeroed, 1)
                dve.sem_inc(counted, G)
                with chunks(dve, EC, G) as i:
                    dve.wait_ge(counted, i + G)
                    dve.tensor_tensor(Hr[:, :, :], s.iota[0:EP, None, 0:NT].to_broadcast([EP, G, NT]),
                                      s.hi[k][:, bass.ds(i, G), None].to_broadcast([EP, G, NT]),
                                      ALU.is_equal).then_inc(hi_made, G)
                    for q in range(G):
                        dve.tensor_scalar(Lr[:, q, :], s.iota_b[0:EP, :], s.lo[k][:, bass.ds(i + q, 1)], None,
                                          ALU.is_equal).then_inc(lo_made, 1)

            @block.tensor
            def _(pe):
                pe.wait_ge(zeroed, 1)
                pe.matmul(hist[0:NT, 0:P], zero[:, 0:NT], zero[:, :], start=True, stop=False, skip_group_check=True)
                with chunks(pe, EC, G) as i:
                    pe.wait_ge(hi_made, i + G)
                    for q in range(G):
                        pe.wait_ge(lo_made, i + q + 1)
                        pe.matmul(hist[0:NT, 0:P], Hr[:, q, :], Lr[:, q, :], start=False, stop=False,
                                  skip_group_check=True).then_inc(counted, 1)
        stage_schedule(nc, s, k, hist, psum)

        keyb = sb("keyb", [P, G, EP], I32)
        hib = sb("hib", [32, G, EP], F32)
        HT = sb("HT", [NT, G, EP], F32)
        snap = sb("snap", [NT, G, P], F32)
        junk = sb("junk", [EP, 2, P], F32)
        within = sb("within", [EP, EC], F32)
        ahead = sb("ahead", [EP, EC], F32)
        key_in = [sem(f"key_in{q}") for q in range(G)]
        hi_in = [sem(f"hi_in{q}") for q in range(G)]
        lo2, hi2, counted2, primed = sem("lo2"), sem("hi2"), sem("counted2"), sem("primed")
        hT_made, snapped, looked, read_ahead = sem("hT_made"), sem("snapped"), sem("looked"), sem("read_ahead")
        compared, ranked = sem("compared"), sem("ranked")
        with nc.Block() as block:
            @block.sync
            def _(sp):
                with chunks(sp, EC, G) as i:
                    for q in range(G):
                        sp.wait_ge(compared, i + q + 1)
                        sp.dma_start(keyb[:, q, :], keyT[bass.ds(i + q, 1), :].to_broadcast([P, EP])).then_inc(key_in[q], 16)
                        sp.wait_ge(hT_made, i + q + 1)
                        sp.dma_start(hib[:, q, :], s.hiT2[k][bass.ds(i + q, 1), :].to_broadcast([32, EP])).then_inc(hi_in[q], 16)

            @block.gpsimd
            def _(pool):
                pool.sem_inc(hT_made, G)
                with chunks(pool, EC, G) as i:
                    for q in range(G):
                        pool.wait_ge(hi_in[q], i * 2 + 16)
                        pool.wait_ge(looked, i + q + 1)
                        pool.sem_inc(s.pool_passed, 1)
                        pool.tensor_scalar(HT[:, q, :], hib[0:NT, q, :], s.pcol[0:NT, :], None,
                                           ALU.is_equal).then_inc(hT_made, 1)

            @block.scalar
            def _(act):
                act.wait_ge(primed, 1)
                with chunks(act, EC, G) as i:
                    for q in range(G):
                        act.wait_ge(counted2, i + q + G)
                        act.wait_ge(looked, i + q + 1)
                        act.activation(snap[:, q, :], hist[0:NT, 0:P], ACT.Copy).then_inc(snapped, 1)

            @block.tensor
            def _(pe):
                pe.matmul(hist[0:NT, 0:P], s.ident[0:NT, 0:NT], s.start[:, :], start=True, stop=False,
                          skip_group_check=True).then_inc(primed, 1)
                pe.sem_inc(looked, G)
                with chunks(pe, EC, G) as i:
                    for q in range(G):
                        pe.wait_ge(snapped, i + q + 1)
                        if q == 0:
                            pe.wait_ge(hi2, i + G)
                        pe.wait_ge(lo2, i + q + 1)
                        pe.matmul(hist[0:NT, 0:P], Hr[:, q, :], Lr[:, q, :], start=False, stop=False,
                                  skip_group_check=True).then_inc(counted2, 1)
                        pe.wait_ge(hT_made, i + q + 1 + G)
                        pe.wait_ge(read_ahead, i + q + 1)
                        pe.matmul(psum[1 + q % 4][0:EP, 0:P], HT[:, q, :], snap[:, q, :], start=True,
                                  stop=True).then_inc(looked, 1)

            @block.vector
            def _(dve):
                dve.sem_inc(counted2, G)
                dve.sem_inc(compared, G)
                dve.sem_inc(read_ahead, 4)
                with chunks(dve, EC, G) as i:
                    dve.wait_ge(counted2, i + G)
                    dve.tensor_tensor(Hr[:, :, :], s.iota[0:EP, None, 0:NT].to_broadcast([EP, G, NT]),
                                      s.hi[k][:, bass.ds(i, G), None].to_broadcast([EP, G, NT]),
                                      ALU.is_equal).then_inc(hi2, G)
                    for q in range(G):
                        dve.tensor_scalar(Lr[:, q, :], s.iota_b[0:EP, :], s.lo[k][:, bass.ds(i + q, 1)], None,
                                          ALU.is_equal).then_inc(lo2, 1)
                    for q in range(G):
                        dve.wait_ge(key_in[q], i * 2 + 16)
                        dve.wait_ge(compared, i + q + G)
                        dve.scalar_tensor_tensor(out=junk[:, 0, 0:EP], in0=keyb[0:EP, q, :],
                                                 scalar=s.key[k][:, bass.ds(i + q, 1)], in1=s.before[0:EP, 0:EP],
                                                 op0=ALU.is_equal, op1=ALU.mult,
                                                 accum_out=within[:, bass.ds(i + q, 1)]).then_inc(compared, 1)
                        dve.wait_ge(looked, i + q + 1 + G)
                        dve.wait_ge(read_ahead, i + q + 4)
                        dve.scalar_tensor_tensor(out=junk[:, 1, :], in0=s.iota[0:EP, :],
                                                 scalar=s.lo[k][:, bass.ds(i + q, 1)],
                                                 in1=psum[1 + q % 4][0:EP, 0:P],
                                                 op0=ALU.is_equal, op1=ALU.mult,
                                                 accum_out=ahead[:, bass.ds(i + q, 1)]).then_inc(read_ahead, 1)
                dve.wait_ge(compared, EC + G)
                dve.wait_ge(read_ahead, EC + 4)
                if k == 0:
                    dve.tensor_tensor(s.rec[:, :, C_RANK], within[:, :], ahead[:, :], ALU.add).then_inc(ranked, 1)
                else:
                    dve.tensor_tensor(s.place[:, :], within[:, :], ahead[:, :], ALU.add).then_inc(ranked, 1)


def stage_sort_records(nc, s):
    with ExitStack() as ctx:
        sb, pb, sem = makers(nc, ctx, "sort_records")
        out = [sb(f"rec_out{q}", [EP, REC], F32) for q in range(G)]
        at = sb("rec_at", [EP, G], I32)
        copied, idx_copied = sem("copied"), sem("idx_copied")
        scattered = [sem(f"rec_scattered{q}") for q in range(G)]
        with nc.Block() as block:
            @block.vector
            def _(dve):
                with chunks(dve, EC, G) as i:
                    for q in range(G):
                        dve.wait_ge(scattered[q], i * 2 + 16)
                        dve.tensor_copy(out[q][:, :], s.rec[:, bass.ds(i + q, 1), :]).then_inc(copied, 1)
                        dve.tensor_copy(at[:, q:q + 1], s.place[:, bass.ds(i + q, 1)]).then_inc(idx_copied, 1)

            @block.gpsimd
            def _(pool):
                for q in range(G):
                    pool.dma_start(out[q][:, :], s.recs[E:E + EP, :]).then_inc(scattered[q], 16)
                with chunks(pool, EC, G) as i:
                    for q in range(G):
                        pool.wait_ge(copied, i + q + 1)
                        pool.wait_ge(idx_copied, i + q + 1)
                        pool.sem_inc(s.pool_passed, 1)
                        pool.indirect_dma_start(
                            out=s.recs, out_offset=bass.IndirectOffsetOnAxis(ap=at[:, q:q + 1], axis=0),
                            in_=out[q][:, :], in_offset=None).then_inc(scattered[q], 16)
                for q in range(G):
                    pool.wait_ge(scattered[q], 16 * (EC // G) + 16)


def stage_project(nc, s, io):
    with ExitStack() as ctx:
        sb, pb, sem = makers(nc, ctx, "project")
        ps = [pb(f"proj{a}", [P, 512], F32) for a in range(2)]
        xT = sb("xT", [P, 2, NPAD], F32)
        W = sb("Wqkv", [P, 2, 512], F32)
        b = sb("bqkv", [1, 512], F32)
        full = sb("full", [P, 2, 512], F32)
        rest = sb("rest", [P, 2, 512], F32)
        rest2 = sb("rest2", [P, 2, 512], F32)
        loads, zeroed = sem("loads"), sem("zeroed")
        made, scaled, copied = sem("made"), sem("scaled"), sem("copied")
        top, mid, sub1, sub2 = sem("top"), sem("mid"), sem("sub1"), sem("sub2")
        with nc.Block() as block:
            @block.sync
            def _(sp):
                for a in range(2):
                    sp.dma_start(xT[:, a, 0:N], io["xT"][a * P:(a + 1) * P, :]).then_inc(loads, 16)
                    w = io["Wqkv"][a * P:(a + 1) * P, :]
                    sp.dma_start(W[:, a, 0:DIM], w[:, 2 * DH:]).then_inc(loads, 16)
                    sp.dma_start(W[:, a, DIM:DIM + DH], w[:, DH:2 * DH]).then_inc(loads, 16)
                    sp.dma_start(W[:, a, DIM + DH:], w[:, 0:DH]).then_inc(loads, 16)
                sp.dma_start(b[:, 0:DIM], io["bqkv"][:, 2 * DH:]).then_inc(loads, 16)
                sp.dma_start(b[:, DIM:DIM + DH], io["bqkv"][:, DH:2 * DH]).then_inc(loads, 16)
                sp.dma_start(b[:, DIM + DH:], io["bqkv"][:, 0:DH]).then_inc(loads, 16)

            @block.tensor
            def _(pe):
                pe.wait_ge(loads, 16 * 11)
                pe.wait_ge(zeroed, 1)
                for t in range(NT):
                    if t >= 2:
                        pe.wait_ge(copied, t - 1)
                        pe.wait_ge(scaled, t - 1)
                    for a in range(2):
                        pe.matmul(ps[t % 2][:, :], xT[:, a, t * P:(t + 1) * P], W[:, a, :], start=(a == 0), stop=False)
                    pe.matmul(ps[t % 2][:, :], s.ones[0:1, :], b[:, :], start=False, stop=True).then_inc(made, 1)

            @block.scalar
            def _(act):
                for t in range(NT):
                    act.wait_ge(made, t + 1)
                    if t >= 2:
                        act.wait_ge(top, t - 1)
                        act.wait_ge(sub1, t - 1)
                    act.activation(full[:, t % 2, 0:384], ps[t % 2][:, 0:384], ACT.Copy).then_inc(copied, 1)
                    act.activation(full[:, t % 2, 384:512], ps[t % 2][:, 384:512], ACT.Copy, scale=SCALE).then_inc(scaled, 1)
                    act.wait_ge(copied, t + 1)
                    act.wait_ge(scaled, t + 1)
                    act.activation(s.tab[:, t, 0, :], full[:, t % 2, :], ACT.Copy).then_inc(top, 1)
                    act.wait_ge(sub1, t + 1)
                    act.activation(s.tab[:, t, 1, :], rest[:, t % 2, :], ACT.Copy).then_inc(mid, 1)

            @block.vector
            def _(dve):
                dve.memset(xT[:, :, N:NPAD], 0.0).then_inc(zeroed, 1)
                for t in range(NT):
                    dve.wait_ge(top, t + 1)
                    if t >= 2:
                        dve.wait_ge(sub2, t - 1)
                    dve.tensor_tensor(rest[:, t % 2, :], full[:, t % 2, :], s.tab[:, t, 0, :], ALU.subtract).then_inc(sub1, 1)
                    dve.wait_ge(mid, t + 1)
                    dve.tensor_tensor(s.tab[:, t, 2, :], rest[:, t % 2, :], s.tab[:, t, 1, :], ALU.subtract).then_inc(sub2, 1)


def stage_rows(nc, s):
    with ExitStack() as ctx:
        sb, pb, sem = makers(nc, ctx, "rows")
        psT = [pb(f"psT{a}", [P, 2 * 512], BF16) for a in range(2)]
        psV = [pb(f"psV{a}", [P, 512], F32) for a in range(4)]
        rec = sb("rec_in", [P, 2, G, REC], F32)
        row = [sb(f"row{q}", [P, ROW], F32) for q in range(G)]
        idx = sb("idx", [P, 2, G], I32)
        low = sb("low", [P, 2, G], F32)
        valid = sb("valid", [P, 2, G], F32)
        idxf = sb("idxf", [P, 2, G], F32)
        oh = sb("oh", [P, G, P], BF16)
        ohT = sb("ohT", [P, G, P], BF16)
        rec_in = [sem(f"rec_in{a}") for a in range(2)]
        rec_free, rel_made, low_made = sem("rec_free"), sem("rel_made"), sem("low_made")
        valid_made, idxf_made, idx_made, src_kept = sem("valid_made"), sem("idxf_made"), sem("idx_made"), sem("src_kept")
        type_kept = sem("type_kept")
        oh_made, turned, ohT_made, fetched, evicted = sem("oh_made"), sem("turned"), sem("ohT_made"), sem("fetched"), sem("evicted")
        scattered = [sem(f"row_scattered{q}") for q in range(G)]
        with nc.Block() as block:
            @block.sync
            def _(sp):
                first = [sp.alloc_register(f"rows_first{q}") for q in range(G)]
                with chunks(sp, J, TWO) as i:
                    for half in range(2):
                        g = i + half * G
                        sp.load(first, s.start_of[1][0:1, bass.ds(g, G)])
                        sp.wait_ge(rec_free, g + G)
                        for q in range(G):
                            at = sp.snap(first[q], min_val=0, max_val=E)
                            sp.dma_start(rec[:, half, q, :], s.recs[bass.ds(at, P), :]).then_inc(rec_in[half], 16)

            @block.vector
            def _(dve):
                dve.sem_inc(rec_free, TWO)
                with chunks(dve, J, TWO) as i:
                    for half in range(2):
                        g = i + half * G
                        dve.wait_ge(rec_in[half], i * G + 16 * G)
                        dve.tensor_tensor(s.relD[:, bass.ds(g, G)], rec[:, half, :, C_DST], s.base[1][:, bass.ds(g, G)],
                                          ALU.subtract).then_inc(rel_made, G)
                        dve.tensor_scalar(s.src_of[:, bass.ds(g, G)], rec[:, half, :, C_SRC], 0.0, None,
                                          ALU.max).then_inc(src_kept, 1)
                        dve.tensor_copy(s.type_of[:, bass.ds(g, G)], rec[:, half, :, C_TYPE]).then_inc(type_kept, 1)
                        dve.wait_ge(rel_made, g + G)
                        dve.tensor_scalar(low[:, half, :], s.relD[:, bass.ds(g, G)], 0.0, None, ALU.is_ge).then_inc(low_made, G)
                        dve.wait_ge(low_made, g + G)
                        dve.scalar_tensor_tensor(out=valid[:, half, :], in0=s.relD[:, bass.ds(g, G)], scalar=P - 1.0,
                                                 in1=low[:, half, :], op0=ALU.is_le, op1=ALU.mult).then_inc(valid_made, G)
                        dve.wait_ge(valid_made, g + G)
                        dve.scalar_tensor_tensor(out=idxf[:, half, :], in0=rec[:, half, :, C_RANK], scalar=-SKIP,
                                                 in1=valid[:, half, :], op0=ALU.add, op1=ALU.mult).then_inc(idxf_made, G)
                        dve.wait_ge(idxf_made, g + G)
                        dve.tensor_scalar(idx[:, half, :], idxf[:, half, :], SKIP, None, ALU.add).then_inc(idx_made, G)
                        for q in range(G):
                            dve.wait_ge(turned, g + q + 1)
                            dve.tensor_scalar(oh[:, q, :], s.iota_b[:, :], s.relD[:, bass.ds(g + q, 1)], None,
                                              ALU.is_equal).then_inc(oh_made, 1)
                            dve.wait_ge(scattered[q], i * 2 + 16 * half + 16)
                            dve.tensor_copy(row[q][:, DIM + DH:ROW], rec[:, half, q, :]).then_inc(rec_free, 1)

            @block.tensor
            def _(pe):
                tile = [pe.alloc_register(f"rows_tile{q}") for q in range(G)]
                pe.sem_inc(turned, G)
                with chunks(pe, J, TWO) as i:
                    for half in range(2):
                        g = i + half * G
                        pe.load(tile, s.tile_of[1][0:1, bass.ds(g, G)])

                        def turn(q):
                            pe.wait_ge(oh_made, g + q + 1)
                            pe.wait_ge(ohT_made, g + q + G - 1)
                            pe.transpose(psT[q % 2][:, 0:P], oh[:, q, :], s.ident_b[:, :]).then_inc(turned, 1)

                        turn(0)
                        for q in range(G):
                            if q + 1 < G:
                                turn(q + 1)
                            pe.wait_ge(ohT_made, g + q + 1 + G)
                            pe.wait_ge(evicted, g + q + 1)
                            t = pe.snap(tile[q], min_val=0, max_val=NT - 1)
                            for a in range(3):
                                last = pe.matmul(psV[q % 4][:, 0:DIM + DH], ohT[:, q, :],
                                                 s.tab[:, bass.ds(t, 1), a, 0:DIM + DH], start=(a == 0), stop=(a == 2))
                            last.then_inc(fetched, 1)

            @block.scalar
            def _(act):
                act.sem_inc(ohT_made, G)
                act.sem_inc(evicted, 4)
                with chunks(act, J, TWO) as i:
                    for half in range(2):
                        g = i + half * G

                        def turned_copy(q):
                            act.wait_ge(turned, g + q + 1 + G)
                            act.activation(ohT[:, q, :], psT[q % 2][:, 0:P], ACT.Copy).then_inc(ohT_made, 1)

                        turned_copy(0)
                        for q in range(G):
                            if q + 1 < G:
                                turned_copy(q + 1)
                            act.wait_ge(fetched, g + q + 1)
                            act.wait_ge(scattered[q], i * 2 + 16 * half + 16)
                            act.activation(row[q][:, 0:DIM + DH], psV[q % 4][:, 0:DIM + DH], ACT.Copy).then_inc(evicted, 1)

            @block.gpsimd
            def _(pool):
                for q in range(G):
                    pool.dma_start(row[q][:, :], s.rows[E:EPAD, :]).then_inc(scattered[q], 16)
                with chunks(pool, J, TWO) as i:
                    for half in range(2):
                        g = i + half * G
                        pool.wait_ge(idx_made, g + G)
                        pool.sem_inc(s.pool_passed, 1)
                        for q in range(G):
                            pool.wait_ge(evicted, g + q + 1 + 4)
                            pool.wait_ge(rec_free, g + q + 1 + TWO)
                            pool.sem_inc(s.pool_passed, 1)
                            pool.indirect_dma_start(
                                out=s.rows, out_offset=bass.IndirectOffsetOnAxis(ap=idx[:, half, q:q + 1], axis=0),
                                in_=row[q][:, :], in_offset=None, bounds_check=E - 1,
                                oob_is_err=False).then_inc(scattered[q], 16)
                for q in range(G):
                    pool.wait_ge(scattered[q], 16 * (J // G) + 16)


def stage_scores(nc, s, io):
    with ExitStack() as ctx:
        sb, pb, sem = makers(nc, ctx, "scores")
        psT = [pb(f"psT{a}", [P, 2 * 512], BF16) for a in range(2)]
        psA = [pb(f"psA{a}", [P, 512], F32) for a in range(2)]
        psQ = [pb(f"psQ{a}", [P, 512], F32) for a in range(4)]
        km = sb("km", [P, 2, G, KM], F32)
        Wr = sb("Wr", [RP + 1, 2 * DH], F32)
        low = sb("low", [P, 2, G], F32)
        oh = sb("oh", [P, G, P], BF16)
        ohT = sb("ohT", [P, G, P], BF16)
        aT = sb("aT", [RP + 1, G, P], F32)
        ke = sb("ke", [P, G, DH], F32)
        prod = sb("prod", [P, 2, G, DH], F32)
        km_in = [sem(f"km_in{a}") for a in range(2)]
        w_in, kept, rel_made, low_made = sem("w_in"), sem("kept"), sem("rel_made"), sem("low_made")
        oh_made, turned, ohT_made = sem("oh_made"), sem("turned"), sem("ohT_made")
        a_turned, aT_made, fetched, keyed = sem("a_turned"), sem("aT_made"), sem("fetched"), sem("keyed")
        valid_made, multiplied, summed = sem("valid_made"), sem("multiplied"), sem("summed")
        with nc.Block() as block:
            @block.sync
            def _(sp):
                sp.dma_start(Wr[0:RP, 0:DH], io["Wq_rpe"]).then_inc(w_in, 16)
                sp.dma_start(Wr[0:RP, DH:], io["Wk_rpe"]).then_inc(w_in, 16)
                sp.dma_start(Wr[RP:RP + 1, 0:DH], io["bq_rpe"]).then_inc(w_in, 16)
                sp.dma_start(Wr[RP:RP + 1, DH:], io["bk_rpe"]).then_inc(w_in, 16)
                first = [sp.alloc_register(f"score_first{q}") for q in range(G)]
                with chunks(sp, J, TWO) as i:
                    for half in range(2):
                        g = i + half * G
                        sp.load(first, s.start_of[0][0:1, bass.ds(g, G)])
                        sp.wait_ge(keyed, g + G)
                        for q in range(G):
                            at = sp.snap(first[q], min_val=0, max_val=E)
                            sp.dma_start(km[:, half, q, :], s.rows[bass.ds(at, P), DIM:ROW]).then_inc(km_in[half], 16)

            @block.vector
            def _(dve):
                dve.sem_inc(keyed, TWO)
                with chunks(dve, J, TWO) as i:
                    for half in range(2):
                        g = i + half * G
                        dve.wait_ge(km_in[half], i * G + 16 * G)
                        dve.tensor_copy(s.src_key[:, bass.ds(g, G)], km[:, half, :, DH + C_SRC]).then_inc(kept, 1)
                        dve.tensor_tensor(s.relS[:, bass.ds(g, G)], km[:, half, :, DH + C_SRC],
                                          s.base[0][:, bass.ds(g, G)], ALU.subtract).then_inc(rel_made, G)
                        dve.wait_ge(rel_made, g + G)
                        dve.tensor_scalar(low[:, half, :], s.relS[:, bass.ds(g, G)], 0.0, None, ALU.is_ge).then_inc(low_made, G)
                        dve.wait_ge(low_made, g + G)
                        dve.scalar_tensor_tensor(out=s.validS[:, bass.ds(g, G)], in0=s.relS[:, bass.ds(g, G)],
                                                 scalar=P - 1.0, in1=low[:, half, :],
                                                 op0=ALU.is_le, op1=ALU.mult).then_inc(valid_made, G)

                        def onehot(q):
                            dve.wait_ge(turned, g + q + 1)
                            dve.tensor_scalar(oh[:, q, :], s.iota_b[:, :], s.relS[:, bass.ds(g + q, 1)], None,
                                              ALU.is_equal).then_inc(oh_made, 1)

                        for q in range(3):
                            onehot(q)
                        for q in range(G):
                            if q + 3 < G:
                                onehot(q + 3)
                            dve.wait_ge(fetched, g + q + 2)
                            dve.tensor_tensor(ke[:, q, :], psQ[q % 4][:, DH:2 * DH], km[:, half, q, 0:DH],
                                              ALU.add).then_inc(keyed, 1)
                            dve.wait_ge(keyed, g + q + 1 + TWO)
                            dve.tensor_tensor(prod[:, half, q, :], psQ[q % 4][:, 0:DH], ke[:, q, :],
                                              ALU.mult).then_inc(multiplied, 1)
                        dve.wait_ge(multiplied, g + G + 4)
                        dve.tensor_reduce(s.score[:, bass.ds(g, G), :],
                                          prod[:, half, :, :].rearrange("p g (h d) -> p g h d", d=D),
                                          AX_X, ALU.add).then_inc(summed, 1)

            @block.tensor
            def _(pe):
                tile = [pe.alloc_register(f"score_tile{q}") for q in range(G)]
                pe.sem_inc(turned, G)
                pe.sem_inc(fetched, 1)
                pe.wait_ge(w_in, 64)
                with chunks(pe, J, TWO) as i:
                    for half in range(2):
                        g = i + half * G
                        pe.load(tile, s.tile_of[0][0:1, bass.ds(g, G)])
                        pe.wait_ge(km_in[half], i * G + 16 * G)

                        def turn(q):
                            pe.wait_ge(aT_made, g + q + G - 1)
                            pe.transpose(psA[q % 2][0:RP + 1, 0:P], km[:, half, q, DH:DH + RP + 1],
                                         s.ident[:, :]).then_inc(a_turned, 1)
                            pe.wait_ge(oh_made, g + q + 1)
                            pe.wait_ge(ohT_made, g + q + G - 1)
                            pe.transpose(psT[q % 2][:, 0:P], oh[:, q, :], s.ident_b[:, :]).then_inc(turned, 1)

                        turn(0)
                        for q in range(G):
                            if q + 1 < G:
                                turn(q + 1)
                            pe.wait_ge(aT_made, g + q + 1 + G)
                            pe.wait_ge(multiplied, g + q + 1)
                            pe.matmul(psQ[q % 4][:, 0:2 * DH], aT[:, q, :], Wr[:, :], start=True, stop=False,
                                      skip_group_check=True)
                            pe.wait_ge(ohT_made, g + q + 1 + G)
                            t = pe.snap(tile[q], min_val=0, max_val=NT - 1)
                            for a in range(3):
                                last = pe.matmul(psQ[q % 4][:, 0:DH], ohT[:, q, :],
                                                 s.tab[:, bass.ds(t, 1), a, DIM + DH:], start=False, stop=(a == 2),
                                                 skip_group_check=True)
                            last.then_inc(fetched, 1)

            @block.scalar
            def _(act):
                act.sem_inc(ohT_made, G)
                act.sem_inc(aT_made, G)
                act.sem_inc(multiplied, 4)
                with chunks(act, J, TWO) as i:
                    for half in range(2):
                        g = i + half * G
                        for q in range(G):
                            act.wait_ge(a_turned, g + q + 1)
                            if q == 0:
                                act.wait_ge(fetched, g + 1)
                            act.activation(aT[:, q, :], psA[q % 2][0:RP + 1, 0:P], ACT.Copy).then_inc(aT_made, 1)
                            act.wait_ge(turned, g + q + 1 + G)
                            act.activation(ohT[:, q, :], psT[q % 2][:, 0:P], ACT.Copy).then_inc(ohT_made, 1)


NG = J // G


def stage_softmax(nc, s):
    L = NG * P
    with ExitStack() as ctx:
        sb, pb, sem = makers(nc, ctx, "softmax")
        ps = [pb(f"sm_ps{a}", [P, 512], F32) for a in range(6)]
        sc = sb("sc", [P, L], F32)
        mx = sb("mx", [P, L], F32)
        pen = sb("pen", [P, L + 1], F32)
        key = sb("keyrow", [P, L + 1], F32)
        group_row = sb("group_row", [P, 2, P], F32)
        blk = sb("blk", [P, G], F32)
        head = sb("head", [P, H], F32)
        headT = sb("headT", [H, P], F32)
        less = sb("less", [P, J], F32)
        by_row = sb("by_row", [P, NG, G, H], F32)
        pi = sb("pi", [P, 2], I32)
        pf = sb("pf", [P, 2], F32)
        edge = sb("edge", [P, 3], F32)
        wide = sb("wide", [P, 3 * G], F32)
        small = sb("small", [H, 3 * G], F32)
        carry = sb("carry", [H, G + 1], F32)
        back = sb("back", [P, G], F32)
        carried = sb("carried", [P, 2], F32)
        step, handed, pe_step, masked, key_rows = sem("step"), sem("handed"), sem("pe_step"), sem("masked"), sem("key_rows")
        sc_turned, sc_evicted, exps, ex_turned, ex_evicted = sem("sc_turned"), sem("sc_evicted"), sem("exps"), sem("ex_turned"), sem("ex_evicted")
        key_turned, key_evicted = sem("key_turned"), sem("key_evicted")
        score_v = s.score[:, :, :].rearrange("p (b g) h -> p b g h", g=NG)
        less_v = less[:, :].rearrange("p (b g) -> p b g", g=NG)
        key_v = s.src_key[:, :].rearrange("p (b g) -> p b g", g=NG)
        with nc.Block() as block:
            @block.vector
            def _(dve):
                n = [0, 0]

                def link(ins):
                    n[0] += 1
                    ins.then_inc(step, 1)
                    dve.wait_ge(step, n[0])

                def hand(ins):
                    n[1] += 1
                    ins.then_inc(handed, 1)
                    dve.wait_ge(handed, n[1])

                link(dve.tensor_scalar(less[:, :], s.validS[:, :], 1.0, BIG, ALU.subtract, ALU.mult))
                link(dve.tensor_tensor(s.score[:, :, :], s.score[:, :, :],
                                       s.validS[:, :, None].to_broadcast([P, J, H]), ALU.mult))
                for b in range(G):
                    dve.tensor_tensor(by_row[:, :, b, :], score_v[:, b, :, :],
                                      less_v[:, b, :, None].to_broadcast([P, NG, H]), ALU.add).then_inc(masked, 1)
                link(dve.tensor_copy(pi[:, 0:1], s.pcol[:, :]))
                link(dve.tensor_scalar(pi[:, 1:2], pi[:, 0:1], H - 1, None, ALU.bitwise_and))
                link(dve.tensor_copy(pf[:, 1:2], pi[:, 1:2]))
                link(dve.tensor_tensor(pf[:, 0:1], s.pcol[:, :], pf[:, 1:2], ALU.subtract))
                link(dve.tensor_scalar(head[:, :], s.iota[:, 0:H], pf[:, 1:2], None, ALU.is_equal))
                link(dve.tensor_scalar(blk[:, :], s.iota[:, 0:G], float(H), None, ALU.mult))
                link(dve.tensor_scalar(blk[:, :], blk[:, :], pf[:, 0:1], None, ALU.is_equal))
                for g in range(NG):
                    if g >= 2:
                        dve.wait_ge(key_turned, g - 1)
                    dve.tensor_copy(group_row[:, g % 2, :].rearrange("p (b h) -> p b h", h=H),
                                    key_v[:, :, g, None].to_broadcast([P, G, H])).then_inc(key_rows, 1)
                    if g >= 1:
                        dve.wait_ge(key_turned, g)
                        dve.tensor_copy(key[:, 1 + (g - 1) * P:1 + g * P], ps[(g - 1) % 2][:, 0:P]).then_inc(key_evicted, 1)
                dve.wait_ge(key_turned, NG)
                dve.tensor_copy(key[:, 1 + (NG - 1) * P:1 + NG * P], ps[(NG - 1) % 2][:, 0:P]).then_inc(key_evicted, 1)
                dve.wait_ge(key_evicted, NG)
                hand(dve.tensor_scalar(wide[:, 0:G], blk[:, :], key[:, L:L + 1], None, ALU.mult))
                dve.wait_ge(pe_step, 2)
                link(dve.tensor_copy(headT[:, :], ps[5][0:H, 0:P]))
                link(dve.memset(carry[:, 0:1], -2.0))
                hand(dve.tensor_copy(carry[:, 1:G + 1], ps[4][0:H, 0:G]))
                dve.wait_ge(pe_step, 3)
                link(dve.tensor_tensor(back[:, :], blk[:, :], ps[4][:, 0:G], ALU.mult))
                link(dve.tensor_reduce(key[:, 0:1], back[:, :], AX_X, ALU.add))
                link(dve.tensor_tensor(pen[:, 0:L], key[:, 1:L + 1], key[:, 0:L], ALU.not_equal))
                link(dve.tensor_scalar(pen[:, 0:L], pen[:, 0:L], -BIG, None, ALU.mult))
                link(dve.tensor_reduce(edge[:, 1:2], pen[:, 0:L], AX_X, ALU.min))
                dve.wait_ge(sc_evicted, NG)
                link(dve.tensor_tensor_scan(mx[:, :], pen[:, 0:L], sc[:, :], -BIG, ALU.add, ALU.max))
                link(dve.tensor_copy(edge[:, 0:1], mx[:, L - 1:L]))
                link(dve.tensor_copy(edge[:, 2:3], pen[:, 0:1]))
                for a in range(3):
                    (hand if a == 2 else link)(dve.tensor_scalar(wide[:, a * G:(a + 1) * G], blk[:, :], edge[:, a:a + 1], None, ALU.mult))
                dve.wait_ge(pe_step, 4)
                link(dve.tensor_copy(small[:, :], ps[4][0:H, 0:3 * G]))
                link(dve.memset(carry[:, 0:1], -BIG))
                hand(dve.tensor_tensor_scan(carry[:, 1:G + 1], small[:, G:2 * G], small[:, 0:G], -BIG, ALU.add, ALU.max))
                dve.wait_ge(pe_step, 5)
                link(dve.tensor_tensor(back[:, :], blk[:, :], ps[4][:, 0:G], ALU.mult))
                link(dve.tensor_reduce(carried[:, 0:1], back[:, :], AX_X, ALU.add))
                link(dve.tensor_tensor_scan(mx[:, :], pen[:, 0:L], sc[:, :], carried[:, 0:1], ALU.add, ALU.max))
                link(dve.memset(carry[:, G:G + 1], -BIG))
                link(dve.tensor_copy(carry[:, 0:G - 1], small[:, 2 * G + 1:3 * G]))
                hand(dve.memset(carry[:, G - 1:G], -BIG))
                dve.wait_ge(pe_step, 6)
                link(dve.tensor_tensor(back[:, :], blk[:, :], ps[4][:, 0:G], ALU.mult))
                link(dve.tensor_reduce(pen[:, L:L + 1], back[:, :], AX_X, ALU.add))
                link(dve.tensor_reduce(edge[:, 1:2], pen[:, 1:L + 1], AX_X, ALU.min))
                link(dve.tensor_tensor_scan(key[:, 0:L][:, ::-1], pen[:, 1:L + 1][:, ::-1], mx[:, :][:, ::-1],
                                            -BIG, ALU.add, ALU.max))
                link(dve.tensor_copy(edge[:, 0:1], key[:, 0:1]))
                for a in range(2):
                    (hand if a == 1 else link)(dve.tensor_scalar(wide[:, a * G:(a + 1) * G], blk[:, :], edge[:, a:a + 1], None, ALU.mult))
                dve.wait_ge(pe_step, 7)
                link(dve.tensor_copy(small[:, 0:2 * G], ps[4][0:H, 0:2 * G]))
                link(dve.memset(carry[:, G - 1:G], -BIG))
                hand(dve.tensor_tensor_scan(carry[:, 0:G - 1][:, ::-1], small[:, G + 1:2 * G][:, ::-1],
                                            small[:, 1:G][:, ::-1], -BIG, ALU.add, ALU.max))
                dve.wait_ge(pe_step, 8)
                link(dve.tensor_tensor(back[:, :], blk[:, :], ps[4][:, 0:G], ALU.mult))
                link(dve.tensor_reduce(carried[:, 1:2], back[:, :], AX_X, ALU.add))
                link(dve.tensor_tensor_scan(key[:, 0:L][:, ::-1], pen[:, 1:L + 1][:, ::-1], mx[:, :][:, ::-1],
                                            carried[:, 1:2], ALU.add, ALU.max))
                hand(dve.tensor_tensor(sc[:, :], sc[:, :], key[:, 0:L], ALU.subtract))

            @block.scalar
            def _(act):
                for g in range(NG):
                    act.wait_ge(sc_turned, g + 1)
                    act.activation(sc[:, g * P:(g + 1) * P], ps[2 + g % 2][:, 0:P], ACT.Copy).then_inc(sc_evicted, 1)
                act.wait_ge(handed, 8)
                for g in range(NG):
                    act.activation(sc[:, g * P:(g + 1) * P], sc[:, g * P:(g + 1) * P], ACT.Exp).then_inc(exps, 1)
                for g in range(NG):
                    act.wait_ge(ex_turned, g + 1)
                    act.activation(s.score[:, :, :].rearrange("p (b g) h -> p b g h", g=NG)[:, :, g, :],
                                   ps[g % 2][:, 0:P].rearrange("p (b h) -> p b h", h=H), ACT.Copy).then_inc(ex_evicted, 1)

            @block.tensor
            def _(pe):
                def spread(after):
                    pe.wait_ge(handed, after)
                    pe.matmul(ps[4][:, 0:G], headT[:, :], carry[:, 0:G], start=True, stop=True).then_inc(pe_step, 1)

                def gather(after, m):
                    pe.wait_ge(handed, after)
                    pe.matmul(ps[4][0:H, 0:m], head[:, :], wide[:, 0:m], start=True, stop=True).then_inc(pe_step, 1)

                for g in range(NG):
                    pe.wait_ge(key_rows, g + 1)
                    if g >= 2:
                        pe.wait_ge(key_evicted, g - 1)
                    pe.transpose(ps[g % 2][:, 0:P], group_row[:, g % 2, :], s.ident[:, :]).then_inc(key_turned, 1)
                pe.wait_ge(masked, G)
                for g in range(NG):
                    if g >= 2:
                        pe.wait_ge(sc_evicted, g - 1)
                    pe.transpose(ps[2 + g % 2][:, 0:P], by_row[:, g, :, :].rearrange("p b h -> p (b h)"), s.ident[:, :]).then_inc(sc_turned, 1)
                gather(1, G)
                pe.transpose(ps[5][0:H, 0:P], head[:, :], s.ident[:, :]).then_inc(pe_step, 1)
                spread(2)
                gather(3, 3 * G)
                spread(4)
                spread(5)
                gather(6, 2 * G)
                spread(7)
                for g in range(NG):
                    pe.wait_ge(exps, g + 1)
                    if g >= 2:
                        pe.wait_ge(ex_evicted, g - 1)
                    pe.transpose(ps[g % 2][:, 0:P], sc[:, g * P:(g + 1) * P], s.ident[:, :]).then_inc(ex_turned, 1)


def stage_attend(nc, s):
    with ExitStack() as ctx:
        sb, pb, sem = makers(nc, ctx, "attend")
        ps = [pb(f"att_ps{a}", [P, 512], F32) for a in range(4)]
        val = sb("val", [P, 2, G, DIM], F32)
        msg = sb("msg", [P, 2, G, UW], F32)
        oh = sb("oh", [P, G, P], F32)
        val_in = [sem(f"val_in{a}") for a in range(2)]
        weighted, copied, oh_made, summed, added, zeroed = (sem("weighted"), sem("copied"), sem("oh_made"),
                                                            sem("summed"), sem("added"), sem("zeroed"))
        with nc.Block() as block:
            @block.sync
            def _(sp):
                first = [sp.alloc_register(f"att_first{q}") for q in range(G)]
                with chunks(sp, J, TWO) as i:
                    for half in range(2):
                        g = i + half * G
                        sp.load(first, s.start_of[0][0:1, bass.ds(g, G)])
                        sp.wait_ge(weighted, g + G)
                        for q in range(G):
                            at = sp.snap(first[q], min_val=0, max_val=E)
                            sp.dma_start(val[:, half, q, :], s.rows[bass.ds(at, P), 0:DIM]).then_inc(val_in[half], 16)

            @block.gpsimd
            def _(pool):
                pool.sem_inc(weighted, TWO)
                with chunks(pool, J, TWO) as i:
                    for half in range(2):
                        g = i + half * G
                        pool.wait_ge(val_in[half], i * G + 16 * G)
                        for q in range(G):
                            pool.wait_ge(summed, g + q + 1)
                            pool.tensor_tensor(msg[:, half, q, 0:DIM].rearrange("p (h d) -> p h d", h=H),
                                               val[:, half, q, :].rearrange("p (h d) -> p h d", h=H),
                                               s.score[:, bass.ds(g + q, 1), :].rearrange("p o h -> p h o").to_broadcast([P, H, DIM // H]),
                                               ALU.mult).then_inc(weighted, 1)

            @block.scalar
            def _(act):
                with chunks(act, J, TWO) as i:
                    for half in range(2):
                        g = i + half * G
                        act.wait_ge(summed, g + G)
                        act.activation(msg[:, half, :, DIM:UW], s.score[:, bass.ds(g, G), :], ACT.Copy).then_inc(copied, G)

            @block.tensor
            def _(pe):
                pe.sem_inc(summed, TWO)
                with chunks(pe, J, TWO) as i:
                    for half in range(2):
                        g = i + half * G
                        pe.wait_ge(copied, g + G)
                        for q in range(G):
                            pe.wait_ge(oh_made, g + q + 1)
                            pe.wait_ge(weighted, g + q + 1 + TWO)
                            pe.wait_ge(added, g + q + 1)
                            pe.matmul(ps[q % 4][:, 0:UW], oh[:, q, :], msg[:, half, q, :], start=True,
                                      stop=True).then_inc(summed, 1)

            @block.vector
            def _(dve):
                tile = [dve.alloc_register(f"att_tile{q}") for q in range(G)]
                dve.sem_inc(added, 4)
                dve.memset(s.acc[:, :, :], 0.0).then_inc(zeroed, 1)
                dve.wait_ge(zeroed, 1)
                with chunks(dve, J, G) as g:
                    dve.load(tile, s.tile_of[0][0:1, bass.ds(g, G)])

                    def onehot(q):
                        dve.wait_ge(summed, g + q + 1 + G)
                        dve.tensor_scalar(oh[:, q, :], s.iota[:, :], s.relS[:, bass.ds(g + q, 1)], None,
                                          ALU.is_equal).then_inc(oh_made, 1)

                    for q in range(3):
                        onehot(q)
                    for q in range(G):
                        if q + 3 < G:
                            onehot(q + 3)
                        t = dve.snap(tile[q], min_val=0, max_val=NT - 1)
                        dve.wait_ge(summed, g + q + 1 + TWO)
                        dve.wait_ge(added, g + q + 4)
                        dve.tensor_tensor(s.acc[:, bass.ds(t, 1), :], s.acc[:, bass.ds(t, 1), :],
                                          ps[q % 4][:, None, 0:UW], ALU.add).then_inc(added, 1)


def stage_norm(nc, s, io):
    with ExitStack() as ctx:
        sb, pb, sem = makers(nc, ctx, "norm")
        x = sb("x_rows", [P, NT, DIM], F32)
        den = sb("den", [P, NT, H], F32)
        rden = sb("rden", [P, NT, H], F32)
        stats = sb("stats", [P, NT, 6], F32)
        mv = sb("mv", [P, NT, 2], F32)
        std = sb("std", [P, NT], F32)
        rstd = sb("rstd", [P, NT], F32)
        x_in, step, normed, rooted, stored = sem("x_in"), sem("step"), sem("normed"), sem("rooted"), sem("stored")
        full = NT - 1
        with nc.Block() as block:
            @block.sync
            def _(sp):
                sp.wait_ge(step, 1)
                sp.dma_start(x[:, 0:full, :], io["x"][0:full * P, :].rearrange("(t p) f -> p t f", p=P)).then_inc(x_in, 16)
                sp.dma_start(x[0:LAST, full, :], io["x"][full * P:N, :]).then_inc(x_in, 16)
                sp.wait_ge(normed, NT)
                sp.dma_start(s.h_dram[0:full * P, :].rearrange("(t p) f -> p t f", p=P), s.h[:, 0:full, :]).then_inc(stored, 16)
                sp.dma_start(s.h_dram[full * P:N, :], s.h[0:LAST, full, :]).then_inc(stored, 16)
                sp.wait_ge(stored, 32)

            @block.scalar
            def _(act):
                act.wait_ge(step, 5)
                act.activation(std[:, :], mv[:, :, 1], ACT.Sqrt, bias=s.eps[:, 0:1]).then_inc(rooted, 1)

            @block.vector
            def _(dve):
                n = [0]

                def link(ins):
                    n[0] += 1
                    ins.then_inc(step, 1)
                    dve.wait_ge(step, n[0])

                link(dve.memset(x[:, full, :], 0.0))
                link(dve.tensor_scalar(den[:, :, :], s.acc[:, :, DIM:UW], EPS_SOFTMAX, None, ALU.add))
                link(dve.reciprocal(rden[:, :, :], den[:, :, :]))
                for t in range(NT):
                    ins = dve.tensor_tensor(s.h[:, t, :].rearrange("p (h d) -> p h d", h=H),
                                            s.acc[:, t, 0:DIM].rearrange("p (h d) -> p h d", h=H),
                                            rden[:, t, :, None].to_broadcast([P, H, DIM // H]), ALU.mult)
                    if t == NT - 1:
                        link(ins)
                dve.wait_ge(x_in, 32)
                for t in range(NT):
                    dve.tensor_tensor(s.h[:, t, :], s.h[:, t, :], x[:, t, :], ALU.add).then_inc(s.sum_made, 1)
                dve.wait_ge(s.sum_made, NT)
                for t in range(NT):
                    dve.bn_stats(stats[:, t, :], s.h[:, t, :]).then_inc(s.sum_made, 1)
                dve.wait_ge(s.sum_made, 2 * NT)
                for t in range(NT):
                    ins = dve.bn_aggr(mv[:, t, :], stats[:, t, :])
                    if t == NT - 1:
                        link(ins)
                dve.wait_ge(rooted, 1)
                link(dve.reciprocal(rstd[:, :], std[:, :]))
                for t in range(NT):
                    dve.tensor_scalar(s.h[:, t, :], s.h[:, t, :], mv[:, t, 0:1], rstd[:, t:t + 1],
                                      ALU.subtract, ALU.mult).then_inc(normed, 1)


def stage_neighbours(nc, s):
    with ExitStack() as ctx:
        sb, pb, sem = makers(nc, ctx, "neighbours")
        ps = [pb(f"nb_ps{a}", [P, 512], F32) for a in range(4)]
        nbr = [sb(f"nbr{q}", [P, LW], F32) for q in range(TWO)]
        idx = sb("nb_idx", [P, 2, G], I32)
        oh = sb("oh", [P, G, P], F32)
        gathered = [sem(f"gathered{q}") for q in range(TWO)]
        idx_made, typed, oh_made, summed, added, zeroed = (sem("idx_made"), sem("typed"), sem("oh_made"),
                                                           sem("summed"), sem("added"), sem("zeroed"))
        with nc.Block() as block:
            @block.gpsimd
            def _(pool):
                with chunks(pool, J, TWO) as i:
                    for half in range(2):
                        g = i + half * G
                        pool.wait_ge(idx_made, g + G)
                        pool.sem_inc(s.pool_passed, 1)
                        for q in range(G):
                            pool.wait_ge(summed, g + q + 1)
                            pool.sem_inc(s.pool_passed, 1)
                            pool.indirect_dma_start(
                                out=nbr[half * G + q][:, 0:DIM], out_offset=None, in_=s.h_dram,
                                in_offset=bass.IndirectOffsetOnAxis(ap=idx[:, half, q:q + 1], axis=0)
                            ).then_inc(gathered[half * G + q], 16)

            @block.tensor
            def _(pe):
                pe.sem_inc(summed, TWO)
                with chunks(pe, J, TWO) as i:
                    for half in range(2):
                        g = i + half * G
                        for q in range(G):
                            pe.wait_ge(typed, g + q + 1)
                            pe.wait_ge(oh_made, g + q + 1)
                            pe.wait_ge(gathered[half * G + q], i + 16)
                            pe.wait_ge(added, g + q + 1)
                            pe.matmul(ps[q % 4][:, 0:LW], oh[:, q, :], nbr[half * G + q][:, :], start=True,
                                      stop=True).then_inc(summed, 1)

            @block.vector
            def _(dve):
                tile = [dve.alloc_register(f"nb_tile{q}") for q in range(G)]
                dve.sem_inc(added, 4)
                dve.memset(s.acc2[:, :, :], 0.0).then_inc(zeroed, 1)
                dve.wait_ge(zeroed, 1)
                with chunks(dve, J, TWO) as i:
                    for half in range(2):
                        g = i + half * G
                        dve.load(tile, s.tile_of[1][0:1, bass.ds(g, G)])
                        dve.wait_ge(summed, g + G)
                        dve.tensor_copy(idx[:, half, :], s.src_of[:, bass.ds(g, G)]).then_inc(idx_made, G)

                        def onehot(q):
                            dve.wait_ge(summed, g + q + 1 + G)
                            dve.tensor_scalar(oh[:, q, :], s.iota[:, :], s.relD[:, bass.ds(g + q, 1)], None,
                                              ALU.is_equal).then_inc(oh_made, 1)
                            dve.tensor_scalar(nbr[half * G + q][:, DIM:LW], s.iota[:, 0:NREL],
                                              s.type_of[:, bass.ds(g + q, 1)], None, ALU.is_equal).then_inc(typed, 1)

                        for q in range(3):
                            onehot(q)
                        for q in range(G):
                            if q + 3 < G:
                                onehot(q + 3)
                            t = dve.snap(tile[q], min_val=0, max_val=NT - 1)
                            dve.wait_ge(summed, g + q + 1 + TWO)
                            dve.wait_ge(added, g + q + 4)
                            dve.tensor_tensor(s.acc2[:, bass.ds(t, 1), :], s.acc2[:, bass.ds(t, 1), :],
                                              ps[q % 4][:, None, 0:LW], ALU.add).then_inc(added, 1)


def stage_gru(nc, s, io, out):
    with ExitStack() as ctx:
        sb, pb, sem = makers(nc, ctx, "gru")
        psC = pb("psC", [P, 512], F32)
        psX = [pb(f"psX{a}", [P, 512], F32) for a in range(2)]
        psRZ = [pb(f"psRZ{a}", [P, 512], F32) for a in range(2)]
        psN = [pb(f"psN{a}", [P, 512], F32) for a in range(2)]
        wi = sb("wi", [P, 2, 3 * DIM], F32)
        wh = sb("wh", [P, 2, 3 * DIM], F32)
        bi = sb("bi", [1, 3 * DIM], F32)
        bh = sb("bh", [1, 3 * DIM], F32)
        rel = sb("rel", [NREL, DIM], F32)
        cT = sb("cT", [NREL, 2, P], F32)
        redT = sb("redT", [P, 2, 2, P], F32)
        hT = sb("hT", [P, 2, 2, P], F32)
        rz = sb("rz", [P, 2, 512], F32)
        nn = sb("nn", [P, 2, DIM], F32)
        w1 = sb("w1", [P, 2, DIM], F32)
        w2 = sb("w2", [P, 2, DIM], F32)
        stats = sb("stats", [P, 2, 6], F32)
        mv = sb("mv", [P, 2, 2], F32)
        std = sb("std", [P, 2], F32)
        rstd = sb("rstd", [P, 2], F32)
        y = sb("y", [P, 4, DIM], F32)
        loads, c_turned, cT_made, turned, T_made = sem("loads"), sem("c_turned"), sem("cT_made"), sem("turned"), sem("T_made")
        gates, gates_n, sig, tanh_done, rooted = sem("gates"), sem("gates_n"), sem("sig"), sem("tanh_done"), sem("rooted")
        step = sem("step")
        stored = [sem(f"stored{a}") for a in range(4)]
        S = 9
        with nc.Block() as block:
            @block.sync
            def _(sp):
                for a in range(2):
                    sp.dma_start(wi[:, a, :], io["wihT"][a * P:(a + 1) * P, :]).then_inc(loads, 16)
                    sp.dma_start(wh[:, a, :], io["whhT"][a * P:(a + 1) * P, :]).then_inc(loads, 16)
                sp.dma_start(bi[:, :], io["b_ih"]).then_inc(loads, 16)
                sp.dma_start(bh[:, :], io["b_hh"]).then_inc(loads, 16)
                sp.dma_start(rel[:, :], io["rel"]).then_inc(loads, 16)
                for t in range(NT):
                    rows = P if t < NT - 1 else LAST
                    sp.wait_ge(step, S * (t + 1))
                    sp.dma_start(out[t * P:t * P + rows, :], y[0:rows, t % 4, :]).then_inc(stored[t % 4], 16)
                for a in range(4):
                    sp.wait_ge(stored[a], 16 * len(range(a, NT, 4)))

            @block.tensor
            def _(pe):
                pe.wait_ge(loads, 16 * 7)

                def prepare(t):
                    b = t % 2
                    if t >= 1:
                        pe.wait_ge(cT_made, t)
                    pe.transpose(psC[0:NREL, 0:P], s.acc2[:, t, DIM:LW], s.ident[:, :]).then_inc(c_turned, 1)
                    if t >= 2:
                        pe.wait_ge(T_made, 2 * (t - 1))
                    for a in range(2):
                        pe.transpose(psX[b][:, 256 + a * P:256 + (a + 1) * P], s.h[:, t, a * P:(a + 1) * P], s.ident[:, :])
                    pe.wait_ge(cT_made, t + 1)
                    for a in range(2):
                        pe.matmul(psX[b][:, a * P:(a + 1) * P], s.acc2[:, t, a * P:(a + 1) * P], s.ident[:, :],
                                  start=True, stop=False)
                        last = pe.matmul(psX[b][:, a * P:(a + 1) * P], rel[:, a * P:(a + 1) * P], cT[:, b, :],
                                         start=False, stop=True)
                    last.then_inc(turned, 1)

                prepare(0)
                for t in range(NT):
                    b = t % 2
                    if t + 1 < NT:
                        prepare(t + 1)
                    pe.wait_ge(T_made, 2 * (t + 1))
                    if t >= 2:
                        pe.wait_ge(sig, t - 1)
                        pe.wait_ge(step, S * (t - 2) + 2)
                    pe.matmul(psRZ[b][:, :], s.ones[0:1, :], bi[:, 0:512], start=True, stop=False)
                    pe.matmul(psRZ[b][:, :], s.ones[0:1, :], bh[:, 0:512], start=False, stop=False)
                    for a in range(2):
                        pe.matmul(psRZ[b][:, :], redT[:, b, a, :], wi[:, a, 0:512], start=False, stop=False)
                    for a in range(2):
                        last = pe.matmul(psRZ[b][:, :], hT[:, b, a, :], wh[:, a, 0:512], start=False, stop=(a == 1))
                    last.then_inc(gates, 1)
                    pe.matmul(psN[b][:, 0:DIM], s.ones[0:1, :], bi[:, 512:], start=True, stop=False)
                    for a in range(2):
                        pe.matmul(psN[b][:, 0:DIM], redT[:, b, a, :], wi[:, a, 512:], start=False, stop=(a == 1))
                    pe.matmul(psN[b][:, DIM:], s.ones[0:1, :], bh[:, 512:], start=True, stop=False)
                    for a in range(2):
                        last = pe.matmul(psN[b][:, DIM:], hT[:, b, a, :], wh[:, a, 512:], start=False, stop=(a == 1))
                    last.then_inc(gates_n, 1)

            @block.scalar
            def _(act):
                def copies(t):
                    b = t % 2
                    act.wait_ge(c_turned, t + 1)
                    act.activation(cT[:, b, :], psC[0:NREL, 0:P], ACT.Copy).then_inc(cT_made, 1)
                    act.wait_ge(turned, t + 1)
                    if t >= 2:
                        act.wait_ge(gates_n, t - 1)
                    act.activation(redT[:, b, :, :], psX[b][:, 0:256].rearrange("p (a n) -> p a n", a=2), ACT.Copy).then_inc(T_made, 1)
                    act.activation(hT[:, b, :, :], psX[b][:, 256:512].rearrange("p (a n) -> p a n", a=2), ACT.Copy).then_inc(T_made, 1)

                copies(0)
                for t in range(NT):
                    b = t % 2
                    if t + 1 < NT:
                        copies(t + 1)
                    act.wait_ge(gates, t + 1)
                    if t >= 2:
                        act.wait_ge(step, S * (t - 2) + 5)
                    act.activation(rz[:, b, :], psRZ[b][:, :], ACT.Sigmoid).then_inc(sig, 1)
                    act.wait_ge(step, S * t + 2)
                    act.activation(nn[:, b, :], w2[:, b, :], ACT.Tanh).then_inc(tanh_done, 1)
                    act.wait_ge(step, S * t + 7)
                    act.activation(std[:, b:b + 1], mv[:, b, 1:2], ACT.Sqrt, bias=s.eps[:, 0:1]).then_inc(rooted, 1)

            @block.vector
            def _(dve):
                n = [0]

                def link(ins):
                    n[0] += 1
                    ins.then_inc(step, 1)
                    dve.wait_ge(step, n[0])

                for t in range(NT):
                    b = t % 2
                    dve.wait_ge(sig, t + 1)
                    dve.wait_ge(gates_n, t + 1)
                    link(dve.tensor_tensor(w1[:, b, :], rz[:, b, 0:DIM], psN[b][:, DIM:], ALU.mult))
                    link(dve.tensor_tensor(w2[:, b, :], w1[:, b, :], psN[b][:, 0:DIM], ALU.add))
                    dve.wait_ge(tanh_done, t + 1)
                    link(dve.tensor_tensor(w1[:, b, :], s.h[:, t, :], nn[:, b, :], ALU.subtract))
                    link(dve.tensor_tensor(w2[:, b, :], rz[:, b, DIM:], w1[:, b, :], ALU.mult))
                    link(dve.tensor_tensor(w1[:, b, :], w2[:, b, :], nn[:, b, :], ALU.add))
                    dve.tensor_tensor(w2[:, b, :], w1[:, b, :], s.h[:, t, :], ALU.add).then_inc(s.sum_made2, 1)
                    dve.wait_ge(s.sum_made2, t + 1)
                    link(dve.bn_stats(stats[:, b, :], w2[:, b, :]))
                    link(dve.bn_aggr(mv[:, b, :], stats[:, b, :]))
                    dve.wait_ge(rooted, t + 1)
                    link(dve.reciprocal(rstd[:, b:b + 1], std[:, b:b + 1]))
                    if t >= 4:
                        dve.wait_ge(stored[t % 4], 16 * (t // 4))
                    link(dve.tensor_scalar(y[:, t % 4, :], w2[:, b, :], mv[:, b, 0:1], rstd[:, b:b + 1],
                                           ALU.subtract, ALU.mult))


def build(nc, io, out, upto=99):
    s = Shared()
    dram = lambda n, sh, dt: nc.dram_tensor(n, sh, dt, kind="Internal").ap()
    s.rows = dram("rows", (EPAD, ROW), F32)
    s.recs = dram("recs", (EPAD, REC), F32)
    s.h_dram = dram("h_rows", (N, DIM), F32)
    s.hiT = [dram(f"hiT{k}", (E,), F32) for k in range(2)]
    s.hiT2 = [a.rearrange("(c p) -> c p", p=EP) for a in s.hiT]
    with ExitStack() as ctx:
        sb = lambda n, sh, dt: ctx.enter_context(nc.sbuf_tensor(n, sh, dt))
        constants(nc, s, sb)
        s.sum_made = ctx.enter_context(nc.semaphore("sum_made"))
        s.pool_passed = ctx.enter_context(nc.semaphore("pool_passed"))
        s.sum_made2 = ctx.enter_context(nc.semaphore("sum_made2"))
        s.tile_of = [sb(f"tile_of{k}", [1, J], I32) for k in range(2)]
        s.start_of = [sb(f"start_of{k}", [1, J], I32) for k in range(2)]
        s.base = [sb(f"base{k}", [P, J], F32) for k in range(2)]
        with ExitStack() as early:
            sbe = lambda n, sh, dt: early.enter_context(nc.sbuf_tensor(n, sh, dt))
            s.start = sbe("start", [NT, P], F32)
            s.rec = sbe("rec", [EP, EC, REC], F32)
            s.place = sbe("place", [EP, EC], F32)
            s.key = [sbe(f"key{k}", [EP, EC], F32) for k in range(2)]
            s.hi = [sbe(f"hi{k}", [EP, EC], F32) for k in range(2)]
            s.lo = [sbe(f"lo{k}", [EP, EC], F32) for k in range(2)]
            stage_constants(nc, s, io)
            stage_rank(nc, s, io, 0)
            stage_rank(nc, s, io, 1)
            stage_sort_records(nc, s)
        s.relD = sb("relD", [P, J], F32)
        s.src_of = sb("src_of", [P, J], I32)
        s.type_of = sb("type_of", [P, J], F32)
        s.h = sb("h", [P, NT, DIM], F32)
        with ExitStack() as layer0:
            sbl = lambda n, sh, dt: layer0.enter_context(nc.sbuf_tensor(n, sh, dt))
            s.relS = sbl("relS", [P, J], F32)
            s.validS = sbl("validS", [P, J], F32)
            s.src_key = sbl("src_key", [P, J], F32)
            s.score = sbl("score", [P, J, H], F32)
            with ExitStack() as tables:
                s.tab = tables.enter_context(nc.sbuf_tensor("tab", [P, NT, 3, 512], BF16))
                stage_project(nc, s, io)
                stage_rows(nc, s)
                stage_scores(nc, s, io)
            stage_softmax(nc, s)
            s.acc = sbl("acc", [P, NT, UW], F32)
            stage_attend(nc, s)
            stage_norm(nc, s, io)
        s.acc2 = sb("acc2", [P, NT, LW], F32)
        stage_neighbours(nc, s)
        stage_gru(nc, s, io, out)


def kernel(x, src, dst, edge_attr_18, edge_type_16, L0_gnn_Wqkv, L0_gnn_bqkv, L0_gnn_Wk_rpe, L0_gnn_bk_rpe,
           L0_gnn_Wq_rpe, L0_gnn_bq_rpe, L1_gnn_relvectors, L1_gnn_w_ih, L1_gnn_w_hh, L1_gnn_b_ih, L1_gnn_b_hh):
    import concourse.bacc as bacc
    from concourse.bass_utils import run_bass_kernel_spmd

    row = lambda a: np.asarray(a).reshape(1, -1)
    grid = lambda a: np.asarray(a).reshape(EP, EC)
    layout = {
        "x": np.asarray(x), "xT": np.asarray(x).T,
        "src": grid(src), "dst": grid(dst), "type": grid(edge_type_16),
        "srcT": grid(src).T, "dstT": grid(dst).T,
        "attr": np.asarray(edge_attr_18).reshape(EP, EC * RP),
        "Wqkv": np.asarray(L0_gnn_Wqkv), "bqkv": row(L0_gnn_bqkv),
        "Wk_rpe": np.asarray(L0_gnn_Wk_rpe), "bk_rpe": row(L0_gnn_bk_rpe),
        "Wq_rpe": np.asarray(L0_gnn_Wq_rpe), "bq_rpe": row(L0_gnn_bq_rpe),
        "rel": np.asarray(L1_gnn_relvectors),
        "wihT": np.asarray(L1_gnn_w_ih).T, "whhT": np.asarray(L1_gnn_w_hh).T,
        "b_ih": row(L1_gnn_b_ih), "b_hh": row(L1_gnn_b_hh),
    }
    layout = {name: np.ascontiguousarray(a) for name, a in layout.items()}
    nc = bacc.Bacc("TRN2", target_bir_lowering=False, num_devices=1)
    io = {name: nc.dram_tensor(f"in_{name}", a.shape, mybir.dt.from_np(a.dtype), kind="ExternalInput").ap()
          for name, a in layout.items()}
    out = nc.dram_tensor("out", (N, DIM), F32, kind="ExternalOutput").ap()
    build(nc, io, out)
    r = run_bass_kernel_spmd(nc, [{f"in_{name}": a for name, a in layout.items()}], core_ids=[0])
    return r.results[0]["out"]
```

```python
from contextlib import ExitStack, contextmanager

import concourse.bass as bass
import numpy as np
from concourse import mybir

ALU = mybir.AluOpType
ACT = mybir.ActivationFunctionType
AX_X = mybir.AxisListType.X
F32 = mybir.dt.float32
BF16 = mybir.dt.bfloat16
I32 = mybir.dt.int32

P = 128
N, E = 3125, 50000
DIM, H, D, RP, NREL = 256, 16, 8, 18, 16
DH = H * D
NT = -(-N // P)
NPAD = NT * P
LAST = N - (NT - 1) * P
EP, EC = 125, 400
G = 8
TWO = 2 * G
J = -(-((E + NT * (P - 1)) // P) // TWO) * TWO
EPAD = E + P
SCALE = D ** -0.5
BIG = 1e30
SKIP = float(1 << 17)

REC = 24
C_ONE, C_SRC, C_DST, C_TYPE, C_RANK = 18, 19, 20, 21, 22
ROW = DIM + DH + REC
KM = DH + REC
UW = DIM + H
LW = DIM + NREL
EPS_SOFTMAX, EPS_NORM = 1e-16, 1e-5


@contextmanager
def chunks(engine, count, body):
    with engine.Fori(0, count // body) as n:
        yield engine.snap(n * body)


@contextmanager
def when(engine, flag):
    if flag is None:
        yield
    else:
        with engine.If(engine.value_load(flag[0:1, 0:1], min_val=0, max_val=1)):
            yield


def makers(nc, ctx, stage):
    sems = []

    def give_back():
        nc.clear_and_free_semaphores(sems)
        nc.all_engine_barrier()

    def sem(name):
        sems.append(nc.alloc_semaphore(f"{stage}_{name}"))
        return sems[-1]

    ctx.callback(give_back)
    return (lambda name, shape, dt: ctx.enter_context(nc.sbuf_tensor(f"{stage}_{name}", shape, dt)),
            lambda name, shape, dt: ctx.enter_context(nc.psum_tensor(f"{stage}_{name}", shape, dt)), sem)


class Shared:
    pass


def constants(nc, s, sb):
    s.iota = sb("iota", [P, P], F32)
    s.iota_b = sb("iota_b", [P, P], BF16)
    s.pcol = sb("pcol", [P, 1], F32)
    s.before = sb("before", [P, P], F32)
    s.after = sb("after", [P, P], F32)
    s.ident = sb("ident", [P, P], F32)
    s.ident_b = sb("ident_b", [P, P], BF16)
    s.ones = sb("ones", [P, P], F32)
    s.negp = sb("negp", [P, 1], F32)
    s.eps = sb("eps", [P, 2], F32)


def stage_constants(nc, s, io):
    with ExitStack() as ctx:
        sb, pb, sem = makers(nc, ctx, "constants")
        attr = s.tab[0:EP, :, :, :].rearrange("p a b c -> p (a b c)")[:, 0:2 * EC * RP].bitcast(F32)
        ints = [sb(f"ints{k}", [EP, EC], I32) for k in range(3)]
        tmp = [sb(f"shifted{k}", [EP, EC], I32) for k in range(4)]
        keysT = [sb(f"keysT{k}", [100, E // 100], I32) for k in range(2)]
        hiTi = [sb(f"hiTi{k}", [100, E // 100], I32) for k in range(2)]
        hiTf = [sb(f"hiTf{k}", [100, E // 100], F32) for k in range(2)]
        iota_i = sb("iota_i", [P, P], I32)
        pcol_i = sb("pcol_i", [P, 1], I32)
        pad = sb("pad", [P, ROW], F32)
        following = sb("following", [EP, EC], I32)
        drop = sb("drop", [EP, EC], F32)
        most = sb("most", [EP, 1], F32)
        ps_most = pb("ps_most", [P, 512], F32)
        loads, loaded_attr, loadedT = sem("loads"), sem("loaded_attr"), sem("loadedT")
        iotas, filled, base_done, dve_done = sem("iotas"), sem("filled"), sem("base_done"), sem("dve_done")
        next_in, flag_step, most_turned = sem("next_in"), sem("flag_step"), sem("most_turned")
        pads, hi_out, attr_done = sem("pads"), sem("hi_out"), sem("attr_done")
        with nc.Block() as block:
            @block.sync
            def _(sp):
                for k, name in enumerate(("src", "dst", "type")):
                    sp.dma_start(ints[k][:, :], io[name]).then_inc(loads, 16)
                for k, name in enumerate(("srcT", "dstT")):
                    sp.dma_start(keysT[k][:, :], io[name].rearrange("(a b) c -> a (b c)", a=100)).then_inc(loadedT, 16)
                dst_flat = io["dst"].rearrange("p c -> (p c)")
                sp.wait_ge(flag_step, 1)
                sp.dma_start(following[0:EP - 1, :], dst_flat[1:1 + (EP - 1) * EC].rearrange("(p c) -> p c", c=EC)).then_inc(next_in, 16)
                sp.dma_start(following[EP - 1:EP, 0:EC - 1], io["dst"][EP - 1:EP, 1:EC]).then_inc(next_in, 16)
                sp.dma_start(attr, io["attr"]).then_inc(loaded_attr, 16)
                sp.wait_ge(base_done, 3)
                sp.dma_start(s.rows[E:EPAD, :], pad[:, :]).then_inc(pads, 16)
                sp.dma_start(s.recs[E:EPAD, :], pad[:, DIM + DH:ROW]).then_inc(pads, 16)
                sp.wait_ge(hi_out, 2)
                for k in range(2):
                    sp.dma_start(s.hiT[k].rearrange("(a b) -> a b", a=100), hiTf[k][:, :]).then_inc(pads, 16)
                sp.wait_ge(pads, 64)

            @block.gpsimd
            def _(pool):
                pool.iota(iota_i[:, :], pattern=[[1, P]], base=0, channel_multiplier=0).then_inc(iotas, 1)
                pool.iota(pcol_i[:, :], pattern=[[0, 1]], base=0, channel_multiplier=1).then_inc(iotas, 1)
                for t in (s.ident, s.before, s.after):
                    pool.memset(t[:, :], 0.0 if t is s.ident else 1.0).then_inc(filled, 1)
                pool.wait_ge(filled, 3)
                pool.affine_select(out=s.ident[:, :], in_=s.ident[:, :], compare_op=ALU.not_equal, fill=1.0,
                                   base=0, pattern=[[-1, P]], channel_multiplier=1).then_inc(filled, 1)
                pool.affine_select(out=s.before[:, :], in_=s.before[:, :], compare_op=ALU.is_gt, fill=0.0,
                                   base=0, pattern=[[-1, P]], channel_multiplier=1).then_inc(filled, 1)
                pool.affine_select(out=s.after[:, :], in_=s.after[:, :], compare_op=ALU.is_gt, fill=0.0,
                                   base=0, pattern=[[1, P]], channel_multiplier=-1).then_inc(filled, 1)
                pool.wait_ge(loaded_attr, 16)
                pool.tensor_copy(s.rec[:, :, 0:RP], attr.rearrange("p (c k) -> p c k", k=RP)).then_inc(attr_done, 1)

            @block.tensor
            def _(pe):
                pe.wait_ge(flag_step, 4)
                pe.transpose(ps_most[0:1, 0:EP], most[:, :], s.ident[0:EP, 0:EP]).then_inc(most_turned, 1)

            @block.vector
            def _(dve):
                dve.memset(following[:, EC - 1:EC], N).then_inc(flag_step, 1)
                dve.memset(pad[:, :], 0.0).then_inc(base_done, 1)
                dve.wait_ge(base_done, 1)
                dve.memset(pad[:, DIM + DH + C_SRC:DIM + DH + C_SRC + 1], -1.0).then_inc(base_done, 1)
                dve.memset(pad[:, DIM + DH + C_DST:DIM + DH + C_DST + 1], -1.0).then_inc(base_done, 1)
                dve.memset(s.ones[:, :], 1.0).then_inc(dve_done, 1)
                dve.memset(s.rec[:, :, C_ONE:C_ONE + 1], 1.0).then_inc(dve_done, 1)
                dve.memset(s.rec[:, :, REC - 1:REC], 0.0).then_inc(dve_done, 1)
                dve.memset(s.eps[:, 0:1], EPS_NORM).then_inc(dve_done, 1)
                dve.wait_ge(iotas, 2)
                dve.tensor_copy(s.iota[:, :], iota_i[:, :]).then_inc(dve_done, 1)
                dve.tensor_copy(s.iota_b[:, :], iota_i[:, :]).then_inc(dve_done, 1)
                dve.tensor_copy(s.pcol[:, :], pcol_i[:, :]).then_inc(dve_done, 1)
                dve.wait_ge(filled, 4)
                dve.tensor_copy(s.ident_b[:, :], s.ident[:, :]).then_inc(dve_done, 1)
                dve.wait_ge(loadedT, 32)
                for k in range(2):
                    dve.tensor_scalar(hiTi[k][:, :], keysT[k][:, :], 7, None, ALU.arith_shift_right).then_inc(dve_done, 1)
                dve.wait_ge(dve_done, 10)
                for k in range(2):
                    dve.tensor_copy(hiTf[k][:, :], hiTi[k][:, :]).then_inc(hi_out, 1)
                dve.wait_ge(loads, 48)
                for k in range(2):
                    dve.tensor_scalar(tmp[2 * k][:, :], ints[k][:, :], 7, None, ALU.arith_shift_right).then_inc(dve_done, 1)
                    dve.tensor_scalar(tmp[2 * k + 1][:, :], ints[k][:, :], 127, None, ALU.bitwise_and).then_inc(dve_done, 1)
                    dve.tensor_copy(s.key[k][:, :], ints[k][:, :]).then_inc(dve_done, 1)
                for k, c in enumerate((C_SRC, C_DST, C_TYPE)):
                    dve.tensor_copy(s.rec[:, :, c], ints[k][:, :]).then_inc(dve_done, 1)
                dve.wait_ge(next_in, 32)
                dve.tensor_copy(drop[:, :], following[:, :]).then_inc(flag_step, 1)
                dve.wait_ge(dve_done, 19)
                dve.wait_ge(flag_step, 2)
                dve.tensor_tensor(drop[:, :], s.key[1][:, :], drop[:, :], ALU.subtract).then_inc(flag_step, 1)
                dve.wait_ge(flag_step, 3)
                dve.tensor_reduce(most[:, :], drop[:, :], AX_X, ALU.max).then_inc(flag_step, 1)
                dve.wait_ge(most_turned, 1)
                dve.tensor_reduce(s.most_drop[:, :], ps_most[0:1, 0:EP], AX_X, ALU.max).then_inc(flag_step, 1)
                dve.wait_ge(flag_step, 5)
                dve.tensor_scalar(s.unsorted[:, :], s.most_drop[:, :], 0.0, None, ALU.is_gt).then_inc(flag_step, 1)
                dve.tensor_scalar(s.sorted[:, :], s.most_drop[:, :], 0.0, None, ALU.is_le).then_inc(flag_step, 1)
                for k in range(2):
                    dve.tensor_copy(s.hi[k][:, :], tmp[2 * k][:, :]).then_inc(dve_done, 1)
                    dve.tensor_copy(s.lo[k][:, :], tmp[2 * k + 1][:, :]).then_inc(dve_done, 1)


def stage_schedule(nc, s, k):
    with ExitStack() as ctx:
        sb, pb, sem = makers(nc, ctx, f"schedule{k}")
        psum = [pb(f"sums{a}", [P, 512], F32) for a in range(3)]
        incl = sb("incl", [NT, P], F32)
        small = sb("small", [NT, 8], F32)
        small_i = sb("small_i", [NT, 2], I32)
        wide = sb("wide", [NT, 3, P], F32)
        gone = sb("gone", [NT, J], F32)
        iotaj_i = sb("iotaj_i", [P, J], I32)
        iotaj = sb("iotaj", [P, J], F32)
        fl = sb("fl", [P, 2, J], F32)
        step = sem("step")
        iota_made = sem("iota_made")
        sums = sem("sums")
        count = s.count[k]
        pre, pt, pst = psum[0][0:NT, 0:2], psum[1][:, 0:J], psum[2][:, 0:J]
        n_t, nch, t0, c0, cend = (small[:, a:a + 1] for a in range(5))
        with nc.Block() as block:
            @block.gpsimd
            def _(pool):
                pool.iota(iotaj_i[:, :], pattern=[[1, J]], base=0, channel_multiplier=0).then_inc(iota_made, 1)

            @block.tensor
            def _(pe):
                pe.wait_ge(step, 6)
                pe.matmul(pre, s.after[0:NT, 0:NT], small[:, 0:2], start=True, stop=True).then_inc(sums, 1)
                pe.wait_ge(step, 15)
                pe.matmul(pt, wide[:, 0, :], gone[:, :], start=True, stop=True).then_inc(sums, 1)
                pe.matmul(pst, wide[:, 1, :], gone[:, :], start=True, stop=True).then_inc(sums, 1)

            @block.vector
            def _(dve):
                n = [0]

                def link(ins):
                    n[0] += 1
                    ins.then_inc(step, 1)
                    dve.wait_ge(step, n[0])

                link(dve.tensor_reduce(n_t, count[:, :], AX_X, ALU.add))
                link(dve.tensor_scalar(small[:, 5:6], n_t, float(P - 1), None, ALU.add))
                link(dve.tensor_copy(small_i[:, 0:1], small[:, 5:6]))
                link(dve.tensor_scalar(small_i[:, 1:2], small_i[:, 0:1], 7, None, ALU.arith_shift_right))
                link(dve.tensor_copy(nch, small_i[:, 1:2]))
                link(dve.tensor_tensor_scan(incl[:, :], s.ones[0:NT, :], count[:, :], 0.0, ALU.mult, ALU.add))
                dve.wait_ge(sums, 1)
                link(dve.tensor_copy(small[:, 2:4], pre))
                link(dve.tensor_tensor(incl[:, :], incl[:, :], count[:, :], ALU.subtract))
                link(dve.tensor_scalar(s.start[k][:, :], incl[:, :], t0, None, ALU.add))
                link(dve.tensor_tensor(cend, c0, nch, ALU.add))
                dve.wait_ge(iota_made, 1)
                link(dve.tensor_copy(iotaj[:, :], iotaj_i[:, :]))
                link(dve.tensor_scalar(gone[:, :], iotaj[0:NT, :], cend, None, ALU.is_ge))
                link(dve.tensor_scalar(small[:, 6:7], nch, -float(P), n_t, ALU.mult, ALU.add))
                link(dve.memset(wide[:, 0, :], 1.0))
                link(dve.tensor_scalar(wide[:, 1, :], s.ones[0:NT, :], small[:, 6:7], None, ALU.mult))
                dve.wait_ge(sums, 3)
                link(dve.tensor_scalar(s.base[k][:, :], pt, float(P), None, ALU.mult))
                link(dve.tensor_scalar(fl[:, 0, :], pt, float(NT - 1), None, ALU.min))
                link(dve.tensor_copy(s.tile_of[k][:, :], fl[0:1, 0, :]))
                link(dve.tensor_scalar(fl[:, 1, :], iotaj[:, :], float(P), None, ALU.mult))
                link(dve.tensor_tensor(fl[:, 1, :], fl[:, 1, :], pst, ALU.add))
                link(dve.tensor_scalar(fl[:, 1, :], fl[:, 1, :], float(E), None, ALU.min))
                link(dve.tensor_copy(s.start_of[k][:, :], fl[0:1, 1, :]))


def stage_count_project(nc, s, io):
    K = EC // NT
    with ExitStack() as ctx:
        sb, pb, sem = makers(nc, ctx, "count")
        hist = [pb(f"hist{k}", [P, 512], F32) for k in range(2)]
        ps = pb("proj", [P, 512], F32)
        Lr = [sb(f"Lr{k}", [EP, K, P], BF16) for k in range(2)]
        Hr = [sb(f"Hr{k}", [EP, K, NT], BF16) for k in range(2)]
        zero = sb("zero", [EP, P], BF16)
        xT = s.scores_or_h[:, 0:2 * NPAD].rearrange("p (a n) -> p a n", a=2)
        W = sb("Wqkv", [P, 2, 512], F32)
        b = sb("bqkv", [1, 512], F32)
        xt = sb("x_tile", [P, 2, P], F32)
        full = sb("full", [P, 512], F32)
        rest = sb("rest", [P, 512], F32)
        counted = [sem(f"counted{k}") for k in range(2)]
        lo_made = [sem(f"lo_made{k}") for k in range(2)]
        hi_made = [sem(f"hi_made{k}") for k in range(2)]
        zeroed, ended, kept, loads = sem("zeroed"), sem("ended"), sem("kept"), sem("loads")
        made, scaled, copied, x_cut = sem("made"), sem("scaled"), sem("copied"), sem("x_cut")
        top, mid, sub1, sub2 = sem("top"), sem("mid"), sem("sub1"), sem("sub2")
        with nc.Block() as block:
            @block.sync
            def _(sp):
                for a in range(2):
                    sp.dma_start(xT[:, a, 0:N], io["xT"][a * P:(a + 1) * P, :]).then_inc(loads, 16)
                    w = io["Wqkv"][a * P:(a + 1) * P, :]
                    sp.dma_start(W[:, a, 0:DIM], w[:, 2 * DH:]).then_inc(loads, 16)
                    sp.dma_start(W[:, a, DIM:DIM + DH], w[:, DH:2 * DH]).then_inc(loads, 16)
                    sp.dma_start(W[:, a, DIM + DH:], w[:, 0:DH]).then_inc(loads, 16)
                sp.dma_start(b[:, 0:DIM], io["bqkv"][:, 2 * DH:]).then_inc(loads, 16)
                sp.dma_start(b[:, DIM:DIM + DH], io["bqkv"][:, DH:2 * DH]).then_inc(loads, 16)
                sp.dma_start(b[:, DIM + DH:], io["bqkv"][:, 0:DH]).then_inc(loads, 16)

            @block.vector
            def _(dve):
                dve.memset(zero[:, :], 0.0).then_inc(zeroed, 1)
                dve.memset(xT[:, :, N:NPAD], 0.0).then_inc(zeroed, 1)
                dve.sem_inc(made, 1)
                dve.wait_ge(loads, 16 * 11)
                dve.wait_ge(zeroed, 2)
                with dve.Fori(0, NT) as t:
                    i = dve.snap(t * K)
                    dve.wait_ge(made, t + 1)
                    dve.tensor_copy(xt[:, :, :], xT[:, :, bass.ds(t * P, P)]).then_inc(x_cut, 1)
                    for k in range(2):
                        dve.wait_ge(counted[k], i + K)
                        dve.tensor_tensor(Hr[k][:, :, :], s.iota[0:EP, None, 0:NT].to_broadcast([EP, K, NT]),
                                          s.hi[k][:, bass.ds(i, K), None].to_broadcast([EP, K, NT]),
                                          ALU.is_equal).then_inc(hi_made[k], K)
                        for q in range(K):
                            dve.tensor_scalar(Lr[k][:, q, :], s.iota_b[0:EP, :], s.lo[k][:, bass.ds(i + q, 1)], None,
                                              ALU.is_equal).then_inc(lo_made[k], 1)
                dve.wait_ge(ended, 1)
                for k in range(2):
                    dve.tensor_copy(s.count[k][:, :], hist[k][0:NT, 0:P]).then_inc(kept, 1)

            @block.tensor
            def _(pe):
                pe.wait_ge(zeroed, 2)
                for k in range(2):
                    pe.matmul(hist[k][0:NT, 0:P], zero[:, 0:NT], zero[:, :], start=True, stop=False, skip_group_check=True)
                    pe.sem_inc(counted[k], K)
                pe.wait_ge(loads, 16 * 11)
                with pe.Fori(0, NT) as t:
                    pe.wait_ge(copied, t + 1)
                    pe.wait_ge(scaled, t + 1)
                    pe.wait_ge(x_cut, t + 1)
                    for a in range(2):
                        pe.matmul(ps[:, :], xt[:, a, :], W[:, a, :], start=(a == 0), stop=False,
                                  skip_group_check=True)
                    pe.matmul(ps[:, :], s.ones[0:1, :], b[:, :], start=False, stop=True,
                              skip_group_check=True).then_inc(made, 1)
                    i = pe.snap(t * K)
                    for k in range(2):
                        pe.wait_ge(hi_made[k], i + K)
                        for q in range(K):
                            pe.wait_ge(lo_made[k], i + q + 1)
                            pe.matmul(hist[k][0:NT, 0:P], Hr[k][:, q, :], Lr[k][:, q, :], start=False, stop=False,
                                      skip_group_check=True).then_inc(counted[k], 1)
                pe.matmul(hist[1][0:NT, 0:P], zero[:, 0:NT], zero[:, :], start=False, stop=True,
                          skip_group_check=True).then_inc(ended, 1)

            @block.scalar
            def _(act):
                act.sem_inc(copied, 1)
                act.sem_inc(scaled, 1)
                with act.Fori(0, NT) as t:
                    act.wait_ge(made, t + 2)
                    act.wait_ge(sub1, t + 1)
                    act.activation(full[:, 0:384], ps[:, 0:384], ACT.Copy).then_inc(copied, 1)
                    act.activation(full[:, 384:512], ps[:, 384:512], ACT.Copy, scale=SCALE).then_inc(scaled, 1)
                    act.wait_ge(copied, t + 2)
                    act.wait_ge(scaled, t + 2)
                    act.activation(s.tab[:, bass.ds(t, 1), 0, :], full[:, None, :], ACT.Copy).then_inc(top, 1)
                    act.wait_ge(sub1, t + 2)
                    act.activation(s.tab[:, bass.ds(t, 1), 1, :], rest[:, None, :], ACT.Copy).then_inc(mid, 1)

            @block.gpsimd
            def _(pool):
                pool.sem_inc(sub1, 1)
                pool.sem_inc(sub2, 1)
                with pool.Fori(0, NT) as t:
                    pool.wait_ge(top, t + 1)
                    pool.wait_ge(sub2, t + 1)
                    pool.tensor_tensor(rest[:, None, :], full[:, None, :], s.tab[:, bass.ds(t, 1), 0, :], ALU.subtract).then_inc(sub1, 1)
                    pool.wait_ge(mid, t + 1)
                    pool.tensor_tensor(s.tab[:, bass.ds(t, 1), 2, :], rest[:, None, :], s.tab[:, bass.ds(t, 1), 1, :],
                                       ALU.subtract).then_inc(sub2, 1)


def stage_rank(nc, s, io, k, flag=None):
    keyT = io[("srcT", "dstT")[k]]
    with ExitStack() as ctx:
        sb, pb, sem = makers(nc, ctx, f"rank{k}")
        hist = pb("hist", [P, 512], F32)
        look = [pb(f"look{a}", [P, 512], F32) for a in range(4)]
        Lr = sb("Lr", [EP, TWO, P], BF16)
        Hr = sb("Hr", [EP, 2, G, NT], BF16)
        same = sb("same", [EP, G, EP], BF16)
        cut = lambda a, p: s.scores_or_h[0:p, a * TWO * EP:(a + 1) * TWO * EP]
        keyb = cut(0, P).bitcast(I32).rearrange("p (a g e) -> p a g e", a=2, g=G)
        hib = cut(1, 32).rearrange("p (a g e) -> p a g e", a=2, g=G)
        off = sb("off", [NT, G, EP], F32)
        HT = sb("HT", [NT, 2, G, EP], F32)
        snap = sb("snap", [NT, G, P], F32)
        junk = sb("junk", [EP, 2, P], F32)
        key_in = [sem(f"key_in{a}") for a in range(2)]
        hi_in = [sem(f"hi_in{a}") for a in range(2)]
        lo_made, hi_made, counted, primed = sem("lo_made"), sem("hi_made"), sem("counted"), sem("primed")
        off_made, hT_made, snapped, looked, ranked = sem("off_made"), sem("hT_made"), sem("snapped"), sem("looked"), sem("ranked")
        compared, negated = sem("compared"), sem("negated")
        with nc.Block() as block:
            @block.sync
            def _(sp):
                with when(sp, flag):
                    with chunks(sp, EC, TWO) as i:
                        for half in range(2):
                            g = i + half * G
                            sp.wait_ge(compared, g + G)
                            sp.dma_start(keyb[:, half, :, :], keyT[None, bass.ds(g, G), :].to_broadcast([P, G, EP])).then_inc(key_in[half], 16)
                            sp.wait_ge(hT_made, g + G)
                            sp.dma_start(hib[:, half, :, :], s.hiT2[k][None, bass.ds(g, G), :].to_broadcast([32, G, EP])).then_inc(hi_in[half], 16)

            @block.scalar
            def _(act):
                with when(act, flag):
                    act.sem_inc(hT_made, TWO)
                    act.wait_ge(primed, 1)
                    act.wait_ge(negated, 1)
                    with chunks(act, EC, TWO) as i:
                        for half in range(2):
                            g = i + half * G
                            act.wait_ge(hi_in[half], i + 16)
                            act.wait_ge(hT_made, g + TWO)
                            act.activation(off[:, :, :], hib[0:NT, half, :, :], ACT.Square, bias=s.negp[0:NT, :]).then_inc(off_made, G)
                            act.wait_ge(off_made, g + G)
                            act.wait_ge(looked, g + G)
                            act.activation(HT[:, half, :, :], off[:, :, :], ACT.Relu, bias=s.ones[0:NT, 0:1], scale=-1.0).then_inc(hT_made, G)
                            for q in range(G):
                                act.wait_ge(counted, g + q + TWO)
                                act.wait_ge(looked, g + q + 1 + G)
                                act.activation(snap[:, q, :], hist[0:NT, 0:P], ACT.Copy).then_inc(snapped, 1)

            @block.tensor
            def _(pe):
                with when(pe, flag):
                    pe.matmul(hist[0:NT, 0:P], s.ident[0:NT, 0:NT], s.start[k][:, :], start=True, stop=False,
                              skip_group_check=True).then_inc(primed, 1)
                    pe.sem_inc(looked, TWO)
                    with chunks(pe, EC, TWO) as i:
                        for half in range(2):
                            g = i + half * G
                            for q in range(G):
                                pe.wait_ge(snapped, g + q + 1)
                                if q == 0:
                                    pe.wait_ge(hi_made, g + G)
                                    pe.wait_ge(hT_made, g + G + TWO)
                                pe.wait_ge(lo_made, g + q + 1)
                                pe.matmul(hist[0:NT, 0:P], Hr[:, half, q, :], Lr[:, half * G + q, :], start=False, stop=False,
                                          skip_group_check=True).then_inc(counted, 1)
                                pe.wait_ge(ranked, g + q + 1)
                                pe.matmul(look[q % 4][0:EP, 0:P], HT[:, half, q, :], snap[:, q, :], start=True,
                                          stop=False, skip_group_check=True)
                                pe.wait_ge(compared, g + q + 1 + TWO)
                                pe.matmul(look[q % 4][0:EP, 0:P], same[:, q, :], Lr[:, half * G + q, :], start=False,
                                          stop=True, skip_group_check=True).then_inc(looked, 1)

            @block.vector
            def _(dve):
                with when(dve, flag):
                    dve.tensor_scalar(s.negp[:, :], s.pcol[:, :], -1.0, None, ALU.mult).then_inc(negated, 1)
                    dve.sem_inc(counted, TWO)
                    dve.sem_inc(compared, TWO)
                    dve.sem_inc(ranked, 4)
                    with chunks(dve, EC, TWO) as i:
                        for half in range(2):
                            g = i + half * G
                            dve.wait_ge(looked, g + G)
                            dve.tensor_tensor(Hr[:, half, :, :], s.iota[0:EP, None, 0:NT].to_broadcast([EP, G, NT]),
                                              s.hi[k][:, bass.ds(g, G), None].to_broadcast([EP, G, NT]),
                                              ALU.is_equal).then_inc(hi_made, G)
                            dve.wait_ge(key_in[half], i + 16)

                            def prepare(q):
                                dve.tensor_scalar(Lr[:, half * G + q, :], s.iota_b[0:EP, :], s.lo[k][:, bass.ds(g + q, 1)], None,
                                                  ALU.is_equal).then_inc(lo_made, 1)
                                dve.wait_ge(looked, g + q + 1 + G)
                                dve.scalar_tensor_tensor(out=same[:, q, :], in0=keyb[0:EP, half, q, :],
                                                         scalar=s.key[k][:, bass.ds(g + q, 1)], in1=s.after[0:EP, 0:EP],
                                                         op0=ALU.is_equal, op1=ALU.mult).then_inc(compared, 1)

                            for q in range(4):
                                prepare(q)
                            for q in range(G):
                                if q + 4 < G:
                                    prepare(q + 4)
                                dve.wait_ge(looked, g + q + 1 + TWO)
                                dve.wait_ge(ranked, g + q + 3)
                                dve.scalar_tensor_tensor(out=junk[:, q % 2, :], in0=s.iota[0:EP, :],
                                                         scalar=s.lo[k][:, bass.ds(g + q, 1)],
                                                         in1=look[q % 4][0:EP, 0:P],
                                                         op0=ALU.is_equal, op1=ALU.mult,
                                                         accum_out=s.place[:, bass.ds(g + q, 1)]).then_inc(ranked, 1)
                    if k == 0:
                        dve.wait_ge(ranked, EC + 4)
                        dve.tensor_copy(s.rec[:, :, C_RANK], s.place[:, :]).then_inc(ranked, 1)


def stage_sort_records(nc, s, flag):
    with ExitStack() as ctx:
        sb, pb, sem = makers(nc, ctx, "sort_records")
        out = [sb(f"rec_out{q}", [EP, REC], F32) for q in range(G)]
        at = sb("rec_at", [EP, G], I32)
        copied, idx_copied = sem("copied"), sem("idx_copied")
        scattered = [sem(f"rec_scattered{q}") for q in range(G)]
        with nc.Block() as block:
            @block.vector
            def _(dve):
                with when(dve, flag):
                    with chunks(dve, EC, G) as i:
                        for q in range(G):
                            dve.wait_ge(scattered[q], i * 2 + 16)
                            dve.tensor_copy(out[q][:, :], s.rec[:, bass.ds(i + q, 1), :]).then_inc(copied, 1)
                            dve.tensor_copy(at[:, q:q + 1], s.place[:, bass.ds(i + q, 1)]).then_inc(idx_copied, 1)

            @block.gpsimd
            def _(pool):
                with when(pool, flag):
                    for q in range(G):
                        pool.dma_start(out[q][:, :], s.recs[E:E + EP, :]).then_inc(scattered[q], 16)
                    with chunks(pool, EC, G) as i:
                        for q in range(G):
                            pool.wait_ge(copied, i + q + 1)
                            pool.wait_ge(idx_copied, i + q + 1)
                            pool.sem_inc(s.pool_passed, 1)
                            pool.indirect_dma_start(
                                out=s.recs, out_offset=bass.IndirectOffsetOnAxis(ap=at[:, q:q + 1], axis=0),
                                in_=out[q][:, :], in_offset=None).then_inc(scattered[q], 16)
                    for q in range(G):
                        pool.wait_ge(scattered[q], 16 * (EC // G) + 16)


def stage_store_records(nc, s, flag):
    with ExitStack() as ctx:
        sb, pb, sem = makers(nc, ctx, "store_records")
        stored = sem("stored")
        with nc.Block() as block:
            @block.sync
            def _(sp):
                with when(sp, flag):
                    sp.dma_start(s.recs[0:E, :].rearrange("(p c) k -> p (c k)", p=EP),
                                 s.rec[:, :, :].rearrange("p c k -> p (c k)")).then_inc(stored, 16)
                    sp.wait_ge(stored, 16)


def stage_rows(nc, s):
    with ExitStack() as ctx:
        sb, pb, sem = makers(nc, ctx, "rows")
        psT = [pb(f"psT{a}", [P, 2 * 512], BF16) for a in range(2)]
        psV = [pb(f"psV{a}", [P, 512], F32) for a in range(4)]
        rec = sb("rec_in", [P, 2, G, REC], F32)
        row = [sb(f"row{q}", [P, ROW], F32) for q in range(G)]
        idx = sb("idx", [P, 2, G], I32)
        low = sb("low", [P, 2, G], F32)
        valid = sb("valid", [P, 2, G], F32)
        idxf = sb("idxf", [P, 2, G], F32)
        oh = sb("oh", [P, G, P], BF16)
        ohT = sb("ohT", [P, G, P], BF16)
        rec_in = [sem(f"rec_in{a}") for a in range(2)]
        rec_free, rel_made, low_made = sem("rec_free"), sem("rel_made"), sem("low_made")
        valid_made, idxf_made, idx_made, src_kept = sem("valid_made"), sem("idxf_made"), sem("idx_made"), sem("src_kept")
        type_kept = sem("type_kept")
        oh_made, turned, ohT_made, fetched, evicted = sem("oh_made"), sem("turned"), sem("ohT_made"), sem("fetched"), sem("evicted")
        scattered = [sem(f"row_scattered{q}") for q in range(G)]
        with nc.Block() as block:
            @block.sync
            def _(sp):
                first = [sp.alloc_register(f"rows_first{q}") for q in range(G)]
                with chunks(sp, J, TWO) as i:
                    for half in range(2):
                        g = i + half * G
                        sp.load(first, s.start_of[1][0:1, bass.ds(g, G)])
                        sp.wait_ge(rec_free, g + G)
                        for q in range(G):
                            at = sp.snap(first[q], min_val=0, max_val=E)
                            sp.dma_start(rec[:, half, q, :], s.recs[bass.ds(at, P), :]).then_inc(rec_in[half], 16)

            @block.vector
            def _(dve):
                dve.sem_inc(rec_free, TWO)
                with chunks(dve, J, TWO) as i:
                    for half in range(2):
                        g = i + half * G
                        dve.wait_ge(rec_in[half], i * G + 16 * G)
                        dve.tensor_tensor(s.relD[:, bass.ds(g, G)], rec[:, half, :, C_DST], s.base[1][:, bass.ds(g, G)],
                                          ALU.subtract).then_inc(rel_made, G)
                        dve.tensor_scalar(s.src_of[:, bass.ds(g, G)], rec[:, half, :, C_SRC], 0.0, None,
                                          ALU.max).then_inc(src_kept, 1)
                        dve.tensor_copy(s.type_of[:, bass.ds(g, G)], rec[:, half, :, C_TYPE]).then_inc(type_kept, 1)
                        dve.wait_ge(rel_made, g + G)
                        dve.tensor_scalar(low[:, half, :], s.relD[:, bass.ds(g, G)], 0.0, None, ALU.is_ge).then_inc(low_made, G)
                        dve.wait_ge(low_made, g + G)
                        dve.scalar_tensor_tensor(out=valid[:, half, :], in0=s.relD[:, bass.ds(g, G)], scalar=P - 1.0,
                                                 in1=low[:, half, :], op0=ALU.is_le, op1=ALU.mult).then_inc(valid_made, G)
                        dve.wait_ge(valid_made, g + G)
                        dve.scalar_tensor_tensor(out=idxf[:, half, :], in0=rec[:, half, :, C_RANK], scalar=-SKIP,
                                                 in1=valid[:, half, :], op0=ALU.add, op1=ALU.mult).then_inc(idxf_made, G)
                        dve.wait_ge(idxf_made, g + G)
                        dve.tensor_scalar(idx[:, half, :], idxf[:, half, :], SKIP, None, ALU.add).then_inc(idx_made, G)
                        for q in range(G):
                            dve.wait_ge(turned, g + q + 1)
                            dve.tensor_scalar(oh[:, q, :], s.iota_b[:, :], s.relD[:, bass.ds(g + q, 1)], None,
                                              ALU.is_equal).then_inc(oh_made, 1)
                            dve.wait_ge(scattered[q], i * 2 + 16 * half + 16)
                            dve.tensor_copy(row[q][:, DIM + DH:ROW], rec[:, half, q, :]).then_inc(rec_free, 1)

            @block.tensor
            def _(pe):
                tile = [pe.alloc_register(f"rows_tile{q}") for q in range(G)]
                pe.sem_inc(turned, G)
                with chunks(pe, J, TWO) as i:
                    for half in range(2):
                        g = i + half * G
                        pe.load(tile, s.tile_of[1][0:1, bass.ds(g, G)])

                        def turn(q):
                            pe.wait_ge(oh_made, g + q + 1)
                            pe.wait_ge(ohT_made, g + q + G - 1)
                            pe.transpose(psT[q % 2][:, 0:P], oh[:, q, :], s.ident_b[:, :]).then_inc(turned, 1)

                        turn(0)
                        for q in range(G):
                            if q + 1 < G:
                                turn(q + 1)
                            pe.wait_ge(ohT_made, g + q + 1 + G)
                            pe.wait_ge(evicted, g + q + 1)
                            t = pe.snap(tile[q], min_val=0, max_val=NT - 1)
                            for a in range(3):
                                last = pe.matmul(psV[q % 4][:, 0:DIM + DH], ohT[:, q, :],
                                                 s.tab[:, bass.ds(t, 1), a, 0:DIM + DH], start=(a == 0), stop=(a == 2))
                            last.then_inc(fetched, 1)

            @block.scalar
            def _(act):
                act.sem_inc(ohT_made, G)
                act.sem_inc(evicted, 4)
                with chunks(act, J, TWO) as i:
                    for half in range(2):
                        g = i + half * G

                        def turned_copy(q):
                            act.wait_ge(turned, g + q + 1 + G)
                            act.activation(ohT[:, q, :], psT[q % 2][:, 0:P], ACT.Copy).then_inc(ohT_made, 1)

                        turned_copy(0)
                        for q in range(G):
                            if q + 1 < G:
                                turned_copy(q + 1)
                            act.wait_ge(fetched, g + q + 1)
                            act.wait_ge(scattered[q], i * 2 + 16 * half + 16)
                            act.activation(row[q][:, 0:DIM + DH], psV[q % 4][:, 0:DIM + DH], ACT.Copy).then_inc(evicted, 1)

            @block.gpsimd
            def _(pool):
                for q in range(G):
                    pool.dma_start(row[q][:, :], s.rows[E:EPAD, :]).then_inc(scattered[q], 16)
                with chunks(pool, J, TWO) as i:
                    for half in range(2):
                        g = i + half * G
                        pool.wait_ge(idx_made, g + G)
                        pool.sem_inc(s.pool_passed, 1)
                        for q in range(G):
                            pool.wait_ge(evicted, g + q + 1 + 4)
                            pool.wait_ge(rec_free, g + q + 1 + TWO)
                            pool.sem_inc(s.pool_passed, 1)
                            pool.indirect_dma_start(
                                out=s.rows, out_offset=bass.IndirectOffsetOnAxis(ap=idx[:, half, q:q + 1], axis=0),
                                in_=row[q][:, :], in_offset=None, bounds_check=E - 1,
                                oob_is_err=False).then_inc(scattered[q], 16)
                for q in range(G):
                    pool.wait_ge(scattered[q], 16 * (J // G) + 16)


def stage_scores(nc, s, io):
    with ExitStack() as ctx:
        sb, pb, sem = makers(nc, ctx, "scores")
        psT = [pb(f"psT{a}", [P, 2 * 512], BF16) for a in range(2)]
        psA = [pb(f"psA{a}", [P, 512], F32) for a in range(2)]
        psQ = [pb(f"psQ{a}", [P, 512], F32) for a in range(4)]
        km = sb("km", [P, 2, G, KM], F32)
        Wr = sb("Wr", [RP + 1, 2 * DH], F32)
        low = sb("low", [P, 2, G], F32)
        oh = sb("oh", [P, G, P], BF16)
        ohT = sb("ohT", [P, G, P], BF16)
        aT = sb("aT", [RP + 1, G, P], F32)
        ke = sb("ke", [P, G, DH], F32)
        prod = sb("prod", [P, 2, G, DH], F32)
        km_in = [sem(f"km_in{a}") for a in range(2)]
        w_in, kept, rel_made, low_made = sem("w_in"), sem("kept"), sem("rel_made"), sem("low_made")
        oh_made, turned, ohT_made = sem("oh_made"), sem("turned"), sem("ohT_made")
        a_turned, aT_made, fetched, keyed = sem("a_turned"), sem("aT_made"), sem("fetched"), sem("keyed")
        valid_made, multiplied, summed = sem("valid_made"), sem("multiplied"), sem("summed")
        with nc.Block() as block:
            @block.sync
            def _(sp):
                sp.dma_start(Wr[0:RP, 0:DH], io["Wq_rpe"]).then_inc(w_in, 16)
                sp.dma_start(Wr[0:RP, DH:], io["Wk_rpe"]).then_inc(w_in, 16)
                sp.dma_start(Wr[RP:RP + 1, 0:DH], io["bq_rpe"]).then_inc(w_in, 16)
                sp.dma_start(Wr[RP:RP + 1, DH:], io["bk_rpe"]).then_inc(w_in, 16)
                first = [sp.alloc_register(f"score_first{q}") for q in range(G)]
                with chunks(sp, J, TWO) as i:
                    for half in range(2):
                        g = i + half * G
                        sp.load(first, s.start_of[0][0:1, bass.ds(g, G)])
                        sp.wait_ge(keyed, g + G)
                        for q in range(G):
                            at = sp.snap(first[q], min_val=0, max_val=E)
                            sp.dma_start(km[:, half, q, :], s.rows[bass.ds(at, P), DIM:ROW]).then_inc(km_in[half], 16)

            @block.vector
            def _(dve):
                dve.sem_inc(keyed, TWO)
                with chunks(dve, J, TWO) as i:
                    for half in range(2):
                        g = i + half * G
                        dve.wait_ge(km_in[half], i * G + 16 * G)
                        dve.tensor_copy(s.src_key[:, bass.ds(g, G)], km[:, half, :, DH + C_SRC]).then_inc(kept, 1)
                        dve.tensor_tensor(s.relS[:, bass.ds(g, G)], km[:, half, :, DH + C_SRC],
                                          s.base[0][:, bass.ds(g, G)], ALU.subtract).then_inc(rel_made, G)
                        dve.wait_ge(rel_made, g + G)
                        dve.tensor_scalar(low[:, half, :], s.relS[:, bass.ds(g, G)], 0.0, None, ALU.is_ge).then_inc(low_made, G)
                        dve.wait_ge(low_made, g + G)
                        dve.scalar_tensor_tensor(out=s.validS[:, bass.ds(g, G)], in0=s.relS[:, bass.ds(g, G)],
                                                 scalar=P - 1.0, in1=low[:, half, :],
                                                 op0=ALU.is_le, op1=ALU.mult).then_inc(valid_made, G)

                        def onehot(q):
                            dve.wait_ge(turned, g + q + 1)
                            dve.tensor_scalar(oh[:, q, :], s.iota_b[:, :], s.relS[:, bass.ds(g + q, 1)], None,
                                              ALU.is_equal).then_inc(oh_made, 1)

                        for q in range(3):
                            onehot(q)
                        for q in range(G):
                            if q + 3 < G:
                                onehot(q + 3)
                            dve.wait_ge(fetched, g + q + 2)
                            dve.tensor_tensor(ke[:, q, :], psQ[q % 4][:, DH:2 * DH], km[:, half, q, 0:DH],
                                              ALU.add).then_inc(keyed, 1)
                            dve.wait_ge(keyed, g + q + 1 + TWO)
                            dve.tensor_tensor(prod[:, half, q, :], psQ[q % 4][:, 0:DH], ke[:, q, :],
                                              ALU.mult).then_inc(multiplied, 1)
                        dve.wait_ge(multiplied, g + G + 4)
                        dve.tensor_reduce(s.score[:, bass.ds(g, G), :],
                                          prod[:, half, :, :].rearrange("p g (h d) -> p g h d", d=D),
                                          AX_X, ALU.add).then_inc(summed, 1)

            @block.tensor
            def _(pe):
                tile = [pe.alloc_register(f"score_tile{q}") for q in range(G)]
                pe.sem_inc(turned, G)
                pe.sem_inc(fetched, 1)
                pe.wait_ge(w_in, 64)
                with chunks(pe, J, TWO) as i:
                    for half in range(2):
                        g = i + half * G
                        pe.load(tile, s.tile_of[0][0:1, bass.ds(g, G)])
                        pe.wait_ge(km_in[half], i * G + 16 * G)

                        def turn(q):
                            pe.wait_ge(aT_made, g + q + G - 1)
                            pe.transpose(psA[q % 2][0:RP + 1, 0:P], km[:, half, q, DH:DH + RP + 1],
                                         s.ident[:, :]).then_inc(a_turned, 1)
                            pe.wait_ge(oh_made, g + q + 1)
                            pe.wait_ge(ohT_made, g + q + G - 1)
                            pe.transpose(psT[q % 2][:, 0:P], oh[:, q, :], s.ident_b[:, :]).then_inc(turned, 1)

                        turn(0)
                        for q in range(G):
                            if q + 1 < G:
                                turn(q + 1)
                            pe.wait_ge(aT_made, g + q + 1 + G)
                            pe.wait_ge(multiplied, g + q + 1)
                            pe.matmul(psQ[q % 4][:, 0:2 * DH], aT[:, q, :], Wr[:, :], start=True, stop=False,
                                      skip_group_check=True)
                            pe.wait_ge(ohT_made, g + q + 1 + G)
                            t = pe.snap(tile[q], min_val=0, max_val=NT - 1)
                            for a in range(3):
                                last = pe.matmul(psQ[q % 4][:, 0:DH], ohT[:, q, :],
                                                 s.tab[:, bass.ds(t, 1), a, DIM + DH:], start=False, stop=(a == 2),
                                                 skip_group_check=True)
                            last.then_inc(fetched, 1)

            @block.scalar
            def _(act):
                act.sem_inc(ohT_made, G)
                act.sem_inc(aT_made, G)
                act.sem_inc(multiplied, 4)
                with chunks(act, J, TWO) as i:
                    for half in range(2):
                        g = i + half * G
                        for q in range(G):
                            act.wait_ge(a_turned, g + q + 1)
                            if q == 0:
                                act.wait_ge(fetched, g + 1)
                            act.activation(aT[:, q, :], psA[q % 2][0:RP + 1, 0:P], ACT.Copy).then_inc(aT_made, 1)
                            act.wait_ge(turned, g + q + 1 + G)
                            act.activation(ohT[:, q, :], psT[q % 2][:, 0:P], ACT.Copy).then_inc(ohT_made, 1)


NG = J // G


def stage_softmax(nc, s):
    L = NG * P
    with ExitStack() as ctx:
        sb, pb, sem = makers(nc, ctx, "softmax")
        ps = [pb(f"sm_ps{a}", [P, 512], F32) for a in range(6)]
        sc = sb("sc", [P, L], F32)
        mx = sb("mx", [P, L], F32)
        pen = sb("pen", [P, L + 1], F32)
        key = sb("keyrow", [P, L + 1], F32)
        group_row = sb("group_row", [P, 2, P], F32)
        blk = sb("blk", [P, G], F32)
        head = sb("head", [P, H], F32)
        headT = sb("headT", [H, P], F32)
        less = sb("less", [P, J], F32)
        by_row = sb("by_row", [P, NG, G, H], F32)
        pi = sb("pi", [P, 2], I32)
        pf = sb("pf", [P, 2], F32)
        edge = sb("edge", [P, 3], F32)
        wide = sb("wide", [P, 3 * G], F32)
        small = sb("small", [H, 3 * G], F32)
        carry = sb("carry", [H, G + 1], F32)
        back = sb("back", [P, G], F32)
        carried = sb("carried", [P, 2], F32)
        step, handed, pe_step, masked, key_rows = sem("step"), sem("handed"), sem("pe_step"), sem("masked"), sem("key_rows")
        sc_turned, sc_evicted, exps, ex_turned, ex_evicted = sem("sc_turned"), sem("sc_evicted"), sem("exps"), sem("ex_turned"), sem("ex_evicted")
        key_turned, key_evicted = sem("key_turned"), sem("key_evicted")
        score_v = s.score[:, :, :].rearrange("p (b g) h -> p b g h", g=NG)
        less_v = less[:, :].rearrange("p (b g) -> p b g", g=NG)
        key_v = s.src_key[:, :].rearrange("p (b g) -> p b g", g=NG)
        with nc.Block() as block:
            @block.vector
            def _(dve):
                n = [0, 0]

                def link(ins):
                    n[0] += 1
                    ins.then_inc(step, 1)
                    dve.wait_ge(step, n[0])

                def hand(ins):
                    n[1] += 1
                    ins.then_inc(handed, 1)
                    dve.wait_ge(handed, n[1])

                link(dve.tensor_scalar(less[:, :], s.validS[:, :], 1.0, BIG, ALU.subtract, ALU.mult))
                link(dve.tensor_tensor(s.score[:, :, :], s.score[:, :, :],
                                       s.validS[:, :, None].to_broadcast([P, J, H]), ALU.mult))
                for b in range(G):
                    dve.tensor_tensor(by_row[:, :, b, :], score_v[:, b, :, :],
                                      less_v[:, b, :, None].to_broadcast([P, NG, H]), ALU.add).then_inc(masked, 1)
                link(dve.tensor_copy(pi[:, 0:1], s.pcol[:, :]))
                link(dve.tensor_scalar(pi[:, 1:2], pi[:, 0:1], H - 1, None, ALU.bitwise_and))
                link(dve.tensor_copy(pf[:, 1:2], pi[:, 1:2]))
                link(dve.tensor_tensor(pf[:, 0:1], s.pcol[:, :], pf[:, 1:2], ALU.subtract))
                link(dve.tensor_scalar(head[:, :], s.iota[:, 0:H], pf[:, 1:2], None, ALU.is_equal))
                link(dve.tensor_scalar(blk[:, :], s.iota[:, 0:G], float(H), None, ALU.mult))
                link(dve.tensor_scalar(blk[:, :], blk[:, :], pf[:, 0:1], None, ALU.is_equal))
                for g in range(NG):
                    if g >= 2:
                        dve.wait_ge(key_turned, g - 1)
                    dve.tensor_copy(group_row[:, g % 2, :].rearrange("p (b h) -> p b h", h=H),
                                    key_v[:, :, g, None].to_broadcast([P, G, H])).then_inc(key_rows, 1)
                    if g >= 1:
                        dve.wait_ge(key_turned, g)
                        dve.tensor_copy(key[:, 1 + (g - 1) * P:1 + g * P], ps[(g - 1) % 2][:, 0:P]).then_inc(key_evicted, 1)
                dve.wait_ge(key_turned, NG)
                dve.tensor_copy(key[:, 1 + (NG - 1) * P:1 + NG * P], ps[(NG - 1) % 2][:, 0:P]).then_inc(key_evicted, 1)
                dve.wait_ge(key_evicted, NG)
                hand(dve.tensor_scalar(wide[:, 0:G], blk[:, :], key[:, L:L + 1], None, ALU.mult))
                dve.wait_ge(pe_step, 2)
                link(dve.tensor_copy(headT[:, :], ps[5][0:H, 0:P]))
                link(dve.memset(carry[:, 0:1], -2.0))
                hand(dve.tensor_copy(carry[:, 1:G + 1], ps[4][0:H, 0:G]))
                dve.wait_ge(pe_step, 3)
                link(dve.tensor_tensor(back[:, :], blk[:, :], ps[4][:, 0:G], ALU.mult))
                link(dve.tensor_reduce(key[:, 0:1], back[:, :], AX_X, ALU.add))
                link(dve.tensor_tensor(pen[:, 0:L], key[:, 1:L + 1], key[:, 0:L], ALU.not_equal))
                link(dve.tensor_scalar(pen[:, 0:L], pen[:, 0:L], -BIG, None, ALU.mult))
                link(dve.tensor_reduce(edge[:, 1:2], pen[:, 0:L], AX_X, ALU.min))
                dve.wait_ge(sc_evicted, NG)
                link(dve.tensor_tensor_scan(mx[:, :], pen[:, 0:L], sc[:, :], -BIG, ALU.add, ALU.max))
                link(dve.tensor_copy(edge[:, 0:1], mx[:, L - 1:L]))
                link(dve.tensor_copy(edge[:, 2:3], pen[:, 0:1]))
                for a in range(3):
                    (hand if a == 2 else link)(dve.tensor_scalar(wide[:, a * G:(a + 1) * G], blk[:, :], edge[:, a:a + 1], None, ALU.mult))
                dve.wait_ge(pe_step, 4)
                link(dve.tensor_copy(small[:, :], ps[4][0:H, 0:3 * G]))
                link(dve.memset(carry[:, 0:1], -BIG))
                hand(dve.tensor_tensor_scan(carry[:, 1:G + 1], small[:, G:2 * G], small[:, 0:G], -BIG, ALU.add, ALU.max))
                dve.wait_ge(pe_step, 5)
                link(dve.tensor_tensor(back[:, :], blk[:, :], ps[4][:, 0:G], ALU.mult))
                link(dve.tensor_reduce(carried[:, 0:1], back[:, :], AX_X, ALU.add))
                link(dve.tensor_tensor_scan(mx[:, :], pen[:, 0:L], sc[:, :], carried[:, 0:1], ALU.add, ALU.max))
                link(dve.memset(carry[:, G:G + 1], -BIG))
                link(dve.tensor_copy(carry[:, 0:G - 1], small[:, 2 * G + 1:3 * G]))
                hand(dve.memset(carry[:, G - 1:G], -BIG))
                dve.wait_ge(pe_step, 6)
                link(dve.tensor_tensor(back[:, :], blk[:, :], ps[4][:, 0:G], ALU.mult))
                link(dve.tensor_reduce(pen[:, L:L + 1], back[:, :], AX_X, ALU.add))
                link(dve.tensor_reduce(edge[:, 1:2], pen[:, 1:L + 1], AX_X, ALU.min))
                link(dve.tensor_tensor_scan(key[:, 0:L][:, ::-1], pen[:, 1:L + 1][:, ::-1], mx[:, :][:, ::-1],
                                            -BIG, ALU.add, ALU.max))
                link(dve.tensor_copy(edge[:, 0:1], key[:, 0:1]))
                for a in range(2):
                    (hand if a == 1 else link)(dve.tensor_scalar(wide[:, a * G:(a + 1) * G], blk[:, :], edge[:, a:a + 1], None, ALU.mult))
                dve.wait_ge(pe_step, 7)
                link(dve.tensor_copy(small[:, 0:2 * G], ps[4][0:H, 0:2 * G]))
                link(dve.memset(carry[:, G - 1:G], -BIG))
                hand(dve.tensor_tensor_scan(carry[:, 0:G - 1][:, ::-1], small[:, G + 1:2 * G][:, ::-1],
                                            small[:, 1:G][:, ::-1], -BIG, ALU.add, ALU.max))
                dve.wait_ge(pe_step, 8)
                link(dve.tensor_tensor(back[:, :], blk[:, :], ps[4][:, 0:G], ALU.mult))
                link(dve.tensor_reduce(carried[:, 1:2], back[:, :], AX_X, ALU.add))
                link(dve.tensor_tensor_scan(key[:, 0:L][:, ::-1], pen[:, 1:L + 1][:, ::-1], mx[:, :][:, ::-1],
                                            carried[:, 1:2], ALU.add, ALU.max))
                hand(dve.tensor_tensor(sc[:, :], sc[:, :], key[:, 0:L], ALU.subtract))

            @block.scalar
            def _(act):
                for g in range(NG):
                    act.wait_ge(sc_turned, g + 1)
                    act.activation(sc[:, g * P:(g + 1) * P], ps[2 + g % 2][:, 0:P], ACT.Copy).then_inc(sc_evicted, 1)
                act.wait_ge(handed, 8)
                for g in range(NG):
                    act.activation(sc[:, g * P:(g + 1) * P], sc[:, g * P:(g + 1) * P], ACT.Exp).then_inc(exps, 1)
                for g in range(NG):
                    act.wait_ge(ex_turned, g + 1)
                    act.activation(s.score[:, :, :].rearrange("p (b g) h -> p b g h", g=NG)[:, :, g, :],
                                   ps[g % 2][:, 0:P].rearrange("p (b h) -> p b h", h=H), ACT.Copy).then_inc(ex_evicted, 1)

            @block.tensor
            def _(pe):
                def spread(after):
                    pe.wait_ge(handed, after)
                    pe.matmul(ps[4][:, 0:G], headT[:, :], carry[:, 0:G], start=True, stop=True).then_inc(pe_step, 1)

                def gather(after, m):
                    pe.wait_ge(handed, after)
                    pe.matmul(ps[4][0:H, 0:m], head[:, :], wide[:, 0:m], start=True, stop=True).then_inc(pe_step, 1)

                for g in range(NG):
                    pe.wait_ge(key_rows, g + 1)
                    if g >= 2:
                        pe.wait_ge(key_evicted, g - 1)
                    pe.transpose(ps[g % 2][:, 0:P], group_row[:, g % 2, :], s.ident[:, :]).then_inc(key_turned, 1)
                pe.wait_ge(masked, G)
                for g in range(NG):
                    if g >= 2:
                        pe.wait_ge(sc_evicted, g - 1)
                    pe.transpose(ps[2 + g % 2][:, 0:P], by_row[:, g, :, :].rearrange("p b h -> p (b h)"), s.ident[:, :]).then_inc(sc_turned, 1)
                gather(1, G)
                pe.transpose(ps[5][0:H, 0:P], head[:, :], s.ident[:, :]).then_inc(pe_step, 1)
                spread(2)
                gather(3, 3 * G)
                spread(4)
                spread(5)
                gather(6, 2 * G)
                spread(7)
                for g in range(NG):
                    pe.wait_ge(exps, g + 1)
                    if g >= 2:
                        pe.wait_ge(ex_evicted, g - 1)
                    pe.transpose(ps[g % 2][:, 0:P], sc[:, g * P:(g + 1) * P], s.ident[:, :]).then_inc(ex_turned, 1)


def stage_attend(nc, s):
    with ExitStack() as ctx:
        sb, pb, sem = makers(nc, ctx, "attend")
        ps = [pb(f"att_ps{a}", [P, 512], F32) for a in range(4)]
        val = sb("val", [P, 2, G, DIM], F32)
        msg = sb("msg", [P, 2, G, UW], F32)
        oh = sb("oh", [P, G, P], F32)
        val_in = [sem(f"val_in{a}") for a in range(2)]
        weighted, copied, oh_made, summed, added, zeroed = (sem("weighted"), sem("copied"), sem("oh_made"),
                                                            sem("summed"), sem("added"), sem("zeroed"))
        with nc.Block() as block:
            @block.sync
            def _(sp):
                first = [sp.alloc_register(f"att_first{q}") for q in range(G)]
                with chunks(sp, J, TWO) as i:
                    for half in range(2):
                        g = i + half * G
                        sp.load(first, s.start_of[0][0:1, bass.ds(g, G)])
                        sp.wait_ge(weighted, g + G)
                        for q in range(G):
                            at = sp.snap(first[q], min_val=0, max_val=E)
                            sp.dma_start(val[:, half, q, :], s.rows[bass.ds(at, P), 0:DIM]).then_inc(val_in[half], 16)

            @block.gpsimd
            def _(pool):
                pool.sem_inc(weighted, TWO)
                with chunks(pool, J, TWO) as i:
                    for half in range(2):
                        g = i + half * G
                        pool.wait_ge(val_in[half], i * G + 16 * G)
                        for q in range(G):
                            pool.wait_ge(summed, g + q + 1)
                            pool.tensor_tensor(msg[:, half, q, 0:DIM].rearrange("p (h d) -> p h d", h=H),
                                               val[:, half, q, :].rearrange("p (h d) -> p h d", h=H),
                                               s.score[:, bass.ds(g + q, 1), :].rearrange("p o h -> p h o").to_broadcast([P, H, DIM // H]),
                                               ALU.mult).then_inc(weighted, 1)

            @block.scalar
            def _(act):
                with chunks(act, J, TWO) as i:
                    for half in range(2):
                        g = i + half * G
                        act.wait_ge(summed, g + G)
                        act.activation(msg[:, half, :, DIM:UW], s.score[:, bass.ds(g, G), :], ACT.Copy).then_inc(copied, G)

            @block.tensor
            def _(pe):
                pe.sem_inc(summed, TWO)
                with chunks(pe, J, TWO) as i:
                    for half in range(2):
                        g = i + half * G
                        pe.wait_ge(copied, g + G)
                        for q in range(G):
                            pe.wait_ge(oh_made, g + q + 1)
                            pe.wait_ge(weighted, g + q + 1 + TWO)
                            pe.wait_ge(added, g + q + 1)
                            pe.matmul(ps[q % 4][:, 0:UW], oh[:, q, :], msg[:, half, q, :], start=True,
                                      stop=True).then_inc(summed, 1)

            @block.vector
            def _(dve):
                tile = [dve.alloc_register(f"att_tile{q}") for q in range(G)]
                dve.sem_inc(added, 4)
                dve.memset(s.acc[:, :, :], 0.0).then_inc(zeroed, 1)
                dve.wait_ge(zeroed, 1)
                with chunks(dve, J, G) as g:
                    dve.load(tile, s.tile_of[0][0:1, bass.ds(g, G)])

                    def onehot(q):
                        dve.wait_ge(summed, g + q + 1 + G)
                        dve.tensor_scalar(oh[:, q, :], s.iota[:, :], s.relS[:, bass.ds(g + q, 1)], None,
                                          ALU.is_equal).then_inc(oh_made, 1)

                    for q in range(3):
                        onehot(q)
                    for q in range(G):
                        if q + 3 < G:
                            onehot(q + 3)
                        t = dve.snap(tile[q], min_val=0, max_val=NT - 1)
                        dve.wait_ge(summed, g + q + 1 + TWO)
                        dve.wait_ge(added, g + q + 4)
                        dve.tensor_tensor(s.acc[:, bass.ds(t, 1), :], s.acc[:, bass.ds(t, 1), :],
                                          ps[q % 4][:, None, 0:UW], ALU.add).then_inc(added, 1)


def stage_norm(nc, s, io):
    with ExitStack() as ctx:
        sb, pb, sem = makers(nc, ctx, "norm")
        x = sb("x_rows", [P, NT, DIM], F32)
        den = sb("den", [P, NT, H], F32)
        rden = sb("rden", [P, NT, H], F32)
        stats = sb("stats", [P, NT, 6], F32)
        mv = sb("mv", [P, NT, 2], F32)
        std = sb("std", [P, NT], F32)
        rstd = sb("rstd", [P, NT], F32)
        x_in, step, normed, rooted, stored = sem("x_in"), sem("step"), sem("normed"), sem("rooted"), sem("stored")
        full = NT - 1
        with nc.Block() as block:
            @block.sync
            def _(sp):
                sp.wait_ge(step, 1)
                sp.dma_start(x[:, 0:full, :], io["x"][0:full * P, :].rearrange("(t p) f -> p t f", p=P)).then_inc(x_in, 16)
                sp.dma_start(x[0:LAST, full, :], io["x"][full * P:N, :]).then_inc(x_in, 16)
                sp.wait_ge(normed, NT)
                sp.dma_start(s.h_dram[0:full * P, :].rearrange("(t p) f -> p t f", p=P), s.h[:, 0:full, :]).then_inc(stored, 16)
                sp.dma_start(s.h_dram[full * P:N, :], s.h[0:LAST, full, :]).then_inc(stored, 16)
                sp.wait_ge(stored, 32)

            @block.scalar
            def _(act):
                act.wait_ge(step, 5)
                act.activation(std[:, :], mv[:, :, 1], ACT.Sqrt, bias=s.eps[:, 0:1]).then_inc(rooted, 1)

            @block.vector
            def _(dve):
                n = [0]

                def link(ins):
                    n[0] += 1
                    ins.then_inc(step, 1)
                    dve.wait_ge(step, n[0])

                link(dve.memset(x[:, full, :], 0.0))
                link(dve.tensor_scalar(den[:, :, :], s.acc[:, :, DIM:UW], EPS_SOFTMAX, None, ALU.add))
                link(dve.reciprocal(rden[:, :, :], den[:, :, :]))
                for t in range(NT):
                    ins = dve.tensor_tensor(s.h[:, t, :].rearrange("p (h d) -> p h d", h=H),
                                            s.acc[:, t, 0:DIM].rearrange("p (h d) -> p h d", h=H),
                                            rden[:, t, :, None].to_broadcast([P, H, DIM // H]), ALU.mult)
                    if t == NT - 1:
                        link(ins)
                dve.wait_ge(x_in, 32)
                for t in range(NT):
                    dve.tensor_tensor(s.h[:, t, :], s.h[:, t, :], x[:, t, :], ALU.add).then_inc(s.sum_made, 1)
                dve.wait_ge(s.sum_made, NT)
                for t in range(NT):
                    dve.bn_stats(stats[:, t, :], s.h[:, t, :]).then_inc(s.sum_made, 1)
                dve.wait_ge(s.sum_made, 2 * NT)
                for t in range(NT):
                    ins = dve.bn_aggr(mv[:, t, :], stats[:, t, :])
                    if t == NT - 1:
                        link(ins)
                dve.wait_ge(rooted, 1)
                link(dve.reciprocal(rstd[:, :], std[:, :]))
                for t in range(NT):
                    dve.tensor_scalar(s.h[:, t, :], s.h[:, t, :], mv[:, t, 0:1], rstd[:, t:t + 1],
                                      ALU.subtract, ALU.mult).then_inc(normed, 1)


def stage_neighbours(nc, s):
    with ExitStack() as ctx:
        sb, pb, sem = makers(nc, ctx, "neighbours")
        ps = [pb(f"nb_ps{a}", [P, 512], F32) for a in range(4)]
        nbr = [sb(f"nbr{q}", [P, LW], F32) for q in range(TWO)]
        idx = sb("nb_idx", [P, 2, G], I32)
        oh = sb("oh", [P, G, P], F32)
        gathered = [sem(f"gathered{q}") for q in range(TWO)]
        idx_made, typed, oh_made, summed, added, zeroed = (sem("idx_made"), sem("typed"), sem("oh_made"),
                                                           sem("summed"), sem("added"), sem("zeroed"))
        with nc.Block() as block:
            @block.gpsimd
            def _(pool):
                with chunks(pool, J, TWO) as i:
                    for half in range(2):
                        g = i + half * G
                        pool.wait_ge(idx_made, g + G)
                        pool.sem_inc(s.pool_passed, 1)
                        for q in range(G):
                            pool.wait_ge(summed, g + q + 1)
                            pool.sem_inc(s.pool_passed, 1)
                            pool.indirect_dma_start(
                                out=nbr[half * G + q][:, 0:DIM], out_offset=None, in_=s.h_dram,
                                in_offset=bass.IndirectOffsetOnAxis(ap=idx[:, half, q:q + 1], axis=0)
                            ).then_inc(gathered[half * G + q], 16)

            @block.tensor
            def _(pe):
                pe.sem_inc(summed, TWO)
                with chunks(pe, J, TWO) as i:
                    for half in range(2):
                        g = i + half * G
                        for q in range(G):
                            pe.wait_ge(typed, g + q + 1)
                            pe.wait_ge(oh_made, g + q + 1)
                            pe.wait_ge(gathered[half * G + q], i + 16)
                            pe.wait_ge(added, g + q + 1)
                            pe.matmul(ps[q % 4][:, 0:LW], oh[:, q, :], nbr[half * G + q][:, :], start=True,
                                      stop=True).then_inc(summed, 1)

            @block.vector
            def _(dve):
                tile = [dve.alloc_register(f"nb_tile{q}") for q in range(G)]
                dve.sem_inc(added, 4)
                dve.memset(s.acc2[:, :, :], 0.0).then_inc(zeroed, 1)
                dve.wait_ge(zeroed, 1)
                with chunks(dve, J, TWO) as i:
                    for half in range(2):
                        g = i + half * G
                        dve.load(tile, s.tile_of[1][0:1, bass.ds(g, G)])
                        dve.wait_ge(summed, g + G)
                        dve.tensor_copy(idx[:, half, :], s.src_of[:, bass.ds(g, G)]).then_inc(idx_made, G)

                        def onehot(q):
                            dve.wait_ge(summed, g + q + 1 + G)
                            dve.tensor_scalar(oh[:, q, :], s.iota[:, :], s.relD[:, bass.ds(g + q, 1)], None,
                                              ALU.is_equal).then_inc(oh_made, 1)
                            dve.tensor_scalar(nbr[half * G + q][:, DIM:LW], s.iota[:, 0:NREL],
                                              s.type_of[:, bass.ds(g + q, 1)], None, ALU.is_equal).then_inc(typed, 1)

                        for q in range(3):
                            onehot(q)
                        for q in range(G):
                            if q + 3 < G:
                                onehot(q + 3)
                            t = dve.snap(tile[q], min_val=0, max_val=NT - 1)
                            dve.wait_ge(summed, g + q + 1 + TWO)
                            dve.wait_ge(added, g + q + 4)
                            dve.tensor_tensor(s.acc2[:, bass.ds(t, 1), :], s.acc2[:, bass.ds(t, 1), :],
                                              ps[q % 4][:, None, 0:LW], ALU.add).then_inc(added, 1)


def stage_gru(nc, s, io, out):
    with ExitStack() as ctx:
        sb, pb, sem = makers(nc, ctx, "gru")
        psC = pb("psC", [P, 512], F32)
        psX = [pb(f"psX{a}", [P, 512], F32) for a in range(2)]
        psRZ = [pb(f"psRZ{a}", [P, 512], F32) for a in range(2)]
        psN = [pb(f"psN{a}", [P, 512], F32) for a in range(2)]
        wi = sb("wi", [P, 2, 3 * DIM], F32)
        wh = sb("wh", [P, 2, 3 * DIM], F32)
        bi = sb("bi", [1, 3 * DIM], F32)
        bh = sb("bh", [1, 3 * DIM], F32)
        rel = sb("rel", [NREL, DIM], F32)
        cT = sb("cT", [NREL, 2, P], F32)
        redT = sb("redT", [P, 2, 2, P], F32)
        hT = sb("hT", [P, 2, 2, P], F32)
        rz = sb("rz", [P, 2, 512], F32)
        nn = sb("nn", [P, 2, DIM], F32)
        w1 = sb("w1", [P, 2, DIM], F32)
        w2 = sb("w2", [P, 2, DIM], F32)
        stats = sb("stats", [P, 2, 6], F32)
        mv = sb("mv", [P, 2, 2], F32)
        std = sb("std", [P, 2], F32)
        rstd = sb("rstd", [P, 2], F32)
        y = sb("y", [P, 4, DIM], F32)
        loads, c_turned, cT_made, turned, T_made = sem("loads"), sem("c_turned"), sem("cT_made"), sem("turned"), sem("T_made")
        gates, gates_n, sig, tanh_done, rooted = sem("gates"), sem("gates_n"), sem("sig"), sem("tanh_done"), sem("rooted")
        step = sem("step")
        stored = [sem(f"stored{a}") for a in range(4)]
        S = 9
        with nc.Block() as block:
            @block.sync
            def _(sp):
                for a in range(2):
                    sp.dma_start(wi[:, a, :], io["wihT"][a * P:(a + 1) * P, :]).then_inc(loads, 16)
                    sp.dma_start(wh[:, a, :], io["whhT"][a * P:(a + 1) * P, :]).then_inc(loads, 16)
                sp.dma_start(bi[:, :], io["b_ih"]).then_inc(loads, 16)
                sp.dma_start(bh[:, :], io["b_hh"]).then_inc(loads, 16)
                sp.dma_start(rel[:, :], io["rel"]).then_inc(loads, 16)
                for t in range(NT):
                    rows = P if t < NT - 1 else LAST
                    sp.wait_ge(step, S * (t + 1))
                    sp.dma_start(out[t * P:t * P + rows, :], y[0:rows, t % 4, :]).then_inc(stored[t % 4], 16)
                for a in range(4):
                    sp.wait_ge(stored[a], 16 * len(range(a, NT, 4)))

            @block.tensor
            def _(pe):
                pe.wait_ge(loads, 16 * 7)

                def prepare(t):
                    b = t % 2
                    if t >= 1:
                        pe.wait_ge(cT_made, t)
                    pe.transpose(psC[0:NREL, 0:P], s.acc2[:, t, DIM:LW], s.ident[:, :]).then_inc(c_turned, 1)
                    if t >= 2:
                        pe.wait_ge(T_made, 2 * (t - 1))
                    for a in range(2):
                        pe.transpose(psX[b][:, 256 + a * P:256 + (a + 1) * P], s.h[:, t, a * P:(a + 1) * P], s.ident[:, :])
                    pe.wait_ge(cT_made, t + 1)
                    for a in range(2):
                        pe.matmul(psX[b][:, a * P:(a + 1) * P], s.acc2[:, t, a * P:(a + 1) * P], s.ident[:, :],
                                  start=True, stop=False)
                        last = pe.matmul(psX[b][:, a * P:(a + 1) * P], rel[:, a * P:(a + 1) * P], cT[:, b, :],
                                         start=False, stop=True)
                    last.then_inc(turned, 1)

                prepare(0)
                for t in range(NT):
                    b = t % 2
                    if t + 1 < NT:
                        prepare(t + 1)
                    pe.wait_ge(T_made, 2 * (t + 1))
                    if t >= 2:
                        pe.wait_ge(sig, t - 1)
                        pe.wait_ge(step, S * (t - 2) + 2)
                    pe.matmul(psRZ[b][:, :], s.ones[0:1, :], bi[:, 0:512], start=True, stop=False)
                    pe.matmul(psRZ[b][:, :], s.ones[0:1, :], bh[:, 0:512], start=False, stop=False)
                    for a in range(2):
                        pe.matmul(psRZ[b][:, :], redT[:, b, a, :], wi[:, a, 0:512], start=False, stop=False)
                    for a in range(2):
                        last = pe.matmul(psRZ[b][:, :], hT[:, b, a, :], wh[:, a, 0:512], start=False, stop=(a == 1))
                    last.then_inc(gates, 1)
                    pe.matmul(psN[b][:, 0:DIM], s.ones[0:1, :], bi[:, 512:], start=True, stop=False)
                    for a in range(2):
                        pe.matmul(psN[b][:, 0:DIM], redT[:, b, a, :], wi[:, a, 512:], start=False, stop=(a == 1))
                    pe.matmul(psN[b][:, DIM:], s.ones[0:1, :], bh[:, 512:], start=True, stop=False)
                    for a in range(2):
                        last = pe.matmul(psN[b][:, DIM:], hT[:, b, a, :], wh[:, a, 512:], start=False, stop=(a == 1))
                    last.then_inc(gates_n, 1)

            @block.scalar
            def _(act):
                def copies(t):
                    b = t % 2
                    act.wait_ge(c_turned, t + 1)
                    act.activation(cT[:, b, :], psC[0:NREL, 0:P], ACT.Copy).then_inc(cT_made, 1)
                    act.wait_ge(turned, t + 1)
                    if t >= 2:
                        act.wait_ge(gates_n, t - 1)
                    act.activation(redT[:, b, :, :], psX[b][:, 0:256].rearrange("p (a n) -> p a n", a=2), ACT.Copy).then_inc(T_made, 1)
                    act.activation(hT[:, b, :, :], psX[b][:, 256:512].rearrange("p (a n) -> p a n", a=2), ACT.Copy).then_inc(T_made, 1)

                copies(0)
                for t in range(NT):
                    b = t % 2
                    if t + 1 < NT:
                        copies(t + 1)
                    act.wait_ge(gates, t + 1)
                    if t >= 2:
                        act.wait_ge(step, S * (t - 2) + 5)
                    act.activation(rz[:, b, :], psRZ[b][:, :], ACT.Sigmoid).then_inc(sig, 1)
                    act.wait_ge(step, S * t + 2)
                    act.activation(nn[:, b, :], w2[:, b, :], ACT.Tanh).then_inc(tanh_done, 1)
                    act.wait_ge(step, S * t + 7)
                    act.activation(std[:, b:b + 1], mv[:, b, 1:2], ACT.Sqrt, bias=s.eps[:, 0:1]).then_inc(rooted, 1)

            @block.vector
            def _(dve):
                n = [0]

                def link(ins):
                    n[0] += 1
                    ins.then_inc(step, 1)
                    dve.wait_ge(step, n[0])

                for t in range(NT):
                    b = t % 2
                    dve.wait_ge(sig, t + 1)
                    dve.wait_ge(gates_n, t + 1)
                    link(dve.tensor_tensor(w1[:, b, :], rz[:, b, 0:DIM], psN[b][:, DIM:], ALU.mult))
                    link(dve.tensor_tensor(w2[:, b, :], w1[:, b, :], psN[b][:, 0:DIM], ALU.add))
                    dve.wait_ge(tanh_done, t + 1)
                    link(dve.tensor_tensor(w1[:, b, :], s.h[:, t, :], nn[:, b, :], ALU.subtract))
                    link(dve.tensor_tensor(w2[:, b, :], rz[:, b, DIM:], w1[:, b, :], ALU.mult))
                    link(dve.tensor_tensor(w1[:, b, :], w2[:, b, :], nn[:, b, :], ALU.add))
                    dve.tensor_tensor(w2[:, b, :], w1[:, b, :], s.h[:, t, :], ALU.add).then_inc(s.sum_made2, 1)
                    dve.wait_ge(s.sum_made2, t + 1)
                    link(dve.bn_stats(stats[:, b, :], w2[:, b, :]))
                    link(dve.bn_aggr(mv[:, b, :], stats[:, b, :]))
                    dve.wait_ge(rooted, t + 1)
                    link(dve.reciprocal(rstd[:, b:b + 1], std[:, b:b + 1]))
                    if t >= 4:
                        dve.wait_ge(stored[t % 4], 16 * (t // 4))
                    link(dve.tensor_scalar(y[:, t % 4, :], w2[:, b, :], mv[:, b, 0:1], rstd[:, b:b + 1],
                                           ALU.subtract, ALU.mult))


def build(nc, io, out, upto=99):
    s = Shared()
    dram = lambda n, sh, dt: nc.dram_tensor(n, sh, dt, kind="Internal").ap()
    s.rows = dram("rows", (EPAD, ROW), F32)
    s.recs = dram("recs", (EPAD, REC), F32)
    s.h_dram = dram("h_rows", (N, DIM), F32)
    s.hiT = [dram(f"hiT{k}", (E,), F32) for k in range(2)]
    s.hiT2 = [a.rearrange("(c p) -> c p", p=EP) for a in s.hiT]
    with ExitStack() as ctx:
        sb = lambda n, sh, dt: ctx.enter_context(nc.sbuf_tensor(n, sh, dt))
        constants(nc, s, sb)
        s.sum_made = ctx.enter_context(nc.semaphore("sum_made"))
        s.pool_passed = ctx.enter_context(nc.semaphore("pool_passed"))
        s.sum_made2 = ctx.enter_context(nc.semaphore("sum_made2"))
        s.tile_of = [sb(f"tile_of{k}", [1, J], I32) for k in range(2)]
        s.start_of = [sb(f"start_of{k}", [1, J], I32) for k in range(2)]
        s.base = [sb(f"base{k}", [P, J], F32) for k in range(2)]
        s.relD = sb("relD", [P, J], F32)
        s.src_of = sb("src_of", [P, J], I32)
        s.type_of = sb("type_of", [P, J], F32)
        s.scores_or_h = sb("scores_or_h", [P, J * H], F32)
        s.score = s.scores_or_h[:, :].rearrange("p (j h) -> p j h", h=H)
        s.h = s.scores_or_h[:, 0:NT * DIM].rearrange("p (t d) -> p t d", d=DIM)
        with ExitStack() as layer0:
            sbl = lambda n, sh, dt: layer0.enter_context(nc.sbuf_tensor(n, sh, dt))
            s.relS = sbl("relS", [P, J], F32)
            s.validS = sbl("validS", [P, J], F32)
            s.src_key = sbl("src_key", [P, J], F32)
            with ExitStack() as tables:
                s.tab = tables.enter_context(nc.sbuf_tensor("tab", [P, NT, 3, 512], BF16))
                with ExitStack() as early:
                    sbe = lambda n, sh, dt: early.enter_context(nc.sbuf_tensor(n, sh, dt))
                    s.start = [sbe(f"start{k}", [NT, P], F32) for k in range(2)]
                    s.rec = sbe("rec", [EP, EC, REC], F32)
                    s.most_drop = sbe("most_drop", [1, 1], F32)
                    s.unsorted = sbe("unsorted", [1, 1], I32)
                    s.sorted = sbe("sorted", [1, 1], I32)
                    s.count = [sbe(f"count{k}", [NT, P], F32) for k in range(2)]
                    s.place = sbe("place", [EP, EC], F32)
                    s.key = [sbe(f"key{k}", [EP, EC], F32) for k in range(2)]
                    s.hi = [sbe(f"hi{k}", [EP, EC], F32) for k in range(2)]
                    s.lo = [sbe(f"lo{k}", [EP, EC], F32) for k in range(2)]
                    stage_constants(nc, s, io)
                    stage_count_project(nc, s, io)
                    stage_schedule(nc, s, 0)
                    stage_schedule(nc, s, 1)
                    stage_rank(nc, s, io, 0)
                    stage_rank(nc, s, io, 1, s.unsorted)
                    stage_sort_records(nc, s, s.unsorted)
                    stage_store_records(nc, s, s.sorted)
                stage_rows(nc, s)
                stage_scores(nc, s, io)
            stage_softmax(nc, s)
            s.acc = sbl("acc", [P, NT, UW], F32)
            stage_attend(nc, s)
            stage_norm(nc, s, io)
        s.acc2 = sb("acc2", [P, NT, LW], F32)
        stage_neighbours(nc, s)
        stage_gru(nc, s, io, out)


def kernel(x, src, dst, edge_attr_18, edge_type_16, L0_gnn_Wqkv, L0_gnn_bqkv, L0_gnn_Wk_rpe, L0_gnn_bk_rpe,
           L0_gnn_Wq_rpe, L0_gnn_bq_rpe, L1_gnn_relvectors, L1_gnn_w_ih, L1_gnn_w_hh, L1_gnn_b_ih, L1_gnn_b_hh):
    import concourse.bacc as bacc
    from concourse.bass_utils import run_bass_kernel_spmd

    row = lambda a: np.asarray(a).reshape(1, -1)
    grid = lambda a: np.asarray(a).reshape(EP, EC)
    layout = {
        "x": np.asarray(x), "xT": np.asarray(x).T,
        "src": grid(src), "dst": grid(dst), "type": grid(edge_type_16),
        "srcT": grid(src).T, "dstT": grid(dst).T,
        "attr": np.asarray(edge_attr_18).reshape(EP, EC * RP),
        "Wqkv": np.asarray(L0_gnn_Wqkv), "bqkv": row(L0_gnn_bqkv),
        "Wk_rpe": np.asarray(L0_gnn_Wk_rpe), "bk_rpe": row(L0_gnn_bk_rpe),
        "Wq_rpe": np.asarray(L0_gnn_Wq_rpe), "bq_rpe": row(L0_gnn_bq_rpe),
        "rel": np.asarray(L1_gnn_relvectors),
        "wihT": np.asarray(L1_gnn_w_ih).T, "whhT": np.asarray(L1_gnn_w_hh).T,
        "b_ih": row(L1_gnn_b_ih), "b_hh": row(L1_gnn_b_hh),
    }
    layout = {name: np.ascontiguousarray(a) for name, a in layout.items()}
    nc = bacc.Bacc("TRN2", target_bir_lowering=False, num_devices=1)
    io = {name: nc.dram_tensor(f"in_{name}", a.shape, mybir.dt.from_np(a.dtype), kind="ExternalInput").ap()
          for name, a in layout.items()}
    out = nc.dram_tensor("out", (N, DIM), F32, kind="ExternalOutput").ap()
    build(nc, io, out)
    r = run_bass_kernel_spmd(nc, [{f"in_{name}": a for name, a in layout.items()}], core_ids=[0])
    return r.results[0]["out"]
```

```python
from contextlib import ExitStack, contextmanager

import concourse.bass as bass
import numpy as np
from concourse import mybir

ALU = mybir.AluOpType
ACT = mybir.ActivationFunctionType
AX_X = mybir.AxisListType.X
F32 = mybir.dt.float32
BF16 = mybir.dt.bfloat16
I32 = mybir.dt.int32

P = 128
N, E = 3125, 50000
DIM, H, D, RP, NREL = 256, 16, 8, 18, 16
DH = H * D
NT = -(-N // P)
NPAD = NT * P
LAST = N - (NT - 1) * P
EP, EC = 125, 400
G = 8
TWO = 2 * G
FOUR = 4 * G
J = -(-((E + NT * (P - 1)) // P) // FOUR) * FOUR
EPAD = E + P
NH = 2 * (J // FOUR)
SCALE = D ** -0.5
BIG = 1e30
SKIP = float(1 << 17)

REC = 24
C_ONE, C_SRC, C_DST, C_TYPE, C_RANK = 18, 19, 20, 21, 22
ROW = DIM + DH + REC
KM = DH + REC
RA = RP + 1
PW = 2 * DH + 4 * DIM
UW = DIM + H
LW = DIM + NREL
EPS_SOFTMAX, EPS_NORM = 1e-16, 1e-5


@contextmanager
def chunks(engine, count, body):
    with engine.Fori(0, count // body) as n:
        yield engine.snap(n * body)


@contextmanager
def when(engine, flag):
    if flag is None:
        yield
    else:
        with engine.If(engine.value_load(flag[0:1, 0:1], min_val=0, max_val=1)):
            yield


def makers(nc, ctx, stage):
    sems = []

    def give_back():
        nc.clear_and_free_semaphores(sems)
        nc.all_engine_barrier()

    def sem(name):
        sems.append(nc.alloc_semaphore(f"{stage}_{name}"))
        return sems[-1]

    ctx.callback(give_back)
    return (lambda name, shape, dt: ctx.enter_context(nc.sbuf_tensor(f"{stage}_{name}", shape, dt)),
            lambda name, shape, dt: ctx.enter_context(nc.psum_tensor(f"{stage}_{name}", shape, dt)), sem)


class Shared:
    pass


def constants(nc, s, sb):
    s.iota = sb("iota", [P, P], F32)
    s.iota_b = sb("iota_b", [P, P], BF16)
    s.pcol = sb("pcol", [P, 1], F32)
    s.before = sb("before", [P, P], F32)
    s.after = sb("after", [P, P], F32)
    s.ident = sb("ident", [P, P], F32)
    s.ident_b = sb("ident_b", [P, P], BF16)
    s.ones = sb("ones", [P, P], F32)
    s.negp = sb("negp", [P, 1], F32)
    s.ones_b = sb("ones_b", [6, P], BF16)
    s.eps = sb("eps", [P, 2], F32)


def stage_constants(nc, s, io):
    with ExitStack() as ctx:
        sb, pb, sem = makers(nc, ctx, "constants")
        attr = s.tab[0:EP, :, :, :].rearrange("p a b c -> p (a b c)")[:, 0:2 * EC * RP].bitcast(F32)
        ints = [sb(f"ints{k}", [EP, EC], I32) for k in range(3)]
        tmp = [sb(f"shifted{k}", [EP, EC], I32) for k in range(4)]
        keysT = [sb(f"keysT{k}", [100, E // 100], I32) for k in range(2)]
        hiTi = [sb(f"hiTi{k}", [100, E // 100], I32) for k in range(2)]
        hiTf = [sb(f"hiTf{k}", [100, E // 100], F32) for k in range(2)]
        iota_i = sb("iota_i", [P, P], I32)
        pcol_i = sb("pcol_i", [P, 1], I32)
        pad = sb("pad", [P, ROW], F32)
        following = sb("following", [EP, EC], I32)
        drop = sb("drop", [EP, EC], F32)
        most = sb("most", [EP, 1], F32)
        ps_most = pb("ps_most", [P, 512], F32)
        loads, loaded_attr, loadedT = sem("loads"), sem("loaded_attr"), sem("loadedT")
        iotas, filled, base_done, dve_done = sem("iotas"), sem("filled"), sem("base_done"), sem("dve_done")
        next_in, flag_step, most_turned = sem("next_in"), sem("flag_step"), sem("most_turned")
        pads, hi_out, attr_done = sem("pads"), sem("hi_out"), sem("attr_done")
        with nc.Block() as block:
            @block.sync
            def _(sp):
                for k, name in enumerate(("src", "dst", "type")):
                    sp.dma_start(ints[k][:, :], io[name]).then_inc(loads, 16)
                for k, name in enumerate(("srcT", "dstT")):
                    sp.dma_start(keysT[k][:, :], io[name].rearrange("(a b) c -> a (b c)", a=100)).then_inc(loadedT, 16)
                dst_flat = io["dst"].rearrange("p c -> (p c)")
                sp.wait_ge(flag_step, 1)
                sp.dma_start(following[0:EP - 1, :], dst_flat[1:1 + (EP - 1) * EC].rearrange("(p c) -> p c", c=EC)).then_inc(next_in, 16)
                sp.dma_start(following[EP - 1:EP, 0:EC - 1], io["dst"][EP - 1:EP, 1:EC]).then_inc(next_in, 16)
                sp.dma_start(attr, io["attr"]).then_inc(loaded_attr, 16)
                sp.wait_ge(base_done, 3)
                sp.dma_start(s.rows[E:EPAD, :], pad[:, :]).then_inc(pads, 16)
                sp.dma_start(s.recs[E:EPAD, :], pad[:, DIM + DH:ROW]).then_inc(pads, 16)
                sp.wait_ge(hi_out, 2)
                for k in range(2):
                    sp.dma_start(s.hiT[k].rearrange("(a b) -> a b", a=100), hiTf[k][:, :]).then_inc(pads, 16)
                sp.wait_ge(pads, 64)

            @block.gpsimd
            def _(pool):
                pool.iota(iota_i[:, :], pattern=[[1, P]], base=0, channel_multiplier=0).then_inc(iotas, 1)
                pool.iota(pcol_i[:, :], pattern=[[0, 1]], base=0, channel_multiplier=1).then_inc(iotas, 1)
                for t in (s.ident, s.before, s.after):
                    pool.memset(t[:, :], 0.0 if t is s.ident else 1.0).then_inc(filled, 1)
                pool.wait_ge(filled, 3)
                pool.affine_select(out=s.ident[:, :], in_=s.ident[:, :], compare_op=ALU.not_equal, fill=1.0,
                                   base=0, pattern=[[-1, P]], channel_multiplier=1).then_inc(filled, 1)
                pool.affine_select(out=s.before[:, :], in_=s.before[:, :], compare_op=ALU.is_gt, fill=0.0,
                                   base=0, pattern=[[-1, P]], channel_multiplier=1).then_inc(filled, 1)
                pool.affine_select(out=s.after[:, :], in_=s.after[:, :], compare_op=ALU.is_gt, fill=0.0,
                                   base=0, pattern=[[1, P]], channel_multiplier=-1).then_inc(filled, 1)

            @block.scalar
            def _(act):
                act.wait_ge(loaded_attr, 16)
                act.activation(s.rec[:, :, 0:RP], attr.rearrange("p (c k) -> p c k", k=RP), ACT.Copy).then_inc(attr_done, 1)

            @block.tensor
            def _(pe):
                pe.wait_ge(flag_step, 4)
                pe.transpose(ps_most[0:1, 0:EP], most[:, :], s.ident[0:EP, 0:EP]).then_inc(most_turned, 1)

            @block.vector
            def _(dve):
                dve.memset(following[:, EC - 1:EC], N).then_inc(flag_step, 1)
                dve.memset(pad[:, :], 0.0).then_inc(base_done, 1)
                dve.wait_ge(base_done, 1)
                dve.memset(pad[:, DIM + DH + C_SRC:DIM + DH + C_SRC + 1], -1.0).then_inc(base_done, 1)
                dve.memset(pad[:, DIM + DH + C_DST:DIM + DH + C_DST + 1], -1.0).then_inc(base_done, 1)
                dve.memset(s.ones[:, :], 1.0).then_inc(dve_done, 1)
                dve.memset(s.rec[:, :, C_ONE:C_ONE + 1], 1.0).then_inc(dve_done, 1)
                dve.memset(s.rec[:, :, REC - 1:REC], 0.0).then_inc(dve_done, 1)
                dve.memset(s.eps[:, 0:1], EPS_NORM).then_inc(dve_done, 1)
                dve.memset(s.ones_b[:, :], 1.0).then_inc(dve_done, 1)
                dve.wait_ge(iotas, 2)
                dve.tensor_scalar(s.negp[:, :], pcol_i[:, :], -1.0, None, ALU.mult).then_inc(dve_done, 1)
                dve.wait_ge(iotas, 2)
                dve.tensor_copy(s.iota[:, :], iota_i[:, :]).then_inc(dve_done, 1)
                dve.tensor_copy(s.iota_b[:, :], iota_i[:, :]).then_inc(dve_done, 1)
                dve.tensor_copy(s.pcol[:, :], pcol_i[:, :]).then_inc(dve_done, 1)
                dve.wait_ge(filled, 4)
                dve.tensor_copy(s.ident_b[:, :], s.ident[:, :]).then_inc(dve_done, 1)
                dve.wait_ge(loadedT, 32)
                for k in range(2):
                    dve.tensor_scalar(hiTi[k][:, :], keysT[k][:, :], 7, None, ALU.arith_shift_right).then_inc(dve_done, 1)
                dve.wait_ge(dve_done, 12)
                for k in range(2):
                    dve.tensor_copy(hiTf[k][:, :], hiTi[k][:, :]).then_inc(hi_out, 1)
                dve.wait_ge(loads, 48)
                for k in range(2):
                    dve.tensor_scalar(tmp[2 * k][:, :], ints[k][:, :], 7, None, ALU.arith_shift_right).then_inc(dve_done, 1)
                    dve.tensor_scalar(tmp[2 * k + 1][:, :], ints[k][:, :], 127, None, ALU.bitwise_and).then_inc(dve_done, 1)
                    dve.tensor_copy(s.key[k][:, :], ints[k][:, :]).then_inc(dve_done, 1)
                for k, c in enumerate((C_SRC, C_DST, C_TYPE)):
                    dve.tensor_copy(s.rec[:, :, c], ints[k][:, :]).then_inc(dve_done, 1)
                dve.wait_ge(next_in, 32)
                dve.tensor_copy(drop[:, :], following[:, :]).then_inc(flag_step, 1)
                dve.wait_ge(dve_done, 21)
                dve.wait_ge(flag_step, 2)
                dve.tensor_tensor(drop[:, :], s.key[1][:, :], drop[:, :], ALU.subtract).then_inc(flag_step, 1)
                dve.wait_ge(flag_step, 3)
                dve.tensor_reduce(most[:, :], drop[:, :], AX_X, ALU.max).then_inc(flag_step, 1)
                dve.wait_ge(most_turned, 1)
                dve.tensor_reduce(s.most_drop[:, :], ps_most[0:1, 0:EP], AX_X, ALU.max).then_inc(flag_step, 1)
                dve.wait_ge(flag_step, 5)
                dve.tensor_scalar(s.unsorted[:, :], s.most_drop[:, :], 0.0, None, ALU.is_gt).then_inc(flag_step, 1)
                dve.tensor_scalar(s.sorted[:, :], s.most_drop[:, :], 0.0, None, ALU.is_le).then_inc(flag_step, 1)
                for k in range(2):
                    dve.tensor_copy(s.hi[k][:, :], tmp[2 * k][:, :]).then_inc(dve_done, 1)
                    dve.tensor_copy(s.lo[k][:, :], tmp[2 * k + 1][:, :]).then_inc(dve_done, 1)


def stage_schedule(nc, s, k):
    with ExitStack() as ctx:
        sb, pb, sem = makers(nc, ctx, f"schedule{k}")
        psum = [pb(f"sums{a}", [P, 512], F32) for a in range(3)]
        incl = sb("incl", [NT, P], F32)
        small = sb("small", [NT, 8], F32)
        small_i = sb("small_i", [NT, 2], I32)
        wide = sb("wide", [NT, 3, P], F32)
        gone = sb("gone", [NT, J], F32)
        iotaj_i = sb("iotaj_i", [P, J], I32)
        iotaj = sb("iotaj", [P, J], F32)
        fl = sb("fl", [P, 2, J], F32)
        step = sem("step")
        iota_made = sem("iota_made")
        sums = sem("sums")
        wa_cut, wa_placed = sem("wa_cut"), sem("wa_placed")
        Wa_rest = s.by_source[:, 0:PW]
        Wa_part = [sb("Wa_mid", [P, PW], BF16)[:, :], s.Wa[:, 0:PW // 2].bitcast(BF16)]
        count = s.count[k]
        pre, pt, pst = psum[0][0:NT, 0:2], psum[1][:, 0:J], psum[2][:, 0:J]
        n_t, nch, t0, c0, cend = (small[:, a:a + 1] for a in range(5))
        with nc.Block() as block:
            @block.gpsimd
            def _(pool):
                pool.iota(iotaj_i[:, :], pattern=[[1, J]], base=0, channel_multiplier=0).then_inc(iota_made, 1)
                if k == 0:
                    pool.wait_ge(wa_cut, 1)
                    pool.tensor_tensor(Wa_rest, s.Wa[:, :], s.parts[:, :], ALU.subtract).then_inc(wa_cut, 1)
                    pool.wait_ge(wa_cut, 3)
                    pool.tensor_tensor(Wa_part[1], Wa_rest, Wa_part[0], ALU.subtract).then_inc(wa_cut, 1)

            @block.scalar
            def _(act):
                if k == 0:
                    act.activation(s.parts[:, :], s.Wa[:, :], ACT.Copy).then_inc(wa_cut, 1)
                    act.wait_ge(wa_cut, 2)
                    act.activation(Wa_part[0], Wa_rest, ACT.Copy).then_inc(wa_cut, 1)

            @block.sync
            def _(sp):
                if k == 0:
                    sp.wait_ge(wa_cut, 4)
                    w = slice(0, 2 * DH)
                    sp.dma_start(s.parts[3 * RA:5 * RA, w], Wa_part[0][3 * RA:5 * RA, w]).then_inc(wa_placed, 16)
                    sp.dma_start(s.parts[5 * RA:6 * RA, w], Wa_part[1][5 * RA:6 * RA, w]).then_inc(wa_placed, 16)
                    for a in (0, 3):
                        for c in range(2):
                            r = slice(a + 1 + c, a + 2 + c)
                            sp.dma_start(s.parts[r, 2 * DH:], Wa_part[c][r, 2 * DH:]).then_inc(wa_placed, 16)
                    sp.wait_ge(wa_placed, 96)

            @block.tensor
            def _(pe):
                pe.wait_ge(step, 6)
                pe.matmul(pre, s.after[0:NT, 0:NT], small[:, 0:2], start=True, stop=True).then_inc(sums, 1)
                pe.wait_ge(step, 15)
                pe.matmul(pt, wide[:, 0, :], gone[:, :], start=True, stop=True).then_inc(sums, 1)
                pe.matmul(pst, wide[:, 1, :], gone[:, :], start=True, stop=True).then_inc(sums, 1)

            @block.vector
            def _(dve):
                n = [0]

                def link(ins):
                    n[0] += 1
                    ins.then_inc(step, 1)
                    dve.wait_ge(step, n[0])

                link(dve.tensor_reduce(n_t, count[:, :], AX_X, ALU.add))
                link(dve.tensor_scalar(small[:, 5:6], n_t, float(P - 1), None, ALU.add))
                link(dve.tensor_copy(small_i[:, 0:1], small[:, 5:6]))
                link(dve.tensor_scalar(small_i[:, 1:2], small_i[:, 0:1], 7, None, ALU.arith_shift_right))
                link(dve.tensor_copy(nch, small_i[:, 1:2]))
                link(dve.tensor_tensor_scan(incl[:, :], s.ones[0:NT, :], count[:, :], 0.0, ALU.mult, ALU.add))
                dve.wait_ge(sums, 1)
                link(dve.tensor_copy(small[:, 2:4], pre))
                link(dve.tensor_tensor(incl[:, :], incl[:, :], count[:, :], ALU.subtract))
                link(dve.tensor_scalar(s.start[k][:, :], incl[:, :], t0, None, ALU.add))
                link(dve.tensor_tensor(cend, c0, nch, ALU.add))
                dve.wait_ge(iota_made, 1)
                link(dve.tensor_copy(iotaj[:, :], iotaj_i[:, :]))
                link(dve.tensor_scalar(gone[:, :], iotaj[0:NT, :], cend, None, ALU.is_ge))
                link(dve.tensor_scalar(small[:, 6:7], nch, -float(P), n_t, ALU.mult, ALU.add))
                link(dve.memset(wide[:, 0, :], 1.0))
                link(dve.tensor_scalar(wide[:, 1, :], s.ones[0:NT, :], small[:, 6:7], None, ALU.mult))
                dve.wait_ge(sums, 3)
                link(dve.tensor_scalar(s.base[k][:, :], pt, float(P), None, ALU.mult))
                link(dve.tensor_scalar(fl[:, 0, :], pt, float(NT - 1), None, ALU.min))
                link(dve.tensor_copy(s.tile_of[k][:, :], fl[0:1, 0, :]))
                link(dve.tensor_scalar(fl[:, 1, :], iotaj[:, :], float(P), None, ALU.mult))
                link(dve.tensor_tensor(fl[:, 1, :], fl[:, 1, :], pst, ALU.add))
                link(dve.tensor_scalar(fl[:, 1, :], fl[:, 1, :], float(E), None, ALU.min))
                link(dve.tensor_copy(s.start_of[k][:, :], fl[0:1, 1, :]))


def stage_count_project(nc, s, io):
    K = EC // NT
    BY_ACT = range(2, K, 3)
    A = len(BY_ACT)
    with ExitStack() as ctx:
        sb, pb, sem = makers(nc, ctx, "count")
        hist = [pb(f"hist{k}", [P, 512], F32) for k in range(2)]
        ps = pb("proj", [P, 512], F32)
        Lr = [sb(f"Lr{k}", [EP, K, P], BF16) for k in range(2)]
        Hr = [sb(f"Hr{k}", [EP, K, NT], BF16) for k in range(2)]
        zero = sb("zero", [EP, P], BF16)
        xT = s.scores_or_h[:, 0:2 * NPAD].rearrange("p (a n) -> p a n", a=2)
        W = sb("Wqkv", [P, 2, 512], F32)
        b = sb("bqkv", [1, 512], F32)
        xt = sb("x_tile", [P, 2, P], F32)
        full = sb("full", [P, 512], F32)
        rest = sb("rest", [P, 512], F32)
        counted = [sem(f"counted{k}") for k in range(2)]
        lo_made = [sem(f"lo_made{k}") for k in range(2)]
        hi_made = [sem(f"hi_made{k}") for k in range(2)]
        minus = sb("minus_lo", [EP, EC], F32)
        off = sb("off", [EP, A, P], F32)
        negated, off_made, act_made = sem("negated"), sem("off_made"), sem("act_made")
        zeroed, ended, kept, loads = sem("zeroed"), sem("ended"), sem("kept"), sem("loads")
        made, scaled, copied, x_cut = sem("made"), sem("scaled"), sem("copied"), sem("x_cut")
        wa_in = sem("wa_in")
        top, mid, sub1, sub2 = sem("top"), sem("mid"), sem("sub1"), sem("sub2")
        with nc.Block() as block:
            @block.sync
            def _(sp):
                for a in range(2):
                    sp.dma_start(xT[:, a, 0:N], io["xT"][a * P:(a + 1) * P, :]).then_inc(loads, 16)
                    w = io["Wqkv"][a * P:(a + 1) * P, :]
                    sp.dma_start(W[:, a, 0:DIM], w[:, 2 * DH:]).then_inc(loads, 16)
                    sp.dma_start(W[:, a, DIM:DIM + DH], w[:, DH:2 * DH]).then_inc(loads, 16)
                    sp.dma_start(W[:, a, DIM + DH:], w[:, 0:DH]).then_inc(loads, 16)
                sp.dma_start(b[:, 0:DIM], io["bqkv"][:, 2 * DH:]).then_inc(loads, 16)
                sp.dma_start(b[:, DIM:DIM + DH], io["bqkv"][:, DH:2 * DH]).then_inc(loads, 16)
                sp.dma_start(b[:, DIM + DH:], io["bqkv"][:, 0:DH]).then_inc(loads, 16)
                sp.wait_ge(zeroed, 3)
                for a in range(6):
                    for c, name in enumerate("qk"):
                        cols = slice(c * DH, (c + 1) * DH)
                        sp.dma_start(s.Wa[a * RA:a * RA + RP, cols], io[f"W{name}_rpe"]).then_inc(wa_in, 16)
                        sp.dma_start(s.Wa[a * RA + RP:(a + 1) * RA, cols], io[f"b{name}_rpe"]).then_inc(wa_in, 16)
                for a in range(3):
                    c = 2 * DH
                    sp.dma_start(s.Wa[a:a + 1, c:c + 2 * DIM], io["b_ih"][:, 0:2 * DIM]).then_inc(wa_in, 16)
                    sp.dma_start(s.Wa[a:a + 1, c + 3 * DIM:c + 4 * DIM], io["b_ih"][:, 2 * DIM:]).then_inc(wa_in, 16)
                    sp.dma_start(s.Wa[3 + a:4 + a, c:c + 3 * DIM], io["b_hh"]).then_inc(wa_in, 16)
                sp.wait_ge(wa_in, 16 * 33)

            @block.vector
            def _(dve):
                dve.memset(zero[:, :], 0.0).then_inc(zeroed, 1)
                dve.memset(xT[:, :, N:NPAD], 0.0).then_inc(zeroed, 1)
                dve.memset(s.Wa[:, :], 0.0).then_inc(zeroed, 1)
                dve.tensor_scalar(minus[:, :], s.lo[1][:, :], -1.0, None, ALU.mult).then_inc(negated, 1)
                dve.sem_inc(made, 1)
                dve.wait_ge(loads, 16 * 11)
                dve.wait_ge(zeroed, 2)
                with dve.Fori(0, NT) as t:
                    i = dve.snap(t * K)
                    dve.wait_ge(made, t + 1)
                    dve.tensor_copy(xt[:, :, :], xT[:, :, bass.ds(t * P, P)]).then_inc(x_cut, 1)
                    for k in range(2):
                        dve.wait_ge(counted[k], i + K)
                        dve.tensor_tensor(Hr[k][:, :, :], s.iota[0:EP, None, 0:NT].to_broadcast([EP, K, NT]),
                                          s.hi[k][:, bass.ds(i, K), None].to_broadcast([EP, K, NT]),
                                          ALU.is_equal).then_inc(hi_made[k], K)
                        for q in (q for q in range(K) if k == 0 or q not in BY_ACT):
                            dve.tensor_scalar(Lr[k][:, q, :], s.iota_b[0:EP, :], s.lo[k][:, bass.ds(i + q, 1)], None,
                                              ALU.is_equal).then_inc(lo_made[k], 1)
                dve.wait_ge(ended, 1)
                for k in range(2):
                    dve.tensor_copy(s.count[k][:, :], hist[k][0:NT, 0:P]).then_inc(kept, 1)

            @block.tensor
            def _(pe):
                pe.wait_ge(zeroed, 2)
                for k in range(2):
                    pe.matmul(hist[k][0:NT, 0:P], zero[:, 0:NT], zero[:, :], start=True, stop=False, skip_group_check=True)
                    pe.sem_inc(counted[k], K)
                pe.wait_ge(loads, 16 * 11)
                with pe.Fori(0, NT) as t:
                    pe.wait_ge(copied, t + 1)
                    pe.wait_ge(scaled, t + 1)
                    pe.wait_ge(x_cut, t + 1)
                    for a in range(2):
                        pe.matmul(ps[:, :], xt[:, a, :], W[:, a, :], start=(a == 0), stop=False,
                                  skip_group_check=True)
                    pe.matmul(ps[:, :], s.ones[0:1, :], b[:, :], start=False, stop=True,
                              skip_group_check=True).then_inc(made, 1)
                    i = pe.snap(t * K)
                    for k in range(2):
                        pe.wait_ge(hi_made[k], i + K)
                        for q in range(K):
                            acts = sum(a < q for a in BY_ACT)
                            if k == 0:
                                pe.wait_ge(lo_made[k], i + q + 1)
                            elif q in BY_ACT:
                                pe.wait_ge(act_made, t * A + acts + 2)
                            else:
                                pe.wait_ge(lo_made[k], t * (K - A) + q - acts + 1)
                            pe.matmul(hist[k][0:NT, 0:P], Hr[k][:, q, :], Lr[k][:, q, :], start=False, stop=False,
                                      skip_group_check=True).then_inc(counted[k], 1)
                pe.matmul(hist[1][0:NT, 0:P], zero[:, 0:NT], zero[:, :], start=False, stop=True,
                          skip_group_check=True).then_inc(ended, 1)

            @block.scalar
            def _(act):
                act.sem_inc(copied, 1)
                act.sem_inc(scaled, 1)
                act.sem_inc(act_made, 1)
                act.wait_ge(negated, 1)
                with act.Fori(0, NT) as t:
                    act.wait_ge(act_made, t * A + 1)
                    for a, q in enumerate(BY_ACT):
                        act.activation(off[:, a, :], s.iota[0:EP, :], ACT.Square,
                                       bias=minus[:, bass.ds(t * K + q, 1)]).then_inc(off_made, 1)
                    for a, q in enumerate(BY_ACT):
                        act.wait_ge(off_made, t * A + a + 1)
                        act.wait_ge(counted[1], t * K + q + 1)
                        act.activation(Lr[1][:, q, :], off[:, a, :], ACT.Relu, bias=s.ones[0:EP, 0:1],
                                       scale=-1.0).then_inc(act_made, 1)
                    act.wait_ge(made, t + 2)
                    act.wait_ge(sub1, t + 1)
                    act.activation(full[:, 0:384], ps[:, 0:384], ACT.Copy).then_inc(copied, 1)
                    act.activation(full[:, 384:512], ps[:, 384:512], ACT.Copy, scale=SCALE).then_inc(scaled, 1)
                    act.wait_ge(copied, t + 2)
                    act.wait_ge(scaled, t + 2)
                    act.activation(s.tab[:, bass.ds(t, 1), 0, :], full[:, None, :], ACT.Copy).then_inc(top, 1)
                    act.wait_ge(sub1, t + 2)
                    act.activation(s.tab[:, bass.ds(t, 1), 1, :], rest[:, None, :], ACT.Copy).then_inc(mid, 1)

            @block.gpsimd
            def _(pool):
                pool.sem_inc(sub1, 1)
                pool.sem_inc(sub2, 1)
                with pool.Fori(0, NT) as t:
                    pool.wait_ge(top, t + 1)
                    pool.wait_ge(sub2, t + 1)
                    pool.tensor_tensor(rest[:, None, :], full[:, None, :], s.tab[:, bass.ds(t, 1), 0, :], ALU.subtract).then_inc(sub1, 1)
                    pool.wait_ge(mid, t + 1)
                    pool.tensor_tensor(s.tab[:, bass.ds(t, 1), 2, :], rest[:, None, :], s.tab[:, bass.ds(t, 1), 1, :],
                                       ALU.subtract).then_inc(sub2, 1)


def stage_rank(nc, s, io, k, flag=None):
    keyT = io[("srcT", "dstT")[k]]
    AHEAD = 4
    with ExitStack() as ctx:
        sb, pb, sem = makers(nc, ctx, f"rank{k}")
        hist = pb("hist", [P, 512], F32)
        look = [pb(f"look{a}", [P, 512], F32) for a in range(4)]
        Lr = sb("Lr", [EP, TWO, P], BF16)
        Hr = sb("Hr", [EP, 2, G, NT], BF16)
        same = sb("same", [EP, G, EP], BF16)
        cut = lambda a, p: s.scores_or_h[0:p, a * TWO * EP:(a + 1) * TWO * EP]
        keyb = cut(0, P).bitcast(I32).rearrange("p (a g e) -> p a g e", a=2, g=G)
        hib = cut(1, 32).rearrange("p (a g e) -> p a g e", a=2, g=G)
        off = sb("off", [NT, 2, EP], F32)
        HT = sb("HT", [NT, 2, G, EP], F32)
        snap = sb("snap", [NT, G, P], F32)
        junk = sb("junk", [EP, 2, P], F32)
        key_in = [sem(f"key_in{a}") for a in range(2)]
        hi_in = [sem(f"hi_in{a}") for a in range(2)]
        lo_made, hi_made, counted, primed = sem("lo_made"), sem("hi_made"), sem("counted"), sem("primed")
        off_made, hT_made, snapped, looked, ranked = sem("off_made"), sem("hT_made"), sem("snapped"), sem("looked"), sem("ranked")
        compared = sem("compared")
        with nc.Block() as block:
            @block.sync
            def _(sp):
                with when(sp, flag):
                    with chunks(sp, EC, TWO) as i:
                        for half in range(2):
                            g = i + half * G
                            sp.wait_ge(compared, g + G)
                            sp.dma_start(keyb[:, half, :, :], keyT[None, bass.ds(g, G), :].to_broadcast([P, G, EP])).then_inc(key_in[half], 16)
                            sp.wait_ge(hT_made, g + G)
                            sp.dma_start(hib[:, half, :, :], s.hiT2[k][None, bass.ds(g, G), :].to_broadcast([32, G, EP])).then_inc(hi_in[half], 16)

            @block.scalar
            def _(act):
                def distances(g, half, q):
                    act.wait_ge(hT_made, g + q + TWO)
                    act.activation(off[:, :, :], hib[0:NT, half, q:q + 2, :], ACT.Square,
                                   bias=s.negp[0:NT, :]).then_inc(off_made, 2)

                def tile_onehots(g, half, q):
                    act.wait_ge(off_made, g + q + 2)
                    act.wait_ge(looked, g + q + 2)
                    act.activation(HT[:, half, q:q + 2, :], off[:, :, :], ACT.Relu, bias=s.ones[0:NT, 0:1],
                                   scale=-1.0).then_inc(hT_made, 2)

                def counts(g, q):
                    act.wait_ge(counted, g + q + TWO)
                    act.wait_ge(looked, g + q + 1 + G)
                    act.activation(snap[:, q, :], hist[0:NT, 0:P], ACT.Copy).then_inc(snapped, 1)

                def two_groups(i, more):
                    for half in range(2):
                        g = i + half * G
                        for q in range(0, G, 2):
                            ahead = (g, half, q + 2) if q + 2 < G else (g + G, 1 - half, 0)
                            ahead = ahead if q + 2 < G or half == 0 or more else None
                            counts(g, q)
                            if ahead:
                                if q + 2 == G:
                                    act.wait_ge(hi_in[1 - half], i + 16 + 16 * half)
                                distances(*ahead)
                            counts(g, q + 1)
                            if ahead:
                                tile_onehots(*ahead)

                with when(act, flag):
                    act.sem_inc(hT_made, TWO)
                    act.wait_ge(primed, 1)
                    act.wait_ge(hi_in[0], 16)
                    distances(0, 0, 0)
                    tile_onehots(0, 0, 0)
                    with chunks(act, EC - TWO, TWO) as i:
                        two_groups(i, True)
                    two_groups(EC - TWO, False)

            @block.tensor
            def _(pe):
                with when(pe, flag):
                    pe.matmul(hist[0:NT, 0:P], s.ident[0:NT, 0:NT], s.start[k][:, :], start=True, stop=False,
                              skip_group_check=True).then_inc(primed, 1)
                    pe.sem_inc(looked, TWO)
                    with chunks(pe, EC, TWO) as i:
                        for half in range(2):
                            g = i + half * G
                            for q in range(G):
                                pe.wait_ge(snapped, g + q + 1)
                                if q == 0:
                                    pe.wait_ge(hi_made, g + G)
                                pe.wait_ge(lo_made, g + q + 1)
                                pe.matmul(hist[0:NT, 0:P], Hr[:, half, q, :], Lr[:, half * G + q, :], start=False, stop=False,
                                          skip_group_check=True).then_inc(counted, 1)
                                pe.wait_ge(hT_made, g + q // 2 * 2 + 2 + TWO)
                                pe.wait_ge(ranked, g + q + 1)
                                pe.matmul(look[q % 4][0:EP, 0:P], HT[:, half, q, :], snap[:, q, :], start=True,
                                          stop=False, skip_group_check=True)
                                pe.wait_ge(compared, g + q + 1 + TWO)
                                pe.matmul(look[q % 4][0:EP, 0:P], same[:, q, :], Lr[:, half * G + q, :], start=False,
                                          stop=True, skip_group_check=True).then_inc(looked, 1)

            @block.vector
            def _(dve):
                def tiles(g, half):
                    dve.wait_ge(looked, g + G)
                    dve.tensor_tensor(Hr[:, half, :, :], s.iota[0:EP, None, 0:NT].to_broadcast([EP, G, NT]),
                                      s.hi[k][:, bass.ds(g, G), None].to_broadcast([EP, G, NT]),
                                      ALU.is_equal).then_inc(hi_made, G)

                def prepare(g, half, q):
                    dve.wait_ge(looked, g + q + 1 + G)
                    dve.tensor_scalar(Lr[:, half * G + q, :], s.iota_b[0:EP, :], s.lo[k][:, bass.ds(g + q, 1)], None,
                                      ALU.is_equal).then_inc(lo_made, 1)
                    dve.scalar_tensor_tensor(out=same[:, q, :], in0=keyb[0:EP, half, q, :],
                                             scalar=s.key[k][:, bass.ds(g + q, 1)], in1=s.after[0:EP, 0:EP],
                                             op0=ALU.is_equal, op1=ALU.mult).then_inc(compared, 1)

                def two_groups(i, more):
                    for half in range(2):
                        g = i + half * G
                        for q in range(G):
                            if q + AHEAD < G:
                                prepare(g, half, q + AHEAD)
                            elif half == 0 or more:
                                if q + AHEAD == G:
                                    tiles(g + G, 1 - half)
                                    dve.wait_ge(key_in[1 - half], i + 16 + 16 * half)
                                prepare(g + G, 1 - half, q + AHEAD - G)
                            dve.wait_ge(looked, g + q + 1 + TWO)
                            dve.wait_ge(ranked, g + q + 3)
                            dve.scalar_tensor_tensor(out=junk[:, q % 2, :], in0=s.iota[0:EP, :],
                                                     scalar=s.lo[k][:, bass.ds(g + q, 1)],
                                                     in1=look[q % 4][0:EP, 0:P],
                                                     op0=ALU.is_equal, op1=ALU.mult,
                                                     accum_out=s.place[:, bass.ds(g + q, 1)]).then_inc(ranked, 1)

                with when(dve, flag):
                    dve.sem_inc(counted, TWO)
                    dve.sem_inc(compared, TWO)
                    dve.sem_inc(ranked, 4)
                    tiles(0, 0)
                    dve.wait_ge(key_in[0], 16)
                    for q in range(AHEAD):
                        prepare(0, 0, q)
                    with chunks(dve, EC - TWO, TWO) as i:
                        two_groups(i, True)
                    two_groups(EC - TWO, False)
                    if k == 0:
                        dve.wait_ge(ranked, EC + 4)
                        dve.tensor_copy(s.rec[:, :, C_RANK], s.place[:, :]).then_inc(ranked, 1)


def stage_sort_records(nc, s, flag):
    with ExitStack() as ctx:
        sb, pb, sem = makers(nc, ctx, "sort_records")
        out = [sb(f"rec_out{q}", [EP, REC], F32) for q in range(G)]
        at = sb("rec_at", [EP, G], I32)
        copied, idx_copied = sem("copied"), sem("idx_copied")
        scattered = [sem(f"rec_scattered{q}") for q in range(G)]
        with nc.Block() as block:
            @block.vector
            def _(dve):
                with when(dve, flag):
                    with chunks(dve, EC, G) as i:
                        for q in range(G):
                            dve.wait_ge(scattered[q], i * 2 + 16)
                            dve.tensor_copy(out[q][:, :], s.rec[:, bass.ds(i + q, 1), :]).then_inc(copied, 1)
                            dve.tensor_copy(at[:, q:q + 1], s.place[:, bass.ds(i + q, 1)]).then_inc(idx_copied, 1)

            @block.gpsimd
            def _(pool):
                with when(pool, flag):
                    for q in range(G):
                        pool.dma_start(out[q][:, :], s.recs[E:E + EP, :]).then_inc(scattered[q], 16)
                    with chunks(pool, EC, G) as i:
                        for q in range(G):
                            pool.wait_ge(copied, i + q + 1)
                            pool.wait_ge(idx_copied, i + q + 1)
                            pool.sem_inc(s.pool_passed, 1)
                            pool.indirect_dma_start(
                                out=s.recs, out_offset=bass.IndirectOffsetOnAxis(ap=at[:, q:q + 1], axis=0),
                                in_=out[q][:, :], in_offset=None).then_inc(scattered[q], 16)
                    for q in range(G):
                        pool.wait_ge(scattered[q], 16 * (EC // G) + 16)


def stage_store_records(nc, s, flag):
    with ExitStack() as ctx:
        sb, pb, sem = makers(nc, ctx, "store_records")
        stored = sem("stored")
        with nc.Block() as block:
            @block.sync
            def _(sp):
                with when(sp, flag):
                    sp.dma_start(s.recs[0:E, :].rearrange("(p c) k -> p (c k)", p=EP),
                                 s.rec[:, :, :].rearrange("p c k -> p (c k)")).then_inc(stored, 16)
                    sp.wait_ge(stored, 16)


def stage_rows(nc, s):
    with ExitStack() as ctx:
        sb, pb, sem = makers(nc, ctx, "rows")
        psT = [pb(f"psT{a}", [P, 2 * 512], BF16) for a in range(2)]
        psV = [pb(f"psV{a}", [P, 512], F32) for a in range(4)]
        rec = sb("rec_in", [P, 2, G, REC], F32)
        row = [sb(f"row{q}", [P, ROW], F32) for q in range(G)]
        idx = sb("idx", [P, 2, G], I32)
        low = sb("low", [P, 2, G], F32)
        valid = sb("valid", [P, 2, G], F32)
        idxf = sb("idxf", [P, 2, G], F32)
        oh = sb("oh", [P, G, P], BF16)
        ohT = sb("ohT", [P, G, P], BF16)
        rec_in = [sem(f"rec_in{a}") for a in range(2)]
        rec_free, rel_made, low_made = sem("rec_free"), sem("rel_made"), sem("low_made")
        valid_made, idxf_made, idx_made, src_kept = sem("valid_made"), sem("idxf_made"), sem("idx_made"), sem("src_kept")
        type_kept = sem("type_kept")
        oh_made, turned, ohT_made, fetched, evicted = sem("oh_made"), sem("turned"), sem("ohT_made"), sem("fetched"), sem("evicted")
        scattered = [sem(f"row_scattered{q}") for q in range(G)]
        with nc.Block() as block:
            @block.sync
            def _(sp):
                first = [sp.alloc_register(f"rows_first{q}") for q in range(G)]
                with chunks(sp, J, TWO) as i:
                    for half in range(2):
                        g = i + half * G
                        sp.load(first, s.start_of[1][0:1, bass.ds(g, G)])
                        sp.wait_ge(rec_free, g + G)
                        for q in range(G):
                            at = sp.snap(first[q], min_val=0, max_val=E)
                            sp.dma_start(rec[:, half, q, :], s.recs[bass.ds(at, P), :]).then_inc(rec_in[half], 16)

            @block.vector
            def _(dve):
                dve.sem_inc(rec_free, TWO)
                with chunks(dve, J, TWO) as i:
                    for half in range(2):
                        g = i + half * G
                        dve.wait_ge(rec_in[half], i * G + 16 * G)
                        dve.tensor_tensor(s.relD[:, bass.ds(g, G)], rec[:, half, :, C_DST], s.base[1][:, bass.ds(g, G)],
                                          ALU.subtract).then_inc(rel_made, G)
                        dve.tensor_scalar(s.src_of[:, bass.ds(g, G)], rec[:, half, :, C_SRC], 0.0, None,
                                          ALU.max).then_inc(src_kept, 1)
                        dve.tensor_copy(s.type_of[:, bass.ds(g, G)], rec[:, half, :, C_TYPE]).then_inc(type_kept, 1)
                        dve.wait_ge(rel_made, g + G)
                        dve.tensor_scalar(low[:, half, :], s.relD[:, bass.ds(g, G)], 0.0, None, ALU.is_ge).then_inc(low_made, G)
                        dve.wait_ge(low_made, g + G)
                        dve.scalar_tensor_tensor(out=valid[:, half, :], in0=s.relD[:, bass.ds(g, G)], scalar=P - 1.0,
                                                 in1=low[:, half, :], op0=ALU.is_le, op1=ALU.mult).then_inc(valid_made, G)
                        dve.wait_ge(valid_made, g + G)
                        dve.scalar_tensor_tensor(out=idxf[:, half, :], in0=rec[:, half, :, C_RANK], scalar=-SKIP,
                                                 in1=valid[:, half, :], op0=ALU.add, op1=ALU.mult).then_inc(idxf_made, G)
                        dve.wait_ge(idxf_made, g + G)
                        dve.tensor_scalar(idx[:, half, :], idxf[:, half, :], SKIP, None, ALU.add).then_inc(idx_made, G)
                        for q in range(G):
                            dve.wait_ge(turned, g + q + 1)
                            dve.tensor_scalar(oh[:, q, :], s.iota_b[:, :], s.relD[:, bass.ds(g + q, 1)], None,
                                              ALU.is_equal).then_inc(oh_made, 1)
                            dve.wait_ge(scattered[q], i * 2 + 16 * half + 16)
                            dve.tensor_copy(row[q][:, DIM + DH:ROW], rec[:, half, q, :]).then_inc(rec_free, 1)

            @block.tensor
            def _(pe):
                tile = [pe.alloc_register(f"rows_tile{q}") for q in range(G)]
                pe.sem_inc(turned, G)
                with chunks(pe, J, TWO) as i:
                    for half in range(2):
                        g = i + half * G
                        pe.load(tile, s.tile_of[1][0:1, bass.ds(g, G)])

                        def turn(q):
                            pe.wait_ge(oh_made, g + q + 1)
                            pe.wait_ge(ohT_made, g + q + G - 1)
                            pe.transpose(psT[q % 2][:, 0:P], oh[:, q, :], s.ident_b[:, :]).then_inc(turned, 1)

                        turn(0)
                        for q in range(G):
                            if q + 1 < G:
                                turn(q + 1)
                            pe.wait_ge(ohT_made, g + q + 1 + G)
                            pe.wait_ge(evicted, g + q + 1)
                            t = pe.snap(tile[q], min_val=0, max_val=NT - 1)
                            for a in range(3):
                                last = pe.matmul(psV[q % 4][:, 0:DIM + DH], ohT[:, q, :],
                                                 s.tab[:, bass.ds(t, 1), a, 0:DIM + DH], start=(a == 0), stop=(a == 2))
                            last.then_inc(fetched, 1)

            @block.scalar
            def _(act):
                act.sem_inc(ohT_made, G)
                act.sem_inc(evicted, 4)
                with chunks(act, J, TWO) as i:
                    for half in range(2):
                        g = i + half * G

                        def turned_copy(q):
                            act.wait_ge(turned, g + q + 1 + G)
                            act.activation(ohT[:, q, :], psT[q % 2][:, 0:P], ACT.Copy).then_inc(ohT_made, 1)

                        turned_copy(0)
                        for q in range(G):
                            if q + 1 < G:
                                turned_copy(q + 1)
                            act.wait_ge(fetched, g + q + 1)
                            act.wait_ge(scattered[q], i * 2 + 16 * half + 16)
                            act.activation(row[q][:, 0:DIM + DH], psV[q % 4][:, 0:DIM + DH], ACT.Copy).then_inc(evicted, 1)

            @block.gpsimd
            def _(pool):
                for q in range(G):
                    pool.dma_start(row[q][:, :], s.rows[E:EPAD, :]).then_inc(scattered[q], 16)
                with chunks(pool, J, TWO) as i:
                    for half in range(2):
                        g = i + half * G
                        pool.wait_ge(idx_made, g + G)
                        pool.sem_inc(s.pool_passed, 1)
                        for q in range(G):
                            pool.wait_ge(evicted, g + q + 1 + 4)
                            pool.wait_ge(rec_free, g + q + 1 + TWO)
                            pool.sem_inc(s.pool_passed, 1)
                            pool.indirect_dma_start(
                                out=s.rows, out_offset=bass.IndirectOffsetOnAxis(ap=idx[:, half, q:q + 1], axis=0),
                                in_=row[q][:, :], in_offset=None, bounds_check=E - 1,
                                oob_is_err=False).then_inc(scattered[q], 16)
                for q in range(G):
                    pool.wait_ge(scattered[q], 16 * (J // G) + 16)


def stage_scores(nc, s, io):
    AHEAD = 2
    with ExitStack() as ctx:
        sb, pb, sem = makers(nc, ctx, "scores")
        psT = [pb(f"psT{a}", [P, 2 * 512], BF16) for a in range(4)]
        psQ = [pb(f"psQ{a}", [P, 512], F32) for a in range(4)]
        km = sb("km", [P, 4, G, KM], F32)
        oh = sb("oh", [P, 2, G, P], BF16)
        A6 = sb("A6", [P, 4, G, P], BF16)
        rest = sb("rest", [P, G, RA], F32)
        turnedT = sb("turnedT", [P, G, 2 * P], BF16)
        ke = sb("ke", [P, 2, 2, DH], F32)
        prod = sb("prod", [P, 2, G, DH], F32)
        km_in = [sem(f"km_in{a}") for a in range(4)]
        rel_made, cut_hi, cut_rest, cut_mid, cut_lo, cut_mids, cut = (
            sem(n) for n in ("rel_made", "cut_hi", "cut_rest", "cut_mid", "cut_lo", "cut_mids", "cut"))
        oh_made, turned, copied, fetched, keyed = sem("oh_made"), sem("turned"), sem("copied"), sem("fetched"), sem("keyed")
        multiplied, summed, cleared = sem("multiplied"), sem("summed"), sem("cleared")
        with nc.Block() as block:
            @block.sync
            def _(sp):
                first = [sp.alloc_register(f"score_first{q}") for q in range(FOUR)]
                with chunks(sp, J, FOUR) as i:
                    sp.load(first, s.start_of[0][0:1, bass.ds(i, FOUR)])
                    for group in range(4):
                        g, half = i + group * G, group % 2
                        sp.wait_ge(keyed, g + G)
                        for q in range(G):
                            at = sp.snap(first[group * G + q], min_val=0, max_val=E)
                            sp.dma_start(km[:, group, q, :], s.rows[bass.ds(at, P), DIM:ROW]).then_inc(km_in[group], 16)

            @block.gpsimd
            def _(pool):
                pool.memset(A6[:, :, :, :], 0.0).then_inc(cleared, 1)
                pool.wait_ge(cleared, 1)
                with chunks(pool, J, FOUR) as i:
                    for group in range(4):
                        g, half = i + group * G, group % 2
                        attr = km[:, group, :, DH:DH + RA]
                        part = lambda a, n=1: A6[:, group, :, a * RA:(a + n) * RA]
                        pool.wait_ge(km_in[group], i * 4 + 16 * G)
                        pool.tensor_tensor(s.relS[:, bass.ds(g, G)], km[:, group, :, DH + C_SRC],
                                           s.base[0][:, bass.ds(g, G)], ALU.subtract).then_inc(rel_made, G)
                        pool.wait_ge(turned, g + G)
                        pool.sem_inc(s.pool_passed, 1)
                        pool.tensor_copy(part(0), attr).then_inc(cut_hi, G)
                        pool.wait_ge(cut_hi, g + G)
                        pool.tensor_tensor(rest[:, :, :], attr, part(0), ALU.subtract).then_inc(cut_rest, G)
                        pool.wait_ge(cut_rest, g + G)
                        pool.sem_inc(s.pool_passed, 1)
                        pool.tensor_copy(part(1), rest[:, :, :]).then_inc(cut_mid, G)
                        pool.wait_ge(cut_mid, g + G)
                        pool.tensor_tensor(part(2), rest[:, :, :], part(1), ALU.subtract).then_inc(cut_lo, G)
                        pool.tensor_copy(part(3, 2), part(0, 2)).then_inc(cut_mids, G)
                        pool.tensor_copy(part(5), part(0)).then_inc(cut, G)
                pool.memset(s.relS[:, J:J + G], -1.0).then_inc(rel_made, G)
                pool.wait_ge(cut_lo, J)
                pool.memset(rest[:, :, :], 0.0).then_inc(cut, G)

            @block.vector
            def _(dve):
                dve.sem_inc(keyed, FOUR)
                dve.sem_inc(multiplied, G)

                def onehot(n, slot, q):
                    dve.wait_ge(turned, n + q + 1 + TWO)
                    dve.tensor_scalar(oh[:, slot, q, :], s.iota_b[:, :], s.relS[:, bass.ds(n + q, 1)], None,
                                      ALU.is_equal).then_inc(oh_made, 1)

                dve.wait_ge(rel_made, G)
                for q in range(G):
                    onehot(0, 0, q)
                with chunks(dve, J, FOUR) as i:
                    for group in range(4):
                        g, half = i + group * G, group % 2
                        dve.wait_ge(rel_made, g + 2 * G)
                        for q in range(0, G, 2):
                            two = psQ[q // 2][:, :].rearrange("p (c x) -> p c x", c=2)
                            b = q // 2 % 2
                            dve.wait_ge(fetched, g + q + 2 + G)
                            dve.wait_ge(multiplied, g + q + G - 2)
                            dve.tensor_tensor(ke[:, b, :, :], two[:, :, DH:], km[:, group, q:q + 2, 0:DH],
                                              ALU.add).then_inc(keyed, 2)
                            for a in range(2):
                                onehot(g + G, 1 - half, q + a)
                            dve.wait_ge(keyed, g + q + 2 + FOUR)
                            dve.tensor_tensor(prod[:, half, q:q + 2, :], two[:, :, 0:DH], ke[:, b, :, :],
                                              ALU.mult).then_inc(multiplied, 2)
                        dve.wait_ge(multiplied, g + 2 * G)
                        dve.tensor_reduce(s.score[:, bass.ds(g, G), :],
                                          prod[:, half, :, :].rearrange("p g (h d) -> p g h d", d=D),
                                          AX_X, ALU.add).then_inc(summed, 1)

            @block.tensor
            def _(pe):
                tile = [pe.alloc_register(f"score_tile{q}") for q in range(FOUR)]
                pe.sem_inc(turned, FOUR)
                pe.sem_inc(fetched, G)

                def turn(n, group, q):
                    pe.wait_ge(oh_made, n + q + 1)
                    pe.wait_ge(cut, n + G)
                    pe.wait_ge(copied, n + q + 1)
                    pe.transpose(psT[q % 4][:, 0:P], oh[:, group % 2, q, :], s.ident_b[:, :])
                    pe.transpose(psT[q % 4][:, P:2 * P], A6[:, group, q, :], s.ident_b[:, :]).then_inc(turned, 1)

                for q in range(AHEAD):
                    turn(0, 0, q)
                with chunks(pe, J, FOUR) as i:
                    pe.load(tile, s.tile_of[0][0:1, bass.ds(i, FOUR)])
                    for group in range(4):
                        g, half = i + group * G, group % 2
                        for q in range(G):
                            if q + AHEAD < G:
                                turn(g, group, q + AHEAD)
                            else:
                                turn(g + G, (group + 1) % 4, q + AHEAD - G)
                            pe.wait_ge(copied, g + q + 1 + 4)
                            pe.wait_ge(multiplied, g + q // 2 * 2 + 2)
                            at = q % 2 * 2 * DH
                            pe.matmul(psQ[q // 2][:, at:at + 2 * DH], turnedT[:, q, P:2 * P], s.parts[:, 0:2 * DH], start=True,
                                      stop=False, skip_group_check=True)
                            t = pe.snap(tile[group * G + q], min_val=0, max_val=NT - 1)
                            for a in range(3):
                                last = pe.matmul(psQ[q // 2][:, at:at + DH], turnedT[:, q, 0:P],
                                                 s.tab[:, bass.ds(t, 1), a, DIM + DH:], start=False, stop=(a == 2),
                                                 skip_group_check=True)
                            last.then_inc(fetched, 1)

            @block.scalar
            def _(act):
                act.sem_inc(copied, 4)
                with chunks(act, J, G) as g:
                    for q in range(G):
                        act.wait_ge(turned, g + q + 1 + FOUR)
                        act.wait_ge(fetched, g + q + 1)
                        act.activation(turnedT[:, q, :], psT[q % 4][:, 0:2 * P], ACT.Copy).then_inc(copied, 1)


NG = J // G


def stage_softmax(nc, s):
    L = NG * P
    QUAD = 4
    with ExitStack() as ctx:
        sb, pb, sem = makers(nc, ctx, "softmax")
        ps = [pb(f"sm_ps{a}", [P, 512], F32) for a in range(6)]
        sc = sb("sc", [P, L], F32)
        mx = sb("mx", [P, L], F32)
        pen = sb("pen", [P, L + 1], F32)
        key = sb("keyrow", [P, L + 1], F32)
        quad_row = sb("quad_row", [P, 2, QUAD * P], F32)
        blk = sb("blk", [P, G], F32)
        head = sb("head", [P, H], F32)
        headT = sb("headT", [H, P], F32)
        less = sb("less", [P, J], F32)
        by_row = sb("by_row", [P, NG, G, H], F32)
        pi = sb("pi", [P, 2], I32)
        pf = sb("pf", [P, 2], F32)
        edge = sb("edge", [P, 3], F32)
        wide = sb("wide", [P, 3 * G], F32)
        small = sb("small", [H, 3 * G], F32)
        carry = sb("carry", [H, G + 1], F32)
        back = sb("back", [P, G], F32)
        carried = sb("carried", [P, 2], F32)
        step, handed, pe_step, masked, key_rows = sem("step"), sem("handed"), sem("pe_step"), sem("masked"), sem("key_rows")
        sc_turned, sc_evicted, exps, ex_turned, ex_evicted = sem("sc_turned"), sem("sc_evicted"), sem("exps"), sem("ex_turned"), sem("ex_evicted")
        key_turned, key_evicted = sem("key_turned"), sem("key_evicted")
        score_v = s.score[:, :, :].rearrange("p (b g) h -> p b g h", g=NG)
        less_v = less[:, :].rearrange("p (b g) -> p b g", g=NG)
        key_v = s.src_key[:, :].rearrange("p (b g) -> p b g", g=NG)
        with nc.Block() as block:
            @block.vector
            def _(dve):
                n = [0, 0]

                def link(ins):
                    n[0] += 1
                    ins.then_inc(step, 1)
                    dve.wait_ge(step, n[0])

                def hand(ins):
                    n[1] += 1
                    ins.then_inc(handed, 1)
                    dve.wait_ge(handed, n[1])

                link(dve.tensor_scalar(less[:, :], s.relS[:, 0:J], 0.0, None, ALU.is_ge))
                link(dve.scalar_tensor_tensor(out=s.validS[:, :], in0=s.relS[:, 0:J], scalar=P - 1.0, in1=less[:, :],
                                              op0=ALU.is_le, op1=ALU.mult))
                link(dve.tensor_tensor(s.src_key[:, :], s.relS[:, 0:J], s.base[0][:, :], ALU.add))
                link(dve.tensor_scalar(less[:, :], s.validS[:, :], 1.0, BIG, ALU.subtract, ALU.mult))
                for b in range(G):
                    dve.tensor_tensor(by_row[:, :, b, :], score_v[:, b, :, :],
                                      less_v[:, b, :, None].to_broadcast([P, NG, H]), ALU.add).then_inc(masked, 1)
                link(dve.tensor_copy(pi[:, 0:1], s.pcol[:, :]))
                link(dve.tensor_scalar(pi[:, 1:2], pi[:, 0:1], H - 1, None, ALU.bitwise_and))
                link(dve.tensor_copy(pf[:, 1:2], pi[:, 1:2]))
                link(dve.tensor_tensor(pf[:, 0:1], s.pcol[:, :], pf[:, 1:2], ALU.subtract))
                link(dve.tensor_scalar(head[:, :], s.iota[:, 0:H], pf[:, 1:2], None, ALU.is_equal))
                link(dve.tensor_scalar(blk[:, :], s.iota[:, 0:G], float(H), None, ALU.mult))
                link(dve.tensor_scalar(blk[:, :], blk[:, :], pf[:, 0:1], None, ALU.is_equal))
                for r in range(NG // QUAD):
                    if r >= 2:
                        dve.wait_ge(key_turned, r - 1)
                    dve.tensor_copy(quad_row[:, r % 2, :].rearrange("p (g b h) -> p g b h", g=QUAD, h=H),
                                    key_v[:, :, r * QUAD:(r + 1) * QUAD].rearrange("p b g -> p g b")[:, :, :, None]
                                    .to_broadcast([P, QUAD, G, H])).then_inc(key_rows, 1)
                dve.wait_ge(key_evicted, NG // QUAD)
                hand(dve.tensor_scalar(wide[:, 0:G], blk[:, :], key[:, L:L + 1], None, ALU.mult))
                dve.wait_ge(pe_step, 2)
                link(dve.tensor_copy(headT[:, :], ps[5][0:H, 0:P]))
                link(dve.memset(carry[:, 0:1], -2.0))
                hand(dve.tensor_copy(carry[:, 1:G + 1], ps[4][0:H, 0:G]))
                dve.wait_ge(pe_step, 3)
                link(dve.tensor_tensor(back[:, :], blk[:, :], ps[4][:, 0:G], ALU.mult))
                link(dve.tensor_reduce(key[:, 0:1], back[:, :], AX_X, ALU.add))
                link(dve.tensor_tensor(pen[:, 0:L], key[:, 1:L + 1], key[:, 0:L], ALU.not_equal))
                link(dve.tensor_scalar(pen[:, 0:L], pen[:, 0:L], -BIG, None, ALU.mult))
                link(dve.tensor_reduce(edge[:, 1:2], pen[:, 0:L], AX_X, ALU.min))
                dve.wait_ge(sc_evicted, NG // QUAD)
                link(dve.tensor_tensor_scan(mx[:, :], pen[:, 0:L], sc[:, :], -BIG, ALU.add, ALU.max))
                link(dve.tensor_copy(edge[:, 0:1], mx[:, L - 1:L]))
                link(dve.tensor_copy(edge[:, 2:3], pen[:, 0:1]))
                for a in range(3):
                    (hand if a == 2 else link)(dve.tensor_scalar(wide[:, a * G:(a + 1) * G], blk[:, :], edge[:, a:a + 1], None, ALU.mult))
                dve.wait_ge(pe_step, 4)
                link(dve.tensor_copy(small[:, :], ps[4][0:H, 0:3 * G]))
                link(dve.memset(carry[:, 0:1], -BIG))
                hand(dve.tensor_tensor_scan(carry[:, 1:G + 1], small[:, G:2 * G], small[:, 0:G], -BIG, ALU.add, ALU.max))
                dve.wait_ge(pe_step, 5)
                link(dve.tensor_tensor(back[:, :], blk[:, :], ps[4][:, 0:G], ALU.mult))
                link(dve.tensor_reduce(carried[:, 0:1], back[:, :], AX_X, ALU.add))
                link(dve.tensor_tensor_scan(mx[:, :], pen[:, 0:L], sc[:, :], carried[:, 0:1], ALU.add, ALU.max))
                link(dve.memset(carry[:, G:G + 1], -BIG))
                link(dve.tensor_copy(carry[:, 0:G - 1], small[:, 2 * G + 1:3 * G]))
                hand(dve.memset(carry[:, G - 1:G], -BIG))
                dve.wait_ge(pe_step, 6)
                link(dve.tensor_tensor(back[:, :], blk[:, :], ps[4][:, 0:G], ALU.mult))
                link(dve.tensor_reduce(pen[:, L:L + 1], back[:, :], AX_X, ALU.add))
                link(dve.tensor_reduce(edge[:, 1:2], pen[:, 1:L + 1], AX_X, ALU.min))
                link(dve.tensor_tensor_scan(key[:, 0:L][:, ::-1], pen[:, 1:L + 1][:, ::-1], mx[:, :][:, ::-1],
                                            -BIG, ALU.add, ALU.max))
                link(dve.tensor_copy(edge[:, 0:1], key[:, 0:1]))
                for a in range(2):
                    (hand if a == 1 else link)(dve.tensor_scalar(wide[:, a * G:(a + 1) * G], blk[:, :], edge[:, a:a + 1], None, ALU.mult))
                dve.wait_ge(pe_step, 7)
                link(dve.tensor_copy(small[:, 0:2 * G], ps[4][0:H, 0:2 * G]))
                link(dve.memset(carry[:, G - 1:G], -BIG))
                hand(dve.tensor_tensor_scan(carry[:, 0:G - 1][:, ::-1], small[:, G + 1:2 * G][:, ::-1],
                                            small[:, 1:G][:, ::-1], -BIG, ALU.add, ALU.max))
                dve.wait_ge(pe_step, 8)
                link(dve.tensor_tensor(back[:, :], blk[:, :], ps[4][:, 0:G], ALU.mult))
                link(dve.tensor_reduce(carried[:, 1:2], back[:, :], AX_X, ALU.add))
                link(dve.tensor_tensor_scan(key[:, 0:L][:, ::-1], pen[:, 1:L + 1][:, ::-1], mx[:, :][:, ::-1],
                                            carried[:, 1:2], ALU.add, ALU.max))
                hand(dve.tensor_tensor(sc[:, :], sc[:, :], key[:, 0:L], ALU.subtract))
                for r in range(NG // QUAD):
                    dve.wait_ge(ex_turned, r + 1)
                    dve.tensor_copy(score_v[:, :, r * QUAD:(r + 1) * QUAD, :].rearrange("p b g h -> p g b h"),
                                    ps[r % 2][:, :].rearrange("p (g b h) -> p g b h", g=QUAD, h=H)).then_inc(ex_evicted, 1)

            @block.scalar
            def _(act):
                for r in range(NG // QUAD):
                    cols = slice(r * QUAD * P, (r + 1) * QUAD * P)
                    act.wait_ge(sc_turned, r + 1)
                    act.activation(sc[:, cols], ps[2 + r % 2][:, :], ACT.Copy).then_inc(sc_evicted, 1)
                    act.wait_ge(key_turned, r + 1)
                    act.activation(key[:, 1 + cols.start:1 + cols.stop], ps[r % 2][:, :], ACT.Copy).then_inc(key_evicted, 1)
                act.wait_ge(handed, 8)
                for r in range(NG // QUAD):
                    cols = slice(r * QUAD * P, (r + 1) * QUAD * P)
                    act.activation(sc[:, cols], sc[:, cols], ACT.Exp).then_inc(exps, 1)

            @block.tensor
            def _(pe):
                def spread(after):
                    pe.wait_ge(handed, after)
                    pe.matmul(ps[4][:, 0:G], headT[:, :], carry[:, 0:G], start=True, stop=True).then_inc(pe_step, 1)

                def gather(after, m):
                    pe.wait_ge(handed, after)
                    pe.matmul(ps[4][0:H, 0:m], head[:, :], wide[:, 0:m], start=True, stop=True).then_inc(pe_step, 1)

                for r in range(NG // QUAD):
                    if r == 0:
                        pe.wait_ge(masked, G)
                    if r >= 2:
                        pe.wait_ge(sc_evicted, r - 1)
                    for a in range(QUAD):
                        last = pe.transpose(ps[2 + r % 2][:, a * P:(a + 1) * P],
                                            by_row[:, r * QUAD + a, :, :].rearrange("p b h -> p (b h)"), s.ident[:, :])
                    last.then_inc(sc_turned, 1)
                    pe.wait_ge(key_rows, r + 1)
                    if r >= 2:
                        pe.wait_ge(key_evicted, r - 1)
                    for a in range(QUAD):
                        last = pe.transpose(ps[r % 2][:, a * P:(a + 1) * P], quad_row[:, r % 2, a * P:(a + 1) * P], s.ident[:, :])
                    last.then_inc(key_turned, 1)
                gather(1, G)
                pe.transpose(ps[5][0:H, 0:P], head[:, :], s.ident[:, :]).then_inc(pe_step, 1)
                spread(2)
                gather(3, 3 * G)
                spread(4)
                spread(5)
                gather(6, 2 * G)
                spread(7)
                for r in range(NG // QUAD):
                    pe.wait_ge(exps, r + 1)
                    if r >= 2:
                        pe.wait_ge(ex_evicted, r - 1)
                    for a in range(QUAD):
                        at = (r * QUAD + a) * P
                        last = pe.transpose(ps[r % 2][:, a * P:(a + 1) * P], sc[:, at:at + P], s.ident[:, :])
                    last.then_inc(ex_turned, 1)


def stage_attend(nc, s):
    with ExitStack() as ctx:
        sb, pb, sem = makers(nc, ctx, "attend")
        ps = [pb(f"att_ps{a}", [P, 512], F32) for a in range(G)]
        val = sb("val", [P, 4, G, DIM], F32)
        msg = sb("msg", [P, 2, G, UW], F32)
        oh = sb("oh", [P, 2, G, P], F32)
        off = sb("off", [P, 2, P], F32)
        minus = s.validS
        negated, off_made, even_made, odd_made = sem("negated"), sem("off_made"), sem("even_made"), sem("odd_made")
        val_in = [sem(f"val_in{a}") for a in range(4)]
        weighted, copied, summed, added, zeroed = (sem("weighted"), sem("copied"),
                                                            sem("summed"), sem("added"), sem("zeroed"))
        with nc.Block() as block:
            @block.sync
            def _(sp):
                first = [sp.alloc_register(f"att_first{q}") for q in range(FOUR)]
                with chunks(sp, J, FOUR) as i:
                    sp.load(first, s.start_of[0][0:1, bass.ds(i, FOUR)])
                    for group in range(4):
                        g, half = i + group * G, group % 2
                        sp.wait_ge(weighted, g + G)
                        for q in range(G):
                            at = sp.snap(first[group * G + q], min_val=0, max_val=E)
                            sp.dma_start(val[:, group, q, :], s.rows[bass.ds(at, P), 0:DIM]).then_inc(val_in[group], 16)

            @block.gpsimd
            def _(pool):
                pool.sem_inc(weighted, FOUR)
                with chunks(pool, J, FOUR) as i:
                    for group in range(4):
                        g, half = i + group * G, group % 2
                        pool.wait_ge(val_in[group], i * 4 + 16 * G)
                        for q in range(0, G, 2):
                            pool.wait_ge(summed, g + q + 2)
                            pool.tensor_tensor(msg[:, half, q:q + 2, 0:DIM].rearrange("p g (h d) -> p g h d", h=H),
                                               val[:, group, q:q + 2, :].rearrange("p g (h d) -> p g h d", h=H),
                                               s.score[:, bass.ds(g + q, 2), :, None].to_broadcast([P, 2, H, DIM // H]),
                                               ALU.mult).then_inc(weighted, 2)

            @block.scalar
            def _(act):
                act.sem_inc(off_made, 1)
                act.wait_ge(negated, 1)
                with act.Fori(0, J // TWO) as n:
                    i = act.snap(n * TWO)
                    for half in range(2):
                        g, g_half = i + half * G, n * G + half * (G // 2)
                        act.wait_ge(summed, g + G)
                        act.activation(msg[:, half, :, DIM:UW], s.score[:, bass.ds(g, G), :], ACT.Copy).then_inc(copied, G)

                        def distance(o):
                            act.wait_ge(odd_made, g_half + o + 1)
                            act.activation(off[:, o % 2, :], s.iota[:, :], ACT.Square,
                                           bias=minus[:, bass.ds(g + 2 * o + 1, 1)]).then_inc(off_made, 1)

                        distance(0)
                        for o in range(G // 2):
                            if o + 1 < G // 2:
                                distance(o + 1)
                            act.wait_ge(off_made, g_half + o + 2)
                            act.wait_ge(summed, g + 2 * o + 2)
                            act.activation(oh[:, half, 2 * o + 1, :], off[:, o % 2, :], ACT.Relu, bias=s.ones[:, 0:1],
                                           scale=-1.0).then_inc(odd_made, 1)

            @block.tensor
            def _(pe):
                pe.sem_inc(summed, TWO)
                with pe.Fori(0, J // FOUR) as n:
                    i = pe.snap(n * FOUR)
                    for group in range(4):
                        g, half, g_half = i + group * G, group % 2, n * TWO + group * (G // 2)
                        pe.wait_ge(copied, g + G)
                        for q in range(G):
                            if q % 2 == 0:
                                pe.wait_ge(even_made, g_half + q // 2 + 1)
                            else:
                                pe.wait_ge(odd_made, g_half + q // 2 + 3)
                            pe.wait_ge(weighted, g + q // 2 * 2 + 2 + FOUR)
                            pe.wait_ge(added, g + q + 1)
                            pe.matmul(ps[q][:, 0:UW], oh[:, half, q, :], msg[:, half, q, :], start=True,
                                      stop=True).then_inc(summed, 1)

            @block.vector
            def _(dve):
                tile = [dve.alloc_register(f"att_tile{q}") for q in range(TWO)]
                dve.sem_inc(added, G)
                dve.sem_inc(odd_made, 2)
                dve.tensor_scalar(minus, s.relS[:, 0:J], -1.0, None, ALU.mult).then_inc(negated, 1)
                for acc in s.acc:
                    dve.memset(acc[:, :, :], 0.0).then_inc(zeroed, 1)
                dve.wait_ge(zeroed, 2)

                def onehot(n, slot, q):
                    dve.wait_ge(summed, n + q + 1)
                    dve.tensor_scalar(oh[:, slot, q, :], s.iota[:, :], s.relS[:, bass.ds(n + q, 1)], None,
                                      ALU.is_equal).then_inc(even_made, 1)

                for q in range(0, G, 2):
                    onehot(0, 0, q)
                with chunks(dve, J, TWO) as i:
                    dve.load(tile, s.tile_of[0][0:1, bass.ds(i, TWO)])
                    for half in range(2):
                        g = i + half * G
                        for q in range(G):
                            if q % 2 == 0:
                                onehot(g + G, 1 - half, q)
                            t = dve.snap(tile[half * G + q], min_val=0, max_val=NT - 1)
                            dve.wait_ge(summed, g + q + 1 + TWO)
                            dve.wait_ge(added, g + q + G - 1)
                            acc = s.acc[q % 2]
                            dve.tensor_tensor(acc[:, bass.ds(t, 1), :], acc[:, bass.ds(t, 1), :],
                                              ps[q][:, None, 0:UW], ALU.add).then_inc(added, 1)


def stage_norm(nc, s, io):
    BATCH = 6
    CUT = 14
    with ExitStack() as ctx:
        sb, pb, sem = makers(nc, ctx, "norm")
        x = sb("x_rows", [P, NT, DIM], F32)
        den = sb("den", [P, NT, H], F32)
        rden = sb("rden", [P, NT, H], F32)
        stats = sb("stats", [P, NT, 6], F32)
        mv = sb("mv", [P, NT, 2], F32)
        std = sb("std", [P, NT], F32)
        rstd = sb("rstd", [P, NT], F32)
        others = sem("others")
        x_in, step, normed, rooted, stored = sem("x_in"), sem("step"), sem("normed"), sem("rooted"), sem("stored")
        full = NT - 1
        with nc.Block() as block:
            @block.sync
            def _(sp):
                sp.wait_ge(step, 1)
                sp.dma_start(x[:, 0:full, :], io["x"][0:full * P, :].rearrange("(t p) f -> p t f", p=P)).then_inc(x_in, 16)
                sp.dma_start(x[0:LAST, full, :], io["x"][full * P:N, :]).then_inc(x_in, 16)
                for t in range(0, full, BATCH):
                    sp.wait_ge(normed, t + BATCH)
                    sp.dma_start(s.h_dram[t * P:(t + BATCH) * P, :].rearrange("(t p) f -> p t f", p=P),
                                 s.h[:, t:t + BATCH, :]).then_inc(stored, 16)
                sp.wait_ge(normed, NT)
                sp.dma_start(s.h_dram[full * P:N, :], s.h[0:LAST, full, :]).then_inc(stored, 16)
                sp.wait_ge(stored, 16 * (full // BATCH + 1))

            @block.gpsimd
            def _(pool):
                pool.tensor_tensor(s.acc[0][:, CUT:, :], s.acc[0][:, CUT:, :], s.acc[1][:, CUT:, :], ALU.add).then_inc(others, 1)

            @block.scalar
            def _(act):
                act.wait_ge(step, 6)
                act.activation(std[:, :], mv[:, :, 1], ACT.Sqrt, bias=s.eps[:, 0:1]).then_inc(rooted, 1)

            @block.vector
            def _(dve):
                n = [0]

                def link(ins):
                    n[0] += 1
                    ins.then_inc(step, 1)
                    dve.wait_ge(step, n[0])

                link(dve.memset(x[:, full, :], 0.0))
                link(dve.tensor_tensor(s.acc[0][:, 0:CUT, :], s.acc[0][:, 0:CUT, :], s.acc[1][:, 0:CUT, :], ALU.add))
                dve.wait_ge(others, 1)
                link(dve.tensor_scalar(den[:, :, :], s.acc[0][:, :, DIM:UW], EPS_SOFTMAX, None, ALU.add))
                link(dve.reciprocal(rden[:, :, :], den[:, :, :]))
                for t in range(NT):
                    ins = dve.tensor_tensor(s.h[:, t, :].rearrange("p (h d) -> p h d", h=H),
                                            s.acc[0][:, t, 0:DIM].rearrange("p (h d) -> p h d", h=H),
                                            rden[:, t, :, None].to_broadcast([P, H, DIM // H]), ALU.mult)
                    if t == NT - 1:
                        link(ins)
                dve.wait_ge(x_in, 32)
                for t in range(NT):
                    dve.tensor_tensor(s.h[:, t, :], s.h[:, t, :], x[:, t, :], ALU.add).then_inc(s.sum_made, 1)
                dve.wait_ge(s.sum_made, NT)
                for t in range(NT):
                    dve.bn_stats(stats[:, t, :], s.h[:, t, :]).then_inc(s.sum_made, 1)
                dve.wait_ge(s.sum_made, 2 * NT)
                for t in range(NT):
                    ins = dve.bn_aggr(mv[:, t, :], stats[:, t, :])
                    if t == NT - 1:
                        link(ins)
                dve.wait_ge(rooted, 1)
                link(dve.reciprocal(rstd[:, :], std[:, :]))
                for t in range(NT):
                    dve.tensor_scalar(s.h[:, t, :], s.h[:, t, :], mv[:, t, 0:1], rstd[:, t:t + 1],
                                      ALU.subtract, ALU.mult).then_inc(normed, 1)


def stage_neighbours(nc, s, io):
    with ExitStack() as ctx:
        sb, pb, sem = makers(nc, ctx, "neighbours")
        ps = [pb(f"nb_ps{a}", [P, 512], F32) for a in range(4)]
        psX = pb("nb_psX", [P, 512], F32)
        psG = [pb(f"nb_psG{a}", [P, 512], F32) for a in range(2)]
        nbr = [sb(f"nbr{q}", [P, LW], F32) for q in range(TWO)]
        idx = sb("nb_idx", [P, 4, G], I32)
        oh = sb("oh", [P, 2, G, P], F32)
        wh = sb("wh", [P, 2, 3 * DIM], F32)
        h_tile = sb("h_tile", [P, DIM], F32)
        hT = sb("hT", [P, 2, P], F32)
        gathered = [sem(f"gathered{q}") for q in range(TWO)]
        idx_made, typed, oh_made, summed, added, zeroed = (sem("idx_made"), sem("typed"), sem("oh_made"),
                                                           sem("summed"), sem("added"), sem("zeroed"))
        w_in, h_cut, h_turned, hT_made, gh_made, gh_kept = (sem(n) for n in (
            "w_in", "h_cut", "h_turned", "hT_made", "gh_made", "gh_kept"))
        with nc.Block() as block:
            @block.sync
            def _(sp):
                for a in range(2):
                    sp.dma_start(wh[:, a, :], io["whhT"][a * P:(a + 1) * P, :]).then_inc(w_in, 16)

            @block.gpsimd
            def _(pool):
                with chunks(pool, J, FOUR) as i:
                    for group in range(4):
                        g, half = i + group * G, group % 2
                        pool.wait_ge(idx_made, g + G)
                        pool.sem_inc(s.pool_passed, 1)
                        for q in range(G):
                            pool.wait_ge(summed, g + q + 1)
                            pool.sem_inc(s.pool_passed, 1)
                            pool.indirect_dma_start(
                                out=nbr[half * G + q][:, 0:DIM], out_offset=None, in_=s.h_dram,
                                in_offset=bass.IndirectOffsetOnAxis(ap=idx[:, group, q:q + 1], axis=0)
                            ).then_inc(gathered[half * G + q], 16)

            @block.tensor
            def _(pe):
                pe.sem_inc(summed, TWO)
                pe.wait_ge(w_in, 32)

                def turn_h(t):
                    pe.wait_ge(h_cut, t + 1)
                    pe.wait_ge(hT_made, t + 1)
                    pe.transpose(psX[:, 0:P], h_tile[:, 0:P], s.ident[:, :])
                    pe.transpose(psX[:, P:2 * P], h_tile[:, P:2 * P], s.ident[:, :]).then_inc(h_turned, 1)

                def products_h(t):
                    pe.wait_ge(hT_made, t + 2)
                    pe.wait_ge(gh_kept, 2 * t + 2)
                    for c, cols in enumerate((slice(0, 2 * DIM), slice(2 * DIM, 3 * DIM))):
                        out = psG[c][:, 0:cols.stop - cols.start]
                        pe.matmul(out, s.ones_b[:, :], s.parts[0:6, 2 * DH + cols.start:2 * DH + cols.stop], start=True,
                                  stop=False)
                        for a in range(2):
                            last = pe.matmul(out, hT[:, a, :], wh[:, a, cols], start=False, stop=(a == 1))
                        last.then_inc(gh_made, 1)

                with pe.Fori(0, J // FOUR) as n:
                    i = pe.snap(n * FOUR)
                    for group in range(4):
                        g, half = i + group * G, group % 2
                        (turn_h, products_h)[half](2 * n + group // 2)
                        for q in range(G):
                            pe.wait_ge(typed, g + q + 1)
                            pe.wait_ge(oh_made, g + q + 1)
                            pe.wait_ge(gathered[half * G + q], i + 16 + 16 * (group // 2))
                            pe.wait_ge(added, g + q + 1)
                            pe.matmul(ps[q % 4][:, 0:LW], oh[:, half, q, :], nbr[half * G + q][:, :], start=True,
                                      stop=True).then_inc(summed, 1)

            @block.scalar
            def _(act):
                def indices(g, slot):
                    act.activation(idx[:, slot, :], s.src_of[:, bass.ds(g, G)], ACT.Copy).then_inc(idx_made, G)

                act.sem_inc(hT_made, 1)
                act.sem_inc(gh_kept, 2)
                act.wait_ge(zeroed, 4)
                for group in range(2):
                    indices(group * G, group)
                with act.Fori(0, J // FOUR) as n:
                    i = act.snap(n * FOUR)
                    for group in range(4):
                        g, t = i + group * G, 2 * n + group // 2
                        act.wait_ge(summed, g + G)
                        indices(g + TWO, (group + 2) % 4)
                        if group % 2 == 0:
                            act.wait_ge(hT_made, t + 1)
                            act.activation(h_tile[:, None, :], s.h[:, bass.ds(t, 1), :], ACT.Copy).then_inc(h_cut, 1)
                            act.wait_ge(h_turned, t + 1)
                            act.wait_ge(gh_kept, 2 * t + 2)
                            act.activation(hT[:, :, :], psX[:, 0:2 * P].rearrange("p (a n) -> p a n", a=2),
                                           ACT.Copy).then_inc(hT_made, 1)
                        else:
                            act.wait_ge(gh_made, 2 * t + 2)
                            act.activation(s.gh[:, bass.ds(t, 1), 0:2 * DIM], psG[0][:, None, :], ACT.Copy).then_inc(gh_kept, 1)
                            act.activation(s.gh[:, bass.ds(t, 1), 2 * DIM:], psG[1][:, None, 0:DIM], ACT.Copy).then_inc(gh_kept, 1)

            @block.vector
            def _(dve):
                tile = [dve.alloc_register(f"nb_tile{q}") for q in range(G)]
                dve.sem_inc(added, 4)
                dve.memset(s.acc2[:, :, :], 0.0).then_inc(zeroed, 1)
                dve.memset(s.relD[:, J:J + G], -1.0).then_inc(zeroed, 1)
                dve.memset(s.type_of[:, J:J + G], 0.0).then_inc(zeroed, 1)
                dve.memset(s.src_of[:, J:J + TWO], 0).then_inc(zeroed, 1)
                dve.wait_ge(zeroed, 4)

                def onehot(n, slot, q):
                    dve.wait_ge(summed, n + q + 1)
                    dve.tensor_scalar(oh[:, slot, q, :], s.iota[:, :], s.relD[:, bass.ds(n + q, 1)], None,
                                      ALU.is_equal).then_inc(oh_made, 1)
                    dve.tensor_scalar(nbr[slot * G + q][:, DIM:LW], s.iota[:, 0:NREL],
                                      s.type_of[:, bass.ds(n + q, 1)], None, ALU.is_equal).then_inc(typed, 1)

                for q in range(G):
                    onehot(0, 0, q)
                with chunks(dve, J, TWO) as i:
                    for half in range(2):
                        g = i + half * G
                        dve.load(tile, s.tile_of[1][0:1, bass.ds(g, G)])
                        for q in range(G):
                            onehot(g + G, 1 - half, q)
                            t = dve.snap(tile[q], min_val=0, max_val=NT - 1)
                            dve.wait_ge(summed, g + q + 1 + TWO)
                            dve.wait_ge(added, g + q + 4)
                            dve.tensor_tensor(s.acc2[:, bass.ds(t, 1), :], s.acc2[:, bass.ds(t, 1), :],
                                              ps[q % 4][:, None, 0:LW], ALU.add).then_inc(added, 1)


def stage_gru(nc, s, io, out):
    BATCH = 5
    with ExitStack() as ctx:
        sb, pb, sem = makers(nc, ctx, "gru")
        psC = pb("psC", [P, 512], F32)
        psX = [pb(f"psX{a}", [P, 512], F32) for a in range(2)]
        psRZ = [pb(f"psRZ{a}", [P, 512], F32) for a in range(2)]
        psN = [pb(f"psN{a}", [P, 512], F32) for a in range(2)]
        wi = sb("wi", [P, 2, 3 * DIM], F32)
        rel = sb("rel", [NREL, DIM], F32)
        cT = sb("cT", [NREL, 2, P], F32)
        redT = sb("redT", [P, 2, 2, P], F32)
        pre = sb("pre", [P, 2, 2 * DIM], F32)
        rz = sb("rz", [P, 3, 2 * DIM], F32)
        rn = sb("rn", [P, 2, DIM], F32)
        pre_n = sb("pre_n", [P, 2, DIM], F32)
        nn = sb("nn", [P, 2, DIM], F32)
        w1 = sb("w1", [P, 2, DIM], F32)
        stats = sb("stats", [P, 2, 6], F32)
        mv = sb("mv", [P, NT, 2], F32)
        std = sb("std", [P, NT], F32)
        rstd = sb("rstd", [P, NT], F32)
        y = sb("y", [P, NT, DIM], F32)
        loads, c_turned, cT_made, turned, T_made = sem("loads"), sem("c_turned"), sem("cT_made"), sem("turned"), sem("T_made")
        gates, gates_n, sig, tanh_done, rooted = sem("gates"), sem("gates_n"), sem("sig"), sem("tanh_done"), sem("rooted")
        gates_added, reset, cand_added, diffed, mixed = (sem(n) for n in ("gates_added", "reset", "cand_added", "diffed", "mixed"))
        blended, y_made, stats_made, mv_made, inverted, normed, stored = (sem(n) for n in (
            "blended", "y_made", "stats_made", "mv_made", "inverted", "normed", "stored"))
        with nc.Block() as block:
            @block.sync
            def _(sp):
                for a in range(2):
                    sp.dma_start(wi[:, a, :], io["wihT"][a * P:(a + 1) * P, :]).then_inc(loads, 16)
                sp.dma_start(rel[:, :], io["rel"]).then_inc(loads, 16)
                full = NT - 1
                for t in range(0, NT, BATCH):
                    end = min(t + BATCH, full)
                    sp.wait_ge(normed, min(t + BATCH, NT))
                    sp.dma_start(out[t * P:end * P, :].rearrange("(t p) f -> p t f", p=P), y[:, t:end, :]).then_inc(stored, 16)
                sp.dma_start(out[full * P:N, :], y[0:LAST, full, :]).then_inc(stored, 16)
                sp.wait_ge(stored, 16 * (NT // BATCH + 1))

            @block.tensor
            def _(pe):
                pe.wait_ge(loads, 16 * 3)

                def turn_counts(t):
                    if t >= 1:
                        pe.wait_ge(cT_made, t)
                    pe.transpose(psC[0:NREL, 0:P], s.acc2[:, t, DIM:LW], s.ident[:, :]).then_inc(c_turned, 1)

                def prepare(t):
                    b = t % 2
                    if t >= 2:
                        pe.wait_ge(T_made, t - 1)
                    pe.wait_ge(cT_made, t + 1)
                    for a in range(2):
                        pe.matmul(psX[b][:, a * P:(a + 1) * P], s.acc2[:, t, a * P:(a + 1) * P], s.ident[:, :],
                                  start=True, stop=False)
                        last = pe.matmul(psX[b][:, a * P:(a + 1) * P], rel[:, a * P:(a + 1) * P], cT[:, b, :],
                                         start=False, stop=True)
                    last.then_inc(turned, 1)

                turn_counts(0)
                turn_counts(1)
                prepare(0)
                for t in range(NT):
                    b = t % 2
                    if t + 2 < NT:
                        turn_counts(t + 2)
                    if t + 1 < NT:
                        prepare(t + 1)
                    pe.wait_ge(T_made, t + 1)
                    if t >= 2:
                        pe.wait_ge(gates_added, t - 1)
                        pe.wait_ge(cand_added, t - 1)
                    for a in range(2):
                        last = pe.matmul(psRZ[b][:, :], redT[:, b, a, :], wi[:, a, 0:2 * DIM], start=(a == 0), stop=(a == 1))
                    last.then_inc(gates, 1)
                    pe.matmul(psN[b][:, 0:DIM], s.ones_b[:, :], s.parts[0:6, 2 * DH + 3 * DIM:], start=True, stop=False)
                    for a in range(2):
                        last = pe.matmul(psN[b][:, 0:DIM], redT[:, b, a, :], wi[:, a, 2 * DIM:], start=False, stop=(a == 1))
                    last.then_inc(gates_n, 1)

            @block.scalar
            def _(act):
                def counts_copy(t):
                    act.wait_ge(c_turned, t + 1)
                    if t >= 2:
                        act.wait_ge(turned, t - 1)
                    act.activation(cT[:, t % 2, :], psC[0:NREL, 0:P], ACT.Copy).then_inc(cT_made, 1)

                def turned_copy(t):
                    b = t % 2
                    act.wait_ge(turned, t + 1)
                    if t >= 2:
                        act.wait_ge(gates_n, t - 1)
                    act.activation(redT[:, b, :, :], psX[b][:, 0:2 * P].rearrange("p (a n) -> p a n", a=2), ACT.Copy).then_inc(T_made, 1)

                counts_copy(0)
                counts_copy(1)
                turned_copy(0)
                for t in range(NT + 1):
                    if t + 2 < NT:
                        counts_copy(t + 2)
                    if t + 1 < NT:
                        turned_copy(t + 1)
                    if t < NT:
                        act.wait_ge(gates_added, t + 1)
                        if t >= 3:
                            act.wait_ge(mixed, t - 2)
                        act.activation(rz[:, t % 3, :], pre[:, t % 2, :], ACT.Sigmoid).then_inc(sig, 1)
                    if t >= 1:
                        act.wait_ge(cand_added, t)
                        if t >= 3:
                            act.wait_ge(blended, t - 2)
                        act.activation(nn[:, (t - 1) % 2, :], pre_n[:, (t - 1) % 2, :], ACT.Tanh).then_inc(tanh_done, 1)
                    if t >= 2 and (t - 1) % BATCH == 0:
                        act.wait_ge(mv_made, t - 1)
                        act.activation(std[:, t - 1 - BATCH:t - 1], mv[:, t - 1 - BATCH:t - 1, 1], ACT.Sqrt,
                                       bias=s.eps[:, 0:1]).then_inc(rooted, 1)
                act.wait_ge(mv_made, NT)
                act.activation(std[:, NT - BATCH:NT], mv[:, NT - BATCH:NT, 1], ACT.Sqrt, bias=s.eps[:, 0:1]).then_inc(rooted, 1)

            @block.vector
            def _(dve):
                def gate_sums(t):
                    b = t % 2
                    dve.wait_ge(gates, t + 1)
                    if t >= 2:
                        dve.wait_ge(sig, t - 1)
                    dve.tensor_tensor(pre[:, b, :], psRZ[b][:, :], s.gh[:, t, 0:2 * DIM], ALU.add).then_inc(gates_added, 1)

                def candidate_sums(t):
                    b = t % 2
                    dve.wait_ge(sig, t + 1)
                    dve.tensor_tensor(rn[:, b, :], rz[:, t % 3, 0:DIM], s.gh[:, t, 2 * DIM:], ALU.mult).then_inc(reset, 1)
                    dve.wait_ge(gates_n, t + 1)
                    dve.wait_ge(reset, t + 1)
                    if t >= 2:
                        dve.wait_ge(tanh_done, t - 1)
                    dve.tensor_tensor(pre_n[:, b, :], rn[:, b, :], psN[b][:, 0:DIM], ALU.add).then_inc(cand_added, 1)

                def output(t):
                    b = t % 2
                    dve.wait_ge(tanh_done, t + 1)
                    dve.tensor_tensor(w1[:, b, :], s.h[:, t, :], nn[:, b, :], ALU.subtract).then_inc(diffed, 1)
                    dve.wait_ge(diffed, t + 1)
                    dve.tensor_tensor(y[:, t, :], rz[:, t % 3, DIM:], w1[:, b, :], ALU.mult).then_inc(mixed, 1)
                    dve.wait_ge(mixed, t + 1)
                    dve.tensor_tensor(w1[:, b, :], y[:, t, :], nn[:, b, :], ALU.add).then_inc(blended, 1)
                    dve.wait_ge(blended, t + 1)
                    dve.tensor_tensor(y[:, t, :], w1[:, b, :], s.h[:, t, :], ALU.add).then_inc(y_made, 1)
                    dve.wait_ge(y_made, t + 1)
                    dve.bn_stats(stats[:, b, :], y[:, t, :]).then_inc(stats_made, 1)
                    dve.wait_ge(stats_made, t + 1)
                    dve.bn_aggr(mv[:, t, :], stats[:, b, :]).then_inc(mv_made, 1)

                def normalise(k):
                    tiles = range(k * BATCH, (k + 1) * BATCH)
                    dve.wait_ge(rooted, k + 1)
                    dve.reciprocal(rstd[:, tiles[0]:tiles[-1] + 1], std[:, tiles[0]:tiles[-1] + 1]).then_inc(inverted, 1)
                    dve.wait_ge(inverted, k + 1)
                    for t in tiles:
                        dve.tensor_scalar(y[:, t, :], y[:, t, :], mv[:, t, 0:1], rstd[:, t:t + 1],
                                          ALU.subtract, ALU.mult).then_inc(normed, 1)

                for t in range(NT + 2):
                    if t < NT:
                        gate_sums(t)
                    if 1 <= t <= NT:
                        candidate_sums(t - 1)
                    if t >= 2:
                        output(t - 2)
                    if t >= 3 and (t - 2) % BATCH == 0 and t - 2 < NT:
                        normalise((t - 2) // BATCH - 1)
                normalise(NT // BATCH - 1)


def build(nc, io, out):
    s = Shared()
    dram = lambda n, sh, dt: nc.dram_tensor(n, sh, dt, kind="Internal").ap()
    s.rows = dram("rows", (EPAD, ROW), F32)
    s.recs = dram("recs", (EPAD, REC), F32)
    s.h_dram = dram("h_rows", (N, DIM), F32)
    s.hiT = [dram(f"hiT{k}", (E,), F32) for k in range(2)]
    s.hiT2 = [a.rearrange("(c p) -> c p", p=EP) for a in s.hiT]
    with ExitStack() as ctx:
        sb = lambda n, sh, dt: ctx.enter_context(nc.sbuf_tensor(n, sh, dt))
        constants(nc, s, sb)
        s.sum_made = ctx.enter_context(nc.semaphore("sum_made"))
        s.pool_passed = ctx.enter_context(nc.semaphore("pool_passed"))
        s.tile_of = [sb(f"tile_of{k}", [1, J], I32) for k in range(2)]
        s.start_of = [sb(f"start_of{k}", [1, J], I32) for k in range(2)]
        s.base = [sb(f"base{k}", [P, J], F32) for k in range(2)]
        s.parts = sb("parts", [P, PW], BF16)
        s.relD = sb("relD", [P, J + G], F32)
        s.src_of = sb("src_of", [P, J + TWO], I32)
        s.type_of = sb("type_of", [P, J + G], F32)
        s.scores_or_h = sb("scores_or_h", [P, J * H], F32)
        s.score = s.scores_or_h[:, :].rearrange("p (j h) -> p j h", h=H)
        s.h = s.scores_or_h[:, 0:NH * DIM].rearrange("p (t d) -> p t d", d=DIM)
        with ExitStack() as layer0:
            sbl = lambda n, sh, dt: layer0.enter_context(nc.sbuf_tensor(n, sh, dt))
            s.by_source = sbl("by_source", [P, max(PW, 3 * J + G)], F32)
            s.validS = s.by_source[:, 0:J]
            s.src_key = s.by_source[:, J:2 * J]
            s.relS = s.by_source[:, 2 * J:3 * J + G]
            with ExitStack() as tables:
                s.tab = tables.enter_context(nc.sbuf_tensor("tab", [P, NT, 3, 512], BF16))
                with ExitStack() as early:
                    sbe = lambda n, sh, dt: early.enter_context(nc.sbuf_tensor(n, sh, dt))
                    s.start = [sbe(f"start{k}", [NT, P], F32) for k in range(2)]
                    s.rec = sbe("rec", [EP, EC, REC], F32)
                    s.most_drop = sbe("most_drop", [1, 1], F32)
                    s.unsorted = sbe("unsorted", [1, 1], I32)
                    s.sorted = sbe("sorted", [1, 1], I32)
                    s.count = [sbe(f"count{k}", [NT, P], F32) for k in range(2)]
                    s.place = sbe("place", [EP, EC], F32)
                    s.key = [sbe(f"key{k}", [EP, EC], F32) for k in range(2)]
                    s.hi = [sbe(f"hi{k}", [EP, EC], F32) for k in range(2)]
                    s.lo = [sbe(f"lo{k}", [EP, EC], F32) for k in range(2)]
                    stage_constants(nc, s, io)
                    s.Wa = sbe("Wa", [P, PW], F32)
                    stage_count_project(nc, s, io)
                    stage_schedule(nc, s, 0)
                    stage_schedule(nc, s, 1)
                    stage_rank(nc, s, io, 0)
                    stage_rank(nc, s, io, 1, s.unsorted)
                    stage_sort_records(nc, s, s.unsorted)
                    stage_store_records(nc, s, s.sorted)
                stage_rows(nc, s)
                stage_scores(nc, s, io)
            stage_softmax(nc, s)
            s.acc = [sbl(f"acc{a}", [P, NT, UW], F32) for a in range(2)]
            stage_attend(nc, s)
            stage_norm(nc, s, io)
        s.acc2 = sb("acc2", [P, NT, LW], F32)
        s.gh = sb("gh", [P, NH, 3 * DIM], F32)
        stage_neighbours(nc, s, io)
        stage_gru(nc, s, io, out)


def kernel(x, src, dst, edge_attr_18, edge_type_16, L0_gnn_Wqkv, L0_gnn_bqkv, L0_gnn_Wk_rpe, L0_gnn_bk_rpe,
           L0_gnn_Wq_rpe, L0_gnn_bq_rpe, L1_gnn_relvectors, L1_gnn_w_ih, L1_gnn_w_hh, L1_gnn_b_ih, L1_gnn_b_hh):
    import concourse.bacc as bacc
    from concourse.bass_utils import run_bass_kernel_spmd

    row = lambda a: np.asarray(a).reshape(1, -1)
    grid = lambda a: np.asarray(a).reshape(EP, EC)
    layout = {
        "x": np.asarray(x), "xT": np.asarray(x).T,
        "src": grid(src), "dst": grid(dst), "type": grid(edge_type_16),
        "srcT": grid(src).T, "dstT": grid(dst).T,
        "attr": np.asarray(edge_attr_18).reshape(EP, EC * RP),
        "Wqkv": np.asarray(L0_gnn_Wqkv), "bqkv": row(L0_gnn_bqkv),
        "Wk_rpe": np.asarray(L0_gnn_Wk_rpe), "bk_rpe": row(L0_gnn_bk_rpe),
        "Wq_rpe": np.asarray(L0_gnn_Wq_rpe), "bq_rpe": row(L0_gnn_bq_rpe),
        "rel": np.asarray(L1_gnn_relvectors),
        "wihT": np.asarray(L1_gnn_w_ih).T, "whhT": np.asarray(L1_gnn_w_hh).T,
        "b_ih": row(L1_gnn_b_ih), "b_hh": row(L1_gnn_b_hh),
    }
    layout = {name: np.ascontiguousarray(a) for name, a in layout.items()}
    nc = bacc.Bacc("TRN2", target_bir_lowering=False, num_devices=1)
    io = {name: nc.dram_tensor(f"in_{name}", a.shape, mybir.dt.from_np(a.dtype), kind="ExternalInput").ap()
          for name, a in layout.items()}
    out = nc.dram_tensor("out", (N, DIM), F32, kind="ExternalOutput").ap()
    build(nc, io, out)
    r = run_bass_kernel_spmd(nc, [{f"in_{name}": a for name, a in layout.items()}], core_ids=[0])
    return r.results[0]["out"]
```
